# Optimizing a Trainium2 kernel written in Bass

```python
import numpy as np
import jax
import jax.numpy as jnp

def _softmax(x, axis=-1):
    return jax.nn.softmax(x, axis=axis)

def _gelu(x):
    return jax.nn.gelu(x, approximate=True)

def _silu(x):
    return jax.nn.silu(x)

def _sigmoid(x):
    return jax.nn.sigmoid(x)

def _layernorm(x, axis=-1, eps=1e-05):
    m = jnp.mean(x, axis=axis, keepdims=True)
    v = jnp.var(x, axis=axis, keepdims=True)
    return (x - m) / jnp.sqrt(v + eps)

def _scatter_add(tgt, idx, src, axis=0):
    return tgt.at[idx].add(src)

def _segment_sum(src, seg, n):
    return jax.ops.segment_sum(src, seg, n)
kernel_name = 'mk_gnn_resnorm_d4_gnn_r16_a645b5'

def setup_inputs(seed: int=0):
    np.random.seed(seed)
    _w = jnp.asarray

    def _rec_inputs():
        import jax
        import jax.numpy as jnp
        _gk = jax.random.key(seed)
        x = -0.0005121 + 1.001 * jax.random.normal(jax.random.fold_in(_gk, 1), (3125, 64), jnp.float32)
        src = jax.random.randint(jax.random.fold_in(_gk, 2), (100000,), 0, 3125, jnp.int32)
        dst = jax.random.randint(jax.random.fold_in(_gk, 3), (100000,), 0, 3125, jnp.int32)
        _o = jnp.argsort(dst, stable=True)
        src = src[_o]
        dst = dst[_o]
        edge_attr_4 = jax.random.uniform(jax.random.fold_in(_gk, 12), (100000, 4), jnp.float32, 0.0, 1)
        edge_type_9 = jax.random.randint(jax.random.fold_in(_gk, 14), (100000,), 0, 9, jnp.int32)
        node_vec = jax.random.uniform(jax.random.fold_in(_gk, 15), (3125,), jnp.float32, 0.0, 31.9963)
        return (x, src, dst, edge_attr_4, edge_type_9, node_vec)
    x, src, dst, edge_attr_4, edge_type_9, node_vec = _rec_inputs()

    def _L0_gnn_setup():
        import jax, jax.numpy as jnp
        import numpy as np
        N = 3125
        E = 50000
        IN = 64
        H = 4
        D = 16
        OH = H * D
        SCALE = float(np.sqrt(IN))
        LN_EPS = 1e-05
        key = jax.random.key(seed)
        ks = jax.random.split(key, 16)
        w = 0.05
        return {'feats': jax.random.normal(ks[0], (N, IN), jnp.float32), 'Wq': jax.random.normal(ks[1], (IN, OH), jnp.float32) * w, 'bq': jnp.zeros((OH,), jnp.float32), 'Wk': jax.random.normal(ks[2], (IN, OH), jnp.float32) * w, 'bk': jnp.zeros((OH,), jnp.float32), 'Wv': jax.random.normal(ks[3], (IN, OH), jnp.float32) * w, 'bv': jnp.zeros((OH,), jnp.float32), 'Wo': jax.random.normal(ks[4], (OH, OH), jnp.float32) * w, 'bo': jnp.zeros((OH,), jnp.float32), 'Wf': jax.random.normal(ks[5], (IN, OH), jnp.float32) * w, 'bf': jnp.zeros((OH,), jnp.float32), 'gamma': jnp.ones((OH,), jnp.float32), 'beta': jnp.zeros((OH,), jnp.float32), 'src': jax.random.randint(ks[6], (E,), 0, N, jnp.int32), 'dst': jax.random.randint(ks[7], (E,), 0, N, jnp.int32)}
    _L0_gnn_all = _L0_gnn_setup()
    _L0_gnn_in = {k: v for k, v in _L0_gnn_all.items() if k in ('Wq', 'bq', 'Wk', 'bk', 'Wv', 'bv', 'Wo', 'bo', 'Wf', 'bf', 'gamma', 'beta')}
    del _L0_gnn_all

    def _L1_gnn_setup():
        import jax, jax.numpy as jnp
        import numpy as np
        N = 3125
        E = 50000
        C = 64
        key = jax.random.key(seed)
        ks = jax.random.split(key, 16)
        s = 0.05
        x = jax.random.normal(ks[0], (N, C), jnp.float32)
        edge_attr = jax.random.uniform(ks[1], (E, 4), dtype=jnp.float32)
        edge_index = jax.random.randint(ks[2], (2, E), 0, N)
        deg_hist = jax.random.uniform(ks[3], (N,), dtype=jnp.float32) * 32.0
        W = jax.random.normal(ks[4], (C, C), jnp.float32) * s
        We = jax.random.normal(ks[5], (3, C), jnp.float32) * s
        be = jnp.zeros((C,), jnp.float32)
        Wpre = jax.random.normal(ks[6], (3 * C, C), jnp.float32) * s
        bpre = jnp.zeros((C,), jnp.float32)
        A_S = 4 * 3
        Wpost = jax.random.normal(ks[7], ((A_S + 1) * C, C), jnp.float32) * s
        bpost = jnp.zeros((C,), jnp.float32)
        Wih = jax.random.normal(ks[8], (C, 3 * C), jnp.float32) * s
        bih = jnp.zeros((3 * C,), jnp.float32)
        Whh = jax.random.normal(ks[9], (C, 3 * C), jnp.float32) * s
        bhh = jnp.zeros((3 * C,), jnp.float32)
        return dict(x=x, edge_attr=edge_attr, deg_hist=deg_hist, W=W, We=We, be=be, Wpre=Wpre, bpre=bpre, Wpost=Wpost, bpost=bpost, Wih=Wih, bih=bih, Whh=Whh, bhh=bhh, edge_index=edge_index)
    _L1_gnn_all = _L1_gnn_setup()
    _L1_gnn_in = {k: v for k, v in _L1_gnn_all.items() if k in ('W', 'We', 'be', 'Wpre', 'bpre', 'Wpost', 'bpost', 'Wih', 'bih', 'Whh', 'bhh')}
    del _L1_gnn_all

    def _L2_gnn_setup():
        import jax, jax.numpy as jnp
        import numpy as np
        N_NODES = 6250
        N_EDGES = 100000
        D_IN, D_HID, D_OUT = (64, 128, 64)

        def _gin_conv(h, src, dst, Wa, ba, Wb, bb, num_nodes):
            agg = jax.ops.segment_sum(h[src], dst, num_segments=num_nodes)
            z = h + agg
            z = jax.nn.relu(z @ Wa + ba)
            return z @ Wb + bb
        key = jax.random.key(seed)
        ks = jax.random.split(key, 12)
        s = lambda d: 1.0 / np.sqrt(d)
        return {'x': jax.random.normal(ks[0], (N_NODES, D_IN), dtype=jnp.float32), 'edge_index': jax.random.randint(ks[1], (2, N_EDGES), 0, N_NODES, dtype=jnp.int64), 'W1a': jax.random.uniform(ks[2], (D_IN, D_HID), jnp.float32, -s(D_IN), s(D_IN)), 'b1a': jnp.zeros((D_HID,), jnp.float32), 'W1b': jax.random.uniform(ks[3], (D_HID, D_HID), jnp.float32, -s(D_HID), s(D_HID)), 'b1b': jnp.zeros((D_HID,), jnp.float32), 'W2a': jax.random.uniform(ks[4], (D_HID, D_HID), jnp.float32, -s(D_HID), s(D_HID)), 'b2a': jnp.zeros((D_HID,), jnp.float32), 'W2b': jax.random.uniform(ks[5], (D_HID, D_HID), jnp.float32, -s(D_HID), s(D_HID)), 'b2b': jnp.zeros((D_HID,), jnp.float32), 'Wlin': jax.random.uniform(ks[6], (D_HID, D_OUT), jnp.float32, -s(D_HID), s(D_HID)), 'blin': jnp.zeros((D_OUT,), jnp.float32)}
    _L2_gnn_all = _L2_gnn_setup()
    _L2_gnn_in = {k: v for k, v in _L2_gnn_all.items() if k in ('W1a', 'b1a', 'W1b', 'b1b', 'W2a', 'b2a', 'W2b', 'b2b', 'Wlin', 'blin')}
    del _L2_gnn_all

    def _L3_gnn_setup():
        import jax, jax.numpy as jnp
        import numpy as np
        N_NODES = 6250
        HIDDEN = 64
        N_REL = 9
        N_LAYERS = 3
        N_EDGES = 62500
        key = jax.random.key(seed)
        k1, k2, k3, k4, k5 = jax.random.split(key, 5)
        edge_index = jax.random.randint(k1, (2, N_EDGES), 0, N_NODES, dtype=jnp.int64)
        edge_type = jax.random.randint(k2, (N_EDGES,), 0, N_REL, dtype=jnp.int64)
        embeddings = jax.random.uniform(k3, (N_NODES, HIDDEN), dtype=jnp.float32)
        weights = jax.random.uniform(k4, (N_LAYERS, 2 * N_REL, HIDDEN, HIDDEN), dtype=jnp.float32)
        biases = jax.random.uniform(k5, (N_LAYERS, 2 * N_REL, HIDDEN), dtype=jnp.float32)
        return {'edge_index': edge_index, 'edge_type': edge_type, 'embeddings': embeddings, 'weights': weights, 'biases': biases}
    _L3_gnn_all = _L3_gnn_setup()
    _L3_gnn_in = {k: v for k, v in _L3_gnn_all.items() if k in ('weights', 'biases')}
    del _L3_gnn_all
    return {'x': x, 'src': src, 'dst': dst, 'edge_attr_4': edge_attr_4, 'edge_type_9': edge_type_9, 'node_vec': node_vec, 'L0_gnn_Wq': _L0_gnn_in['Wq'], 'L0_gnn_bq': _L0_gnn_in['bq'], 'L0_gnn_Wk': _L0_gnn_in['Wk'], 'L0_gnn_bk': _L0_gnn_in['bk'], 'L0_gnn_Wv': _L0_gnn_in['Wv'], 'L0_gnn_bv': _L0_gnn_in['bv'], 'L0_gnn_Wo': _L0_gnn_in['Wo'], 'L0_gnn_bo': _L0_gnn_in['bo'], 'L0_gnn_Wf': _L0_gnn_in['Wf'], 'L0_gnn_bf': _L0_gnn_in['bf'], 'L0_gnn_gamma': _L0_gnn_in['gamma'], 'L0_gnn_beta': _L0_gnn_in['beta'], 'L1_gnn_W': _L1_gnn_in['W'], 'L1_gnn_We': _L1_gnn_in['We'], 'L1_gnn_be': _L1_gnn_in['be'], 'L1_gnn_Wpre': _L1_gnn_in['Wpre'], 'L1_gnn_bpre': _L1_gnn_in['bpre'], 'L1_gnn_Wpost': _L1_gnn_in['Wpost'], 'L1_gnn_bpost': _L1_gnn_in['bpost'], 'L1_gnn_Wih': _L1_gnn_in['Wih'], 'L1_gnn_bih': _L1_gnn_in['bih'], 'L1_gnn_Whh': _L1_gnn_in['Whh'], 'L1_gnn_bhh': _L1_gnn_in['bhh'], 'L2_gnn_W1a': _L2_gnn_in['W1a'], 'L2_gnn_b1a': _L2_gnn_in['b1a'], 'L2_gnn_W1b': _L2_gnn_in['W1b'], 'L2_gnn_b1b': _L2_gnn_in['b1b'], 'L2_gnn_W2a': _L2_gnn_in['W2a'], 'L2_gnn_b2a': _L2_gnn_in['b2a'], 'L2_gnn_W2b': _L2_gnn_in['W2b'], 'L2_gnn_b2b': _L2_gnn_in['b2b'], 'L2_gnn_Wlin': _L2_gnn_in['Wlin'], 'L2_gnn_blin': _L2_gnn_in['blin'], 'L3_gnn_weights': _L3_gnn_in['weights'], 'L3_gnn_biases': _L3_gnn_in['biases']}

def reference(x, src, dst, edge_attr_4, edge_type_9, node_vec, L0_gnn_Wq, L0_gnn_bq, L0_gnn_Wk, L0_gnn_bk, L0_gnn_Wv, L0_gnn_bv, L0_gnn_Wo, L0_gnn_bo, L0_gnn_Wf, L0_gnn_bf, L0_gnn_gamma, L0_gnn_beta, L1_gnn_W, L1_gnn_We, L1_gnn_be, L1_gnn_Wpre, L1_gnn_bpre, L1_gnn_Wpost, L1_gnn_bpost, L1_gnn_Wih, L1_gnn_bih, L1_gnn_Whh, L1_gnn_bhh, L2_gnn_W1a, L2_gnn_b1a, L2_gnn_W1b, L2_gnn_b1b, L2_gnn_W2a, L2_gnn_b2a, L2_gnn_W2b, L2_gnn_b2b, L2_gnn_Wlin, L2_gnn_blin, L3_gnn_weights, L3_gnn_biases):
    import jax
    import jax.numpy as jnp

    def _L0_gnn_ref(feats, Wq, bq, Wk, bk, Wv, bv, Wo, bo, Wf, bf, gamma, beta, src, dst):
        import jax, jax.numpy as jnp
        import numpy as np
        N = 3125
        E = 50000
        IN = 64
        H = 4
        D = 16
        OH = H * D
        SCALE = float(np.sqrt(IN))
        LN_EPS = 1e-05
        n = feats.shape[0]
        q = (feats @ Wq + bq).reshape(n, H, D)
        k = (feats @ Wk + bk).reshape(n, H, D)
        v = (feats @ Wv + bv).reshape(n, H, D)
        score = jnp.sum(k[src] * q[dst], axis=-1)
        score = jnp.exp(jnp.clip(score / SCALE, -5.0, 5.0))
        wv = jax.ops.segment_sum(v[src] * score[..., None], dst, num_segments=n)
        z = jax.ops.segment_sum(score, dst, num_segments=n)
        wv = wv / (z[..., None] + 1.0)
        o = wv.reshape(n, OH) @ Wo + bo
        h = feats @ Wf + bf + o
        mu = jnp.mean(h, axis=-1, keepdims=True)
        var = jnp.var(h, axis=-1, keepdims=True)
        ln = (h - mu) * jax.lax.rsqrt(var + LN_EPS) * gamma + beta
        return h + ln

    def _L1_gnn_ref(x, edge_attr, deg_hist, W, We, be, Wpre, bpre, Wpost, bpost, Wih, bih, Whh, bhh, edge_index):
        import jax, jax.numpy as jnp
        import numpy as np
        N = 3125
        E = 50000
        C = 64
        n_nodes = x.shape[0]
        m = x @ W
        src, dst = (edge_index[0], edge_index[1])
        ew = edge_attr[:, 3:4]
        ea = edge_attr[:, :3] @ We + be
        xi = ew * m[dst]
        xj = ew * m[src]
        ea = ew * ea
        h = jnp.concatenate([xi, xj, ea], axis=-1) @ Wpre + bpre
        ones = jnp.ones((h.shape[0],), h.dtype)
        cnt = jax.ops.segment_sum(ones, dst, num_segments=n_nodes)
        safe = jnp.maximum(cnt, 1.0)[:, None]
        s1 = jax.ops.segment_sum(h, dst, num_segments=n_nodes)
        s2 = jax.ops.segment_sum(h * h, dst, num_segments=n_nodes)
        mean = s1 / safe
        mean_sq = s2 / safe
        std = jnp.sqrt(jax.nn.relu(mean_sq - mean * mean) + 1e-05)
        has = (cnt > 0)[:, None]
        mn = jnp.where(has, jax.ops.segment_min(h, dst, num_segments=n_nodes), 0.0)
        mx = jnp.where(has, jax.ops.segment_max(h, dst, num_segments=n_nodes), 0.0)
        agg = jnp.concatenate([mean, mn, mx, std], axis=-1)
        deg = jnp.maximum(cnt, 1.0)[:, None]
        avg_log = jnp.mean(jnp.log(deg_hist + 1.0))
        logd = jnp.log(deg + 1.0)
        o1 = agg
        o2 = o1 * (logd / avg_log)
        o3 = o2 * (avg_log / logd)
        out = jnp.concatenate([o1, o2, o3], axis=-1)
        out = jnp.concatenate([m, out], axis=-1) @ Wpost + bpost
        gi = out @ Wih + bih
        gh = x @ Whh + bhh
        ir, iz, i_n = jnp.split(gi, 3, axis=-1)
        hr, hz, h_n = jnp.split(gh, 3, axis=-1)
        r = jax.nn.sigmoid(ir + hr)
        z = jax.nn.sigmoid(iz + hz)
        n = jnp.tanh(i_n + r * h_n)
        return (1.0 - z) * n + z * x

    def _L2_gnn_ref(x, edge_index, W1a, b1a, W1b, b1b, W2a, b2a, W2b, b2b, Wlin, blin):
        import jax, jax.numpy as jnp
        import numpy as np
        N_NODES = 6250
        N_EDGES = 100000
        D_IN, D_HID, D_OUT = (64, 128, 64)

        def _gin_conv(h, src, dst, Wa, ba, Wb, bb, num_nodes):
            agg = jax.ops.segment_sum(h[src], dst, num_segments=num_nodes)
            z = h + agg
            z = jax.nn.relu(z @ Wa + ba)
            return z @ Wb + bb
        n = x.shape[0]
        src, dst = (edge_index[0], edge_index[1])
        h = jax.nn.relu(_gin_conv(x, src, dst, W1a, b1a, W1b, b1b, n))
        h = jax.nn.relu(_gin_conv(h, src, dst, W2a, b2a, W2b, b2b, n))
        return h @ Wlin + blin

    def _L3_gnn_ref(edge_index, edge_type, embeddings, weights, biases):
        import jax, jax.numpy as jnp
        import numpy as np
        N_NODES = 6250
        HIDDEN = 64
        N_REL = 9
        N_LAYERS = 3
        N_EDGES = 62500
        N, E = embeddings.shape
        L = weights.shape[0]
        R = weights.shape[1] // 2
        idx0 = edge_index[0]
        idx1 = edge_index[1]
        rel0 = edge_type
        rel1 = edge_type + R
        output = embeddings
        for l in range(L):
            T = jnp.einsum('ne,reo->rno', embeddings, weights[l])
            m0 = T[rel0, idx0] + biases[l][rel0]
            m1 = T[rel1, idx1] + biases[l][rel1]
            m = jnp.concatenate([m0, m1], axis=0)
            d = jnp.concatenate([idx0, idx1], axis=0)
            s = jax.ops.segment_sum(m, d, num_segments=N)
            cnt = jax.ops.segment_sum(jnp.ones((d.shape[0],), m.dtype), d, num_segments=N)
            hidden = jnp.where(cnt[:, None] > 0, s / jnp.maximum(cnt, 1.0)[:, None], 0.0)
            if l + 1 < L:
                hidden = jax.nn.relu(hidden)
            output = hidden
        return output
    edge_index = jnp.stack([src, dst])
    x = _layernorm(x + _L0_gnn_ref(x, L0_gnn_Wq, L0_gnn_bq, L0_gnn_Wk, L0_gnn_bk, L0_gnn_Wv, L0_gnn_bv, L0_gnn_Wo, L0_gnn_bo, L0_gnn_Wf, L0_gnn_bf, L0_gnn_gamma, L0_gnn_beta, src, dst), axis=-1)
    x = _layernorm(x + _L1_gnn_ref(x, edge_attr_4, node_vec, L1_gnn_W, L1_gnn_We, L1_gnn_be, L1_gnn_Wpre, L1_gnn_bpre, L1_gnn_Wpost, L1_gnn_bpost, L1_gnn_Wih, L1_gnn_bih, L1_gnn_Whh, L1_gnn_bhh, edge_index), axis=-1)
    x = _layernorm(x + _L2_gnn_ref(x, edge_index, L2_gnn_W1a, L2_gnn_b1a, L2_gnn_W1b, L2_gnn_b1b, L2_gnn_W2a, L2_gnn_b2a, L2_gnn_W2b, L2_gnn_b2b, L2_gnn_Wlin, L2_gnn_blin), axis=-1)
    x = _layernorm(x + _L3_gnn_ref(edge_index, edge_type_9, x, L3_gnn_weights, L3_gnn_biases), axis=-1)
    return x

_drawn_inputs = setup_inputs


def setup_inputs(seed=0):
    import zlib

    import numpy as np

    out = dict(_drawn_inputs(seed))
    spreads = {'L0_gnn_bq': (0.0, 0.8),
     'L0_gnn_bk': (0.0, 2.0),
     'L0_gnn_bv': (0.0, 0.1),
     'L0_gnn_bo': (0.0, 0.1),
     'L0_gnn_bf': (0.0, 0.1),
     'L0_gnn_gamma': (1.0, 0.2),
     'L0_gnn_beta': (0.0, 0.1),
     'L1_gnn_be': (0.0, 0.8),
     'L1_gnn_bpre': (0.0, 2.0),
     'L1_gnn_bpost': (0.0, 2.0),
     'L1_gnn_bih': (0.0, 0.8),
     'L1_gnn_bhh': (0.0, 0.8),
     'L2_gnn_b1a': (0.0, 2.0),
     'L2_gnn_b1b': (0.0, 0.411),
     'L2_gnn_b2a': (0.0, 2.0),
     'L2_gnn_b2b': (0.0, 2.0),
     'L2_gnn_blin': (0.0, 0.52)}
    factors = {'edge_attr_4': 30.807,
     'node_vec': 8.0,
     'L0_gnn_Wq': 8.0,
     'L0_gnn_Wk': 8.0,
     'L0_gnn_Wv': 4.691,
     'L1_gnn_We': 8.0,
     'L1_gnn_Wpre': 2.78,
     'L1_gnn_Whh': 6.483}
    for name, (base, spread) in spreads.items():
        noise = np.random.default_rng([zlib.crc32(name.encode()), seed]).standard_normal(out[name].shape)
        drawn = base * np.exp(spread * noise) if base else spread * noise
        out[name] = jnp.asarray(drawn.astype(out[name].dtype))
    for name, factor in factors.items():
        out[name] = (out[name] * factor).astype(out[name].dtype)
    return out
```

```python
from contextlib import ExitStack, nullcontext

import concourse.bass as bass
from concourse import mybir

F32 = mybir.dt.float32
BF16 = mybir.dt.bfloat16
I32 = mybir.dt.int32
I16 = mybir.dt.int16
ALU = mybir.AluOpType
ACT = mybir.ActivationFunctionType
X_AXIS = mybir.AxisListType.X

P = 128
N, E, C, R = 3125, 100000, 64, 9
NB = 25
NP = NB * P
NV = N // NB
HEADS, HD = 4, 16
SLOTS = 16
SUB = 4
REC = 6
EP, EW = 80, 1250
ROW = 125
NROW = E // ROW
NSTAGE = 2
STEPS = 6400
SP_ = STEPS // P
HT, HI = 16, 25
KEY = 4096.0
BIG = 1.0e30
EPS = 1e-5
GROUPS = [list(range(g, min(g + 4, NB))) for g in range(0, NB, 4)]
PAIRS = [list(range(g, min(g + 2, NB))) for g in range(0, NB, 2)]


def build(nc, a, out):
    dram = lambda name, shape, dt=F32: nc.dram_tensor(name, shape, dt, kind="Internal").ap()
    rec_tab = dram("rec_tab", [E + SLOTS, REC], I32)
    tmin_tab = dram("tmin_tab", [NROW])
    start_tab = dram("start_tab", [NP + 1])
    key_tab = dram("key_tab", [NP])
    info_tab = dram("info_tab", [NP, 3], I32)
    blk_tab = dram("blk_tab", [STEPS], I16)
    left_tab = dram("left_tab", [STEPS], I16)
    kv_tab = dram("kv_tab", [NP, 2 * C])
    own_tab = dram("own_tab", [NP, 3 * C])
    b_tab = dram("b_tab", [NP, C])
    x2_tab = dram("x2_tab", [NP, C])
    h1_tab = dram("h1_tab", [NP, 2 * C])
    cnt_tab = dram("cnt_tab", [NP, R])

    with ExitStack() as ctx:
        sb = lambda name, shape, dt=F32: ctx.enter_context(nc.sbuf_tensor(name, shape, dt))
        sem = lambda name: ctx.enter_context(nc.semaphore(name))

        arena = sb("arena", [P, 26600])

        def at(off, parts, *shape, dt=F32):
            n = 1
            for s in shape:
                n *= s
            v = arena[0:parts, off:off + n]
            if dt != F32:
                v = v.bitcast(dt)
            if len(shape) == 2:
                v = v.rearrange("p (a b) -> p a b", b=shape[1])
            if len(shape) == 3:
                v = v.rearrange("p (a b c) -> p a b c", b=shape[1], c=shape[2])
            return v

        rec_sb = at(0, EP, EW, REC, dt=I32)
        attr_sb = at(7500, EP, EW, 4)
        dst_sb = at(12500, EP, EW, dt=I32)
        src_sb = at(13750, EP, EW, dt=I32)
        typ_sb = at(15000, EP, EW, dt=I32)
        keyB = at(16250, P, NP)
        dstrow = at(19450, P, NB, ROW, dt=I32)
        junk_dve = at(22575, P, NP)
        tminB = at(25775, P, NROW)
        junk_act = at(12500, P, NP)
        ind3 = at(16250, P, SP_, NB)
        indw = at(17500, P, SP_, NB)
        G = [at(0, P, SLOTS, 2 * C), at(2048, P, SLOTS, 2 * C)]
        G1 = [at(0, P, SLOTS, C), at(2048, P, SLOTS, C)]
        prod = at(4096, P, SLOTS, 2 * C)
        weighted = at(6144, P, SLOTS, C + HEADS)
        ownR = at(7296, P, NB, 3 * C)
        accV = at(12100, P, NB, C + HEADS)
        hsrc = at(19450, ROW, NROW, dt=I32)
        accMx = at(14100, P, NB, C)
        accMn = at(15700, P, NB, C)
        accS1 = at(17300, P, NB, C)
        accS2 = at(18900, P, NB, C)
        aR = at(20500, P, NB, C)
        mpR = at(22100, P, NB, C)
        sR = at(23700, P, NB, C)
        agg = at(7296, P, NB, 4, C)
        aggT = [at(14100, P, NP), at(17300, P, NP)]
        gates = at(0, P, NB, 4 * C)
        h1R = at(7296, P, NB, 2 * C)
        acc3 = at(10496, P, NB, 2 * C)
        acc2 = at(14100, P, NB, C)
        hT = at(15700, P, NP)
        cntR = at(18900, P, NB, 2, R)
        prodL3 = at(0, P, 2 * R * C)
        sumL3 = at(23700, P, NB, C)

        T1 = sb("T1", [P, NP])
        T2 = sb("T2", [P, NP])
        xN = sb("xN", [P, NB, C])
        x1R = sb("x1R", [P, NB, C])
        stepB = sb("step_block", [1, STEPS], I16)
        stepL = sb("step_left", [1, STEPS], I16)
        stage = sb("stage", [P, NSTAGE, 2, 4 * C])
        accT = sb("accT", [P, NB, R])
        histo = sb("histo", [P, NB * R])
        rec = [sb(f"rec{u}", [P, SLOTS, REC], I32) for u in range(2)]
        win = [sb(f"win{u}", [P, 1], I32) for u in range(2)]
        mask = sb("mask", [P, SLOTS])
        neg = sb("neg", [P, SLOTS])
        pos = sb("pos", [P, SLOTS])
        ewm = sb("ewm", [P, SLOTS])
        eam = sb("eam", [P, 3, SLOTS])
        score = [sb(f"score{u}", [P, SLOTS, HEADS]) for u in range(2)]
        expd = [sb(f"expd{u}", [P, SLOTS, HEADS]) for u in range(2)]
        red = sb("red", [P, 2 * C + 4])
        eqt = sb("eqt", [P, R, SLOTS])
        redt = sb("redt", [P, R])
        oh_lo = sb("oh_lo", [ROW, 2, 4, P], BF16)
        oh_hi = sb("oh_hi", [ROW, 2, 4, NB * R], BF16)
        part = at(21050, ROW, NROW)
        code = at(21850, ROW, NROW)
        htyp = at(22650, ROW, NROW, dt=I32)
        zerosb = sb("zerosb", [P, NB * R], BF16)

        ident = sb("ident", [P, P])
        nodeI = sb("nodeI", [P, NB], I32)
        nodeF = sb("nodeF", [P, NB])
        slotI = sb("slotI", [P, SLOTS], I32)
        slotF = sb("slotF", [P, SLOTS])
        relI = sb("relI", [P, R], I32)
        relF = sb("relF", [P, R])
        laneI = sb("laneI", [P, P], I16)
        codeI = sb("codeI", [P, NB * R], I16)
        gI = sb("gI", [P, SP_], I32)
        gF = sb("gF", [P, SP_])
        triI = sb("triI", [NB, NB])
        triE = sb("triE", [NB, NB])
        zrow = sb("zrow", [1, SLOTS * REC])
        small = sb("small", [P, 24, NB])
        smallI = sb("smallI", [P, 6, NB], I32)
        info = sb("info", [P, NB, 3], I32)
        infoR = sb("infoR", [P, NB, 3], I32)
        bcast = sb("bcast", [NB, 2, P])
        cum = sb("cum", [P, 3, NB])
        fval = sb("fval", [P, 2, NB])
        tabF = sb("tabF", [P, 2, SP_])
        tabI = sb("tabI", [P, 2, SP_], I16)
        totI = sb("totI", [P, 2], I32)
        totF = sb("totF", [P, 2])
        nv = sb("nv", [P, NB])
        lsum = sb("lsum", [P, 2])
        ones = sb("ones", [P, P])
        epsb = sb("epsb", [P, 1])

        Wkvqf = sb("Wkvqf", [C + 1, 4 * C])
        Wo = sb("Wo", [C + 1, C])
        W1 = sb("W1", [C, C])
        Wabm = sb("Wabm", [C + 1, 3 * C])
        Wedge = sb("Wedge", [C, C])
        WeT = sb("WeT", [C, 4])
        WeB = at(16250, C, 4, P)
        edgeB = sb("edgeB", [P, 4, C])
        Wpost = sb("Wpost", [P, 3, 2, C])
        Wagg = sb("Wagg", [P, 2, 2, C])
        Wih = sb("Wih", [C + 1, 3 * C])
        Whh = sb("Whh", [C + 1, 3 * C])
        W1a = sb("W1a", [C, 2 * C])
        W1b = sb("W1b", [P, 2 * C])
        W2a = sb("W2a", [P, 2 * C])
        W2b = sb("W2b", [P, 2 * C])
        bcol = sb("bcol", [P, 4])
        Wlin = sb("Wlin", [P, C])
        rowsB = sb("rowsB", [P, 4, C])
        Wrel = sb("Wrel", [C + 1, 2 * R, C])

        tp = ctx.enter_context(nc.psum_tensor("tp", [P, 2, 512], F32))
        mm = ctx.enter_context(nc.psum_tensor("mm", [P, 2, 512], F32))
        l3 = ctx.enter_context(nc.psum_tensor("l3", [P, 3, 512], F32))
        hist = ctx.enter_context(nc.psum_tensor("hist", [P, 512], F32))

        consts = sem("consts")
        x_in = sem("x_in")
        edges_in, pads_clear = sem("edges_in"), sem("pads_clear")
        w_in = sem("w_in")
        tmin_cast, tmin_out, tmin_in = sem("tmin_cast"), sem("tmin_out"), sem("tmin_in")
        rec_built, rec_out = sem("rec_built"), sem("rec_out")
        row_index, row_in = sem("row_index"), sem("row_in")
        start_done, start_out, end_in = sem("start_done"), sem("start_out"), sem("end_in")
        key_done, key_out, key_in = sem("key_done"), sem("key_out"), sem("key_in")
        rank_act, rank_done = sem("rank_act"), sem("rank_done")
        info_out, info_in = sem("info_out"), sem("info_in")
        deg_done, degT_full, nit_done, cum_full = sem("deg_done"), sem("degT_full"), sem("nit_done"), sem("cum_full")
        steps_done, steps_out, steps_in = sem("steps_done"), sem("steps_out"), sem("steps_in")
        tp_full, tp_evac = sem("tp_full"), sem("tp_evac")
        mm_full, mm_evac = sem("mm_full"), sem("mm_evac")
        act_q, act_r = sem("act_q"), sem("act_r")
        stage_out = [sem(f"stage_out{k}") for k in range(NSTAGE)]
        stage_ready, own_x_out = sem("stage_ready"), sem("own_x_out")
        we_spread, row_cmp = sem("we_spread"), sem("row_cmp")
        own_in = sem("own_in")
        x1_done, x2_done, wv_done, ab_done, agg_done, out_done = (
            sem(n) for n in ("x1_done", "x2_done", "wv_done", "ab_done", "agg_done", "out_done"))
        b_out, x2_out, h1_done, h1_out = sem("b_out"), sem("x2_out"), sem("h1_done"), sem("h1_out")
        z_done = sem("z_done")
        edge_full = sem("edge_full")
        hist_in, hist_oh, hist_mm, hist_done, hist_out, hist_back = (
            sem(n) for n in ("hist_in", "hist_oh", "hist_mm", "hist_done", "hist_out", "hist_back"))
        cnt_in = sem("cnt_in")
        x3_done, l3_full, l3_used, final_done, final_out = (
            sem(n) for n in ("x3_done", "l3_full", "l3_used", "final_done", "final_out"))
        pool_steps = sem("pool_steps")
        score_ready, exp_ready = sem("score_ready"), sem("exp_ready")

        class Gather:

            def __init__(self, name):
                self.win_ready = sem(name + "_win_ready")
                self.rec_landed = [sem(f"{name}_rec_landed{u}") for u in range(2)]
                self.rows_landed = [sem(f"{name}_rows_landed{u}") for u in range(2)]
                self.free = sem(name + "_free")

        LOOP0, LOOP1, LOOP2, LOOP3 = (Gather(f"loop{n}") for n in range(4))

        block = ctx.enter_context(nc.Block())
        NCONST = 11
        NW = 42
        RANK_DVE = 12
        TP_H1 = 8 * len(GROUPS)
        MM_MLP = [2 * len(GROUPS) + 1 + len(GROUPS) + 3 * len(PAIRS), 5 * len(GROUPS) + 1 + len(GROUPS) - len(GROUPS) + 3 * len(PAIRS)]
        tmin_small = at(26575, EP, 10)
        hsrc_q = at(20250, ROW, NROW, dt=I32)

        K_, CNT_, START_, END_, DEG_, KEYN_, NKEY_, RANK_, RA_, RB_, DEGR_, PTR_, REM_, MAXD_, NIT_, ZP_, SAFE_, HAS_, RATIO_, MU_, VAR_, STD_, LOGD_, CNTT_ = range(24)
        S = lambda k: small[:, k, :]
        SI = lambda k: smallI[:, k, :]

        def bc(ap2, n):
            return ap2.unsqueeze(2).to_broadcast([ap2.shape[0], ap2.shape[1], n])

        def bm(ap2, n):
            return ap2.unsqueeze(1).to_broadcast([ap2.shape[0], n, ap2.shape[1]])

        @block.sync
        def _(sp):
            dma = sp.dma_start
            row = lambda v: v.rearrange("(a n) -> a n", a=1)
            dma(dst_sb, a["dst"].rearrange("(p n) -> p n", p=EP)).then_inc(edges_in, 16)
            dma(src_sb, a["src"].rearrange("(p n) -> p n", p=EP)).then_inc(edges_in, 16)
            dma(typ_sb, a["edge_type_9"].rearrange("(p n) -> p n", p=EP)).then_inc(edges_in, 16)
            dma(attr_sb, a["edge_attr_4"].rearrange("(p n) c -> p n c", p=EP)).then_inc(edges_in, 16)
            sp.wait_ge(pads_clear, 1)
            dma(xN[0:NV], a["x"].rearrange("(p b) c -> p b c", b=NB)).then_inc(x_in, 16)
            dma(nv[0:NV], a["node_vec"].rearrange("(p b) -> p b", b=NB)).then_inc(x_in, 16)
            sp.wait_ge(tmin_cast, 1)
            dma(tmin_tab.rearrange("(p n) -> p n", p=EP), tmin_small).then_inc(tmin_out, 16)
            sp.wait_ge(tmin_out, 16)
            dma(tminB, row(tmin_tab).to_broadcast([P, NROW])).then_inc(tmin_in, 16)
            sp.wait_ge(rec_built, 1)
            dma(rec_tab[0:E, :].rearrange("(p n) c -> p n c", p=EP), rec_sb).then_inc(rec_out, 16)
            dma(rec_tab[E:, :].rearrange("(a n) c -> a (n c)", a=1), zrow[:].bitcast(I32)).then_inc(rec_out, 16)
            kv_rows = kv_tab.rearrange("(p b) c -> p b c", b=NB)
            own_rows = own_tab.rearrange("(p b) c -> p b c", b=NB)
            dma(own_rows[:, :, 2 * C:], xN[:]).then_inc(own_x_out, 16)
            for k, pair in enumerate(PAIRS):
                s, b = k % NSTAGE, slice(pair[0], pair[-1] + 1)
                sp.wait_ge(stage_ready, k + 1)
                dma(kv_rows[:, b], stage[:, s, 0:len(pair), 0:2 * C]).then_inc(stage_out[s], 16)
                dma(own_rows[:, b, 0:2 * C], stage[:, s, 0:len(pair), 2 * C:]).then_inc(stage_out[s], 16)
            sp.wait_ge(start_done, 1)
            dma(start_tab[0:NP].rearrange("(p b) -> p b", b=NB), S(START_)).then_inc(start_out, 16)
            dma(start_tab[NP:].rearrange("(a n) -> a n", a=1), totF[0:1, 1:2]).then_inc(start_out, 16)
            sp.wait_ge(start_out, 32)
            dma(S(END_), start_tab[1:].rearrange("(p b) -> p b", b=NB)).then_inc(end_in, 16)
            sp.wait_ge(key_done, 1)
            dma(key_tab.rearrange("(p b) -> p b", b=NB), S(KEYN_)).then_inc(key_out, 16)
            sp.wait_ge(key_out, 16)
            dma(keyB, row(key_tab).to_broadcast([P, NP])).then_inc(key_in, 16)
            sp.wait_ge(info_out, 16 * NB)
            dma(infoR[:], info_tab.rearrange("(p b) c -> p b c", b=NB)).then_inc(info_in, 16)
            sp.wait_ge(steps_done, 1)
            dma(blk_tab.rearrange("(p n) -> p n", p=P), tabI[:, 0]).then_inc(steps_out, 16)
            dma(left_tab.rearrange("(p n) -> p n", p=P), tabI[:, 1]).then_inc(steps_out, 16)
            sp.wait_ge(steps_out, 32)
            dma(stepB[:], row(blk_tab)).then_inc(steps_in, 16)
            dma(stepL[:], row(left_tab)).then_inc(steps_in, 16)
            dma(hsrc, a["src"].rearrange("(p n) -> p n", p=ROW)).then_inc(hist_in, 16)
            dma(htyp, a["edge_type_9"].rearrange("(p n) -> p n", p=ROW)).then_inc(hist_in, 16)
            sp.wait_ge(hist_done, 1)
            dma(cnt_tab.rearrange("(p b) c -> p b c", b=NB),
                histo[:].rearrange("p (b c) -> p b c", c=R)).then_inc(hist_out, 16)


        @block.gpsimd
        def _(pool):
            pool.iota(nodeI[:], pattern=[[1, NB]], base=0, channel_multiplier=NB).then_inc(consts, 1)
            pool.iota(slotI[:], pattern=[[1, SLOTS]], base=0, channel_multiplier=0).then_inc(consts, 1)
            pool.iota(relI[:], pattern=[[1, R]], base=0, channel_multiplier=0).then_inc(consts, 1)
            pool.iota(gI[:], pattern=[[1, SP_]], base=0, channel_multiplier=SP_).then_inc(consts, 1)
            pool.iota(laneI[:], pattern=[[1, P]], base=0, channel_multiplier=0,
                      allow_small_or_imprecise_dtypes=True).then_inc(consts, 1)
            pool.iota(codeI[:], pattern=[[1, NB * R]], base=0, channel_multiplier=0,
                      allow_small_or_imprecise_dtypes=True).then_inc(consts, 1)
            pool.memset(ident[:], 0.0)
            pool.memset(ones[:], 1.0).then_inc(consts, 1)
            pool.memset(triI[:], 0.0)
            pool.memset(triE[:], 0.0)
            pool.memset(zrow[:], 0.0).then_inc(consts, 1)
            pool.wait_ge(consts, 8)
            pool.drain()
            pool.affine_select(out=ident[:], in_=ident[:], compare_op=ALU.not_equal, fill=1.0, base=0,
                               pattern=[[-1, P]], channel_multiplier=1).then_inc(consts, 1)
            pool.affine_select(out=triI[:], in_=triI[:], compare_op=ALU.is_gt, fill=1.0, base=0,
                               pattern=[[-1, NB]], channel_multiplier=1).then_inc(consts, 1)
            pool.affine_select(out=triE[:], in_=triE[:], compare_op=ALU.is_ge, fill=1.0, base=0,
                               pattern=[[-1, NB]], channel_multiplier=1).then_inc(consts, 1)

            offs = bass.IndirectOffsetOnAxis

            def gather(dst, table, index):
                return pool.indirect_dma_start(dst, None, table, offs(ap=index, axis=0))

            def scatter(table, index, src, **kw):
                return pool.indirect_dma_start(table, offs(ap=index, axis=0), src, None, **kw)

            pool.wait_ge(row_index, 1)
            dst_rows = a["dst"].rearrange("(t n) -> t n", n=ROW)
            for b in range(NB):
                gather(dstrow[:, b], dst_rows, SI(0)[:, b:b + 1]).then_inc(row_in, 16)
            pool.wait_ge(rank_done, 1)
            for b in range(NB):
                scatter(info_tab, SI(3)[:, b:b + 1], info[:, b]).then_inc(info_out, 16)
            pool.wait_ge(info_in, 16)
            for k in range(NSTAGE):
                pool.wait_ge(stage_out[k], 32 * len(PAIRS[k::NSTAGE]))
            pool.wait_ge(own_x_out, 16)
            pool.wait_ge(rec_out, 32)
            for b in range(NB):
                gather(ownR[:, b], own_tab, infoR[:, b, 0:1]).then_inc(own_in, 16)

            def gather_loop(L, buf, table, base):
                pairs = pool.value_load(totI[0:1, 0:1], min_val=HI + 1, max_val=STEPS // 2 - 1)
                pool.wait_ge(L.win_ready, 1)
                gather(rec[0][:].rearrange("p s c -> p (s c)"), rec_tab, win[0][:]).then_inc(L.rec_landed[0], 16)
                with pool.Fori(0, pairs) as i:
                    for u in range(2):
                        left = pool.value_load(stepL[0:1, bass.ds(2 * i + u, 1)], min_val=0, max_val=SLOTS)
                        pool.wait_ge(L.rec_landed[u], 16 * (i + 1))
                        pool.wait_ge(L.free, 2 * i + u + 1)
                        pool.sem_inc(pool_steps, 1)
                        for s in range(SLOTS // SUB):
                            if s == 2:
                                pool.wait_ge(L.win_ready, 2 * i + u + 2)
                                pool.wait_ge(L.free, 2 * i + u + 2)
                                pool.sem_inc(pool_steps, 1)
                                gather(rec[1 - u][:].rearrange("p s c -> p (s c)"), rec_tab,
                                       win[1 - u][:]).then_inc(L.rec_landed[1 - u], 16)
                            with (pool.If(left >= s * SUB + 1) if s else nullcontext()):
                                for j in range(s * SUB, s * SUB + SUB):
                                    gather(buf[u][:, j], table, rec[u][:, j, 0:1]).then_inc(
                                        L.rows_landed[u], 16)
                pool.wait_ge(L.rec_landed[0], 16 * (pairs + 1))
                pool.sem_inc(pool_steps, 1)

            pool.wait_ge(steps_in, 32)
            gather_loop(LOOP0, G, kv_tab, 0)
            pool.wait_ge(ab_done, 1)
            for b in range(NB):
                scatter(b_tab, infoR[:, b, 0:1], sR[:, b]).then_inc(b_out, 16)
            pool.wait_ge(b_out, 16 * NB)
            gather_loop(LOOP1, G1, b_tab, 0)
            pool.wait_ge(x2_done, 1)
            for b in range(NB):
                scatter(x2_tab, infoR[:, b, 0:1], xN[:, b]).then_inc(x2_out, 16)
            pool.wait_ge(x2_out, 16 * NB)
            gather_loop(LOOP2, G1, x2_tab, 0)
            pool.wait_ge(tp_evac, TP_H1)
            for b in range(NB):
                scatter(h1_tab, infoR[:, b, 0:1], h1R[:, b]).then_inc(h1_out, 16)
            pool.wait_ge(h1_out, 16 * NB)
            gather_loop(LOOP3, G, h1_tab, 0)
            pool.wait_ge(hist_out, 16)
            pool.wait_ge(z_done, 2)
            for b in range(NB):
                gather(cntR[:, b, 0], cnt_tab, infoR[:, b, 0:1]).then_inc(cnt_in, 16)
            pool.wait_ge(final_done, 1)
            for b in range(NB):
                scatter(out, infoR[:, b, 0:1], sumL3[:, b], bounds_check=N - 1, oob_is_err=False).then_inc(
                    final_out, 16)
            pool.wait_ge(final_out, 16 * NB)

        @block.tensor
        def _(pe):
            ring = {"tp": 0, "mm": 0}

            def transpose_group(aps):
                k = ring["tp"]
                if k >= 2:
                    pe.wait_ge(tp_evac, k - 1)
                for j, ap in enumerate(aps):
                    last = pe.transpose(tp[0:ap.shape[1], k % 2, j * P:(j + 1) * P], ap, ident[:])
                last.then_inc(tp_full, 1)
                ring["tp"] = k + 1

            def transpose_all(src, w=None):
                for g in GROUPS:
                    transpose_group([src(b) for b in g])
                pe.wait_ge(tp_evac, ring["tp"])

            def product_group(parts):
                k = ring["mm"]
                if k >= 2:
                    pe.wait_ge(mm_evac, k - 1)
                for rows, cols, terms in parts:
                    for t, (l, r) in enumerate(terms):
                        last = pe.matmul(mm[0:rows, k % 2, cols[0]:cols[1]], l, r,
                                         start=(t == 0), stop=(t == len(terms) - 1))
                last.then_inc(mm_full, 1)
                ring["mm"] = k + 1

            cols = lambda b: slice(b * P, (b + 1) * P)

            pe.wait_ge(consts, NCONST)
            pe.wait_ge(pads_clear, 1)
            pe.wait_ge(x_in, 32)
            transpose_all(lambda b: xN[:, b])
            pe.wait_ge(w_in, 16 * NW)
            for pair in PAIRS:
                product_group([(P, (4 * C * j, 4 * C * (j + 1)), [(T1[0:C + 1, cols(b)], Wkvqf[:])])
                               for j, b in enumerate(pair)])
            pe.wait_ge(edge_full, 1)
            pe.wait_ge(we_spread, 1)
            product_group([(P, (C * j, C * (j + 1)), [(WeB[:, j], Wedge[:])]) for j in range(4)]
                          + [(P, (4 * C, 4 * C + 1), [(ones[0:NV, :], lsum[0:NV, 0:1])])])
            pe.wait_ge(deg_done, 1)
            pe.transpose(l3[0:NB, 0, 0:P], S(DEGR_), ident[:]).then_inc(degT_full, 1)
            pe.wait_ge(nit_done, 1)
            pe.matmul(l3[:, 1, 0:NB], bcast[:, 0], triI[:], start=True, stop=True)
            pe.matmul(l3[:, 1, NB:2 * NB], bcast[:, 0], triE[:], start=True, stop=True)
            pe.matmul(l3[:, 1, 2 * NB:3 * NB], bcast[:, 1], ident[0:NB, 0:NB], start=True, stop=True).then_inc(
                cum_full, 1)
            pe.wait_ge(hist_oh, 1)
            pe.matmul(hist[:, 0:NB * R], zerosb[:, 0:P], zerosb[:], start=True, stop=True)
            with pe.Fori(0, HI) as i:
                for u in range(2):
                    for q in range(4):
                        pe.wait_ge(hist_oh, 8 * i + 4 * u + q + 2)
                        for j in range(4):
                            last = pe.matmul(hist[:, 0:NB * R], oh_lo[:, q % 2, j], oh_hi[:, q % 2, j],
                                             start=False, stop=True, skip_group_check=True)
                        last.then_inc(hist_mm, 1)
            pe.wait_ge(wv_done, 1)
            transpose_all(lambda b: sR[:, b])
            for g in GROUPS:
                product_group([(P, (C * j, C * (j + 1)), [(T1[0:C + 1, cols(b)], Wo[:])])
                               for j, b in enumerate(g)])
            pe.wait_ge(x1_done, 1)
            transpose_all(lambda b: x1R[:, b])
            for g in GROUPS:
                product_group([(C, (0, P * len(g)), [(W1[:], T2[0:C, g[0] * P:(g[-1] + 1) * P])])])
            pe.wait_ge(mm_evac, ring["mm"])
            for pair in PAIRS:
                product_group([(P, (4 * C * j, 4 * C * j + 3 * C), [(T1[0:C + 1, cols(b)], Wabm[:])])
                               for j, b in enumerate(pair)])
            pe.wait_ge(agg_done, 1)
            for h in range(2):
                for g in GROUPS:
                    transpose_group([agg[:, b, 2 * h:2 * h + 2].rearrange("p a c -> p (a c)") for b in g])
            pe.wait_ge(tp_evac, ring["tp"])
            for g in GROUPS:
                product_group([(P, (P * j, P * (j + 1)),
                                [(aggT[h][:, cols(b)], Wagg[:, h].rearrange("p a c -> p (a c)")) for h in range(2)])
                               for j, b in enumerate(g)])
            pe.wait_ge(out_done, 1)
            transpose_all(lambda b: sR[:, b])
            for pair in PAIRS:
                parts = []
                for j, b in enumerate(pair):
                    o = 4 * C * j
                    xb, ob = T2[0:C + 1, cols(b)], T1[0:C + 1, cols(b)]
                    parts += [(P, (o, o + 2 * C), [(xb, Whh[:, 0:2 * C]), (ob, Wih[:, 0:2 * C])]),
                              (P, (o + 2 * C, o + 3 * C), [(ob, Wih[:, 2 * C:])]),
                              (P, (o + 3 * C, o + 4 * C), [(xb, Whh[:, 2 * C:])])]
                product_group(parts)

            def mlp(Wa, Wb, src, rows):
                transpose_all(src)
                for g in GROUPS:
                    product_group([(P, (0, P * len(g)), [(Wa[:], T1[0:rows, g[0] * P:(g[-1] + 1) * P])])])
                first = ring["mm"] - len(GROUPS)
                for n, g in enumerate(GROUPS):
                    pe.wait_ge(mm_evac, first + n + 1)
                    product_group([(P, (0, P * len(g)), [(Wb[:], T2[:, g[0] * P:(g[-1] + 1) * P])])])
                pe.wait_ge(mm_evac, ring["mm"])

            pe.wait_ge(z_done, 1)
            mlp(W1a, W1b, lambda b: sR[:, b], C)
            transpose_all(lambda b: hT[:, cols(b)])
            pe.wait_ge(z_done, 2)
            mlp(W2a, W2b, lambda b: h1R[:, b], P)
            for g in GROUPS:
                product_group([(P, (C * j, C * (j + 1)), [(hT[:, cols(b)], Wlin[:])]) for j, b in enumerate(g)])
            pe.wait_ge(x3_done, 1)
            transpose_all(lambda b: x1R[:, b])
            for b in range(NB):
                if b:
                    pe.wait_ge(l3_used, b)
                for j in range(3):
                    last = pe.matmul(l3[:, j, 0:6 * C], T1[0:C + 1, cols(b)],
                                     Wrel[:, 6 * j:6 * j + 6].rearrange("k r n -> k (r n)"), start=True, stop=True)
                last.then_inc(l3_full, 1)

        @block.scalar
        def _(act):
            row = lambda v: v.rearrange("(a n) -> a n", a=1)
            ring = {"tp": 0, "mm": 0, "q": 0}

            def copy_transposed(dst, n, width):
                k = ring["tp"]
                act.wait_ge(tp_full, k + 1)
                act.activation(dst, tp[0:width, k % 2, 0:n], ACT.Copy).then_inc(tp_evac, 1)
                ring["tp"] = k + 1

            def copy_all(dst, width):
                for g in GROUPS:
                    copy_transposed(dst[0:width, g[0] * P:(g[-1] + 1) * P], P * len(g), width)

            def asked():
                act.wait_ge(act_q, ring["q"] + 1)
                ring["q"] += 1

            n = 0

            def w(dst, src):
                nonlocal n
                act.dma_start(dst, src).then_inc(w_in, 16)
                n += 1

            row = lambda v: v.rearrange("(a n) -> a n", a=1)
            for j, k in enumerate(("k", "v", "q", "f")):
                w(Wkvqf[0:C, j * C:(j + 1) * C], a["L0_gnn_W" + k])
                w(Wkvqf[C:C + 1, j * C:(j + 1) * C], row(a["L0_gnn_b" + k]))
            w(Wo[0:C], a["L0_gnn_Wo"])
            w(Wo[C:C + 1], row(a["L0_gnn_bo"]))
            w(W1[:], a["L1_gnn_W"])
            for j in range(2):
                w(Wabm[0:C, j * C:(j + 1) * C], a["L1_gnn_Wpre"][j * C:(j + 1) * C, :])
            w(Wabm[0:C, 2 * C:], a["L1_gnn_Wpost"][0:C, :])
            w(Wabm[C:C + 1, 2 * C:], row(a["L1_gnn_bpost"]))
            w(Wedge[:], a["L1_gnn_Wpre"][2 * C:, :])
            for k in range(3):
                w(WeT[:, 1 + k:2 + k], a["L1_gnn_We"][k, :].rearrange("(n a) -> n a", a=1))
            w(WeT[:, 0:1], a["L1_gnn_be"].rearrange("(n a) -> n a", a=1))
            for j in range(3):
                w(Wpost[:, j], a["L1_gnn_Wpost"][(1 + 4 * j) * C:(5 + 4 * j) * C, :].rearrange(
                    "(h p) n -> p h n", p=P))
            for t, k in ((Wih, "ih"), (Whh, "hh")):
                w(t[0:C], a["L1_gnn_W" + k])
                w(t[C:C + 1], row(a["L1_gnn_b" + k]))
            for t, k in ((W1a, "1a"), (W1b, "1b"), (W2a, "2a"), (W2b, "2b"), (Wlin, "lin")):
                w(t[:], a["L2_gnn_W" + k])
            for j, k in enumerate(("b1a", "b1b", "b2a", "b2b")):
                w(bcol[:, j:j + 1], a["L2_gnn_" + k].rearrange("(n a) -> n a", a=1))
            for j, k in enumerate(("L0_gnn_gamma", "L0_gnn_beta", "L1_gnn_bpre", "L2_gnn_blin")):
                w(rowsB[:, j], row(a[k]).to_broadcast([P, C]))
            w(Wrel[0:C], a["L3_gnn_weights"][2].rearrange("r k n -> k r n"))
            w(Wrel[C:C + 1], a["L3_gnn_biases"][2:3])
            assert n == NW
            copy_all(T1, C)
            act.wait_ge(x_in, 32)
            act.activation(nv[:], nv[:], ACT.Ln, bias=ones[:, 0:1], accum_out=lsum[:, 0:1]).then_inc(edge_full, 1)
            act.wait_ge(key_in, 16)
            for b in range(RANK_DVE, NB):
                act.activation(junk_act, keyB, ACT.Sign, bias=S(NKEY_)[:, b:b + 1], accum_out=S(RANK_)[:, b:b + 1])
                last = act.drain()
            last.then_inc(rank_act, 1)
            act.wait_ge(steps_in, 32)
            pairs = act.value_load(totI[0:1, 0:1], min_val=HI + 1, max_val=STEPS // 2 - 1)
            with act.Fori(0, pairs) as i:
                for u in range(2):
                    act.wait_ge(score_ready, 2 * i + u + 1)
                    act.activation(expd[u][:], score[u][:], ACT.Exp, scale=1.0 / 8.0).then_inc(exp_ready, 1)
            copy_all(T1, C)

            def std(first=True):
                asked()
                act.activation(S(STD_), S(VAR_), ACT.Sqrt, bias=epsb[:], scale=1.0 / C).then_inc(act_r, 1)

            std()
            std()
            copy_all(T2, C)
            asked()
            act.activation(S(LOGD_), S(LOGD_), ACT.Ln, bias=ones[:, 0:1]).then_inc(act_r, 1)
            asked()
            act.activation(agg[:, :, 3], accS2, ACT.Sqrt, bias=epsb[:]).then_inc(act_r, 1)
            for h in range(2):
                copy_all(aggT[h], P)
            copy_all(T1, C)
            asked()
            act.activation(gates[:, :, 0:2 * C], gates[:, :, 0:2 * C], ACT.Sigmoid).then_inc(act_r, 1)
            asked()
            act.activation(sR, sR, ACT.Tanh).then_inc(act_r, 1)
            std()
            for first in (True, False):
                copy_all(T1, C if first else P)
                for layer in range(2):
                    for g in GROUPS:
                        k = MM_MLP[0 if first else 1] + layer * 7 + g[0] // 4
                        n = P * len(g)
                        act.wait_ge(mm_full, k + 1)
                        act.activation((T2 if layer == 0 else hT)[:, g[0] * P:g[0] * P + n], mm[:, k % 2, 0:n], ACT.Relu,
                                       bias=bcol[:, (0 if first else 2) + layer:(0 if first else 2) + layer + 1]).then_inc(
                                           mm_evac, 1)
                if first:
                    for g in GROUPS:
                        copy_transposed(h1R[:, g[0]:g[-1] + 1].rearrange("p b c -> p (b c)"), P * len(g), P)
            std()
            copy_all(T1, C)
            std()

        @block.vector
        def _(dve):
            ring = {"mm": 0, "q": 0, "stage": 0}
            tt, ts, stt, red_ = dve.tensor_tensor, dve.tensor_scalar, dve.scalar_tensor_tensor, dve.tensor_reduce
            d = dve.drain

            def mm_take(fn):
                k = ring["mm"]
                dve.wait_ge(mm_full, k + 1)
                fn(mm[:, k % 2]).then_inc(mm_evac, 1)
                ring["mm"] = k + 1

            def ask(ins):
                ins.then_inc(act_q, 1)
                ring["q"] += 1
                dve.wait_ge(act_r, ring["q"])

            dve.memset(xN[96:P], 0.0)
            dve.memset(nv[96:P], 0.0)
            dve.memset(T1[C:C + 1], 1.0)
            dve.memset(T2[C:C + 1], 1.0)
            dve.memset(Wabm[C:C + 1, 0:2 * C], 0.0)
            dve.memset(zerosb[:], 0.0)
            dve.memset(totF[:, 1:2], float(E))
            dve.memset(epsb[:], EPS)
            dve.memset(accT[:], 0.0)
            d().then_inc(pads_clear, 1)
            dve.wait_ge(consts, NCONST)
            dve.tensor_copy(nodeF[:], nodeI[:])
            dve.tensor_copy(slotF[:], slotI[:])
            dve.tensor_copy(relF[:], relI[:])
            dve.tensor_copy(gF[:], gI[:])
            dve.wait_ge(edges_in, 64)
            dve.tensor_copy(tmin_small, dst_sb[:, 0:EW:ROW]).then_inc(tmin_cast, 1)
            dve.tensor_copy(rec_sb[:, :, 0], src_sb)
            dve.tensor_copy(rec_sb[:, :, 5], typ_sb)
            dve.tensor_copy(rec_sb[:, :, 1:5], attr_sb.bitcast(I32)).then_inc(rec_built, 1)
            dve.wait_ge(tmin_in, 16)
            d()
            for b in range(NB):
                ts(junk_dve[:, 0:NROW], tminB, nodeF[:, b:b + 1], None, op0=ALU.is_lt, op1=ALU.add,
                   accum_out=S(K_)[:, b:b + 1])
                d()
            ts(S(K_), S(K_), -1.0, 0.0, op0=ALU.add, op1=ALU.max)
            d()
            dve.tensor_copy(SI(0), S(K_)).then_inc(row_index, 1)
            dve.wait_ge(w_in, 16 * NW)
            dve.tensor_copy(WeB, bc(WeT[:], P))
            tt(Wagg[:, :, 0], Wpost[:, 0], Wpost[:, 2], ALU.add)
            dve.tensor_copy(Wagg[:, :, 1], Wpost[:, 1])
            d().then_inc(we_spread, 1)
            for pair in PAIRS:
                s = ring["stage"] % NSTAGE
                if ring["stage"] >= NSTAGE:
                    dve.wait_ge(stage_out[s], 32 * (ring["stage"] // NSTAGE))
                n = len(pair)
                mm_take(lambda bank: dve.tensor_copy(stage[:, s, 0:n].rearrange("p a c -> p (a c)"),
                                                     bank[:, 0:4 * C * n]))
                d().then_inc(stage_ready, 1)
                ring["stage"] += 1
            dve.wait_ge(mm_full, ring["mm"] + 1)
            dve.tensor_copy(edgeB[:].rearrange("p a c -> p (a c)"), mm[:, ring["mm"] % 2, 0:4 * C])
            ts(lsum[:, 1:2], mm[:, ring["mm"] % 2, 4 * C:4 * C + 1], 1.0 / N, None, op0=ALU.mult).then_inc(mm_evac, 1)
            ring["mm"] += 1
            dve.wait_ge(row_in, 16 * NB)
            cmp_row = junk_dve[:, 0:NB * ROW].rearrange("p (b n) -> p b n", n=ROW)
            tt(cmp_row, dstrow, bc(nodeF[:], ROW), ALU.is_lt)
            d()
            red_(S(CNT_), cmp_row, X_AXIS, ALU.add)
            d()
            stt(out=S(START_), in0=S(K_), scalar=float(ROW), in1=S(CNT_), op0=ALU.mult, op1=ALU.add).then_inc(start_done, 1)
            dve.wait_ge(end_in, 16)
            tt(S(DEG_), S(END_), S(START_), ALU.subtract)
            d()
            ts(S(KEYN_), S(DEG_), 4000.0, KEY, op0=ALU.min, op1=ALU.mult)
            d()
            tt(S(KEYN_), S(KEYN_), nodeF[:], ALU.add)
            d()
            ts(S(NKEY_), S(KEYN_), -1.0, None, op0=ALU.mult)
            dve.tensor_copy(info[:, :, 0], nodeI[:])
            dve.tensor_copy(info[:, :, 1], S(START_))
            dve.tensor_copy(info[:, :, 2], S(END_))
            d().then_inc(key_done, 1)
            dve.wait_ge(key_in, 16)
            for b in range(RANK_DVE):
                ts(junk_dve, keyB, S(KEYN_)[:, b:b + 1], None, op0=ALU.is_gt, op1=ALU.add,
                   accum_out=S(RANK_)[:, b:b + 1])
                d()
            dve.wait_ge(rank_act, 1)
            ts(S(RANK_)[:, RANK_DVE:], S(RANK_)[:, RANK_DVE:], float(NP - 1), 0.5, op0=ALU.add, op1=ALU.mult)
            d()
            dve.tensor_copy(SI(1), S(RANK_))
            d()
            ts(SI(2), SI(1), 7, None, op0=ALU.logical_shift_right)
            ts(SI(4), SI(1), 127, None, op0=ALU.bitwise_and)
            d()
            stt(out=SI(3), in0=SI(4), scalar=float(NB), in1=SI(2), op0=ALU.mult, op1=ALU.add).then_inc(rank_done, 1)
            dve.wait_ge(info_in, 16)
            dve.tensor_copy(S(PTR_), infoR[:, :, 1])
            dve.tensor_copy(S(END_), infoR[:, :, 2])
            d()
            tt(S(DEGR_), S(END_), S(PTR_), ALU.subtract)
            d()
            dve.tensor_copy(S(REM_), S(DEGR_)).then_inc(deg_done, 1)
            dve.wait_ge(degT_full, 1)
            red_(S(MAXD_)[0:NB, 0:1], l3[0:NB, 0, 0:P], X_AXIS, ALU.max)
            d()
            ts(SI(5)[0:NB, 0:1], S(MAXD_)[0:NB, 0:1], float(SLOTS - 1), None, op0=ALU.add)
            d()
            ts(SI(5)[0:NB, 1:2], SI(5)[0:NB, 0:1], 4, None, op0=ALU.logical_shift_right)
            d()
            dve.tensor_copy(S(NIT_)[0:NB, 0:1], SI(5)[0:NB, 1:2])
            d()
            dve.tensor_copy(bcast[:, 0], S(NIT_)[0:NB, 0:1].to_broadcast([NB, P]))
            dve.tensor_copy(bcast[:, 1], S(MAXD_)[0:NB, 0:1].to_broadcast([NB, P]))
            d().then_inc(nit_done, 1)
            dve.wait_ge(cum_full, 1)
            dve.tensor_copy(cum[:].rearrange("p a b -> p (a b)"), l3[:, 1, 0:3 * NB])
            d()
            stt(out=fval[:, 0], in0=cum[:, 1], scalar=float(SLOTS), in1=cum[:, 2], op0=ALU.mult, op1=ALU.add)
            tt(ind3, bc(gF[:], NB), bm(cum[:, 0], SP_), ALU.is_ge)
            ts(totI[:, 1:2], cum[:, 0, NB - 1:NB], 1.0, None, op0=ALU.add)
            d()
            tt(fval[:, 1, 0:NB - 1], fval[:, 0, 1:NB], fval[:, 0, 0:NB - 1], ALU.subtract)
            red_(tabF[:, 0], ind3, X_AXIS, ALU.add)
            ts(totI[:, 0:1], totI[:, 1:2], 1, None, op0=ALU.logical_shift_right)
            d()
            tt(indw[:, :, 0:NB - 1], ind3[:, :, 0:NB - 1], bm(fval[:, 1, 0:NB - 1], SP_), ALU.mult)
            ts(totI[:, 0:1], totI[:, 0:1], float(HI + 1), None, op0=ALU.max)
            d()
            red_(tabF[:, 1], indw[:, :, 0:NB - 1], X_AXIS, ALU.add)
            d()
            ts(tabF[:, 1], tabF[:, 1], fval[:, 0, 0:1], None, op0=ALU.add)
            d()
            stt(out=tabF[:, 1], in0=gF[:], scalar=-float(SLOTS), in1=tabF[:, 1], op0=ALU.mult, op1=ALU.add)
            ts(tabI[:, 0], tabF[:, 0], float(NB - 1), None, op0=ALU.min)
            d()
            ts(tabI[:, 1], tabF[:, 1], 0.0, float(SLOTS), op0=ALU.max, op1=ALU.min)
            d().then_inc(steps_done, 1)

            dve.wait_ge(hist_in, 32)
            ts(hsrc_q, hsrc, 5243.0, None, op0=ALU.mult)
            d()
            ts(hsrc_q, hsrc_q, 17, None, op0=ALU.logical_shift_right)
            d()
            dve.tensor_copy(part, hsrc_q)
            d()
            stt(out=code, in0=part, scalar=-float(NB), in1=hsrc, op0=ALU.mult, op1=ALU.add)
            d()
            stt(out=code, in0=code, scalar=float(R), in1=htyp, op0=ALU.mult, op1=ALU.add)
            d().then_inc(hist_oh, 1)

            landed = [dve.alloc_register(f"rows_expected{u}") for u in range(2)]

            def wait_rows(L, i, u):
                left = dve.value_load(stepL[0:1, bass.ds(2 * i + u, 1)], min_val=0, max_val=SLOTS)
                fours = dve.snap(((left + 3) >> 2) + (left < 1))
                dve.reg_add(landed[u], landed[u], dve.snap(fours * 64))
                dve.wait_ge(L.rows_landed[u], dve.snap(landed[u]))

            def begin_loop(L):
                for u in range(2):
                    dve.reg_mov(landed[u], 0)
                for u in range(2):
                    blk = dve.value_load(stepB[0:1, u:u + 1], min_val=0, max_val=NB - 1)
                    next_window(L, u, blk)
                d().then_inc(L.free, 2)

            def next_window(L, u, blk):
                p_ = small[:, PTR_, bass.ds(blk, 1)]
                ts(win[u][:], p_, float(E), None, op0=ALU.min)
                d()
                ts(p_, p_, float(SLOTS), None, op0=ALU.add)
                d().then_inc(L.win_ready, 1)

            def step_head(L, i, u):
                blk = dve.value_load(stepB[0:1, bass.ds(2 * i + u, 1)], min_val=0, max_val=NB - 1)
                ahead = dve.value_load(stepB[0:1, bass.ds(2 * i + u + 2, 1)], min_val=0, max_val=NB - 1)
                dve.wait_ge(L.rec_landed[u], 16 * (i + 1))
                next_window(L, u, ahead)
                r_ = small[:, REM_, bass.ds(blk, 1)]
                ts(mask[:], slotF[:], r_, None, op0=ALU.is_lt)
                d()
                ts(r_, r_, -float(SLOTS), None, op0=ALU.add)
                return blk

            def reset_loop():
                dve.tensor_copy(S(PTR_), infoR[:, :, 1])
                dve.tensor_copy(S(REM_), S(DEGR_))

            flat = lambda ap: ap.rearrange("p s c -> p (s c)")

            dve.wait_ge(steps_in, 32)
            dve.wait_ge(own_in, 16 * NB)
            dve.memset(accV, 0.0)
            dve.wait_ge(rec_out, 32)
            for u in range(2):
                dve.memset(G[u], 0.0)
            begin_loop(LOOP0)
            dve.wait_ge(steps_in, 32)

            def step0(i, u, with_hist):
                blk = step_head(LOOP0, i, u)
                tt(eqt[:], bm(rec[u][:, :, 5], R), bc(relF[:], SLOTS), ALU.is_equal)
                d()
                tt(eqt[:], eqt[:], bm(mask[:], R), ALU.mult)
                d()
                red_(redt[:], eqt[:], X_AXIS, ALU.add)
                d()
                t_ = accT[:, bass.ds(blk, 1), :]
                tt(t_, t_, redt[:].unsqueeze(1), ALU.add)
                wait_rows(LOOP0, i, u)
                q_ = ownR[:, bass.ds(blk, 1), 0:C].to_broadcast([P, SLOTS, C])
                tt(prod[:, :, 0:C], G[u][:, :, 0:C], q_, ALU.mult)
                d()
                red_(score[u][:], prod[:, :, 0:C].rearrange("p s (h c) -> p s h c", h=HEADS), X_AXIS, ALU.add)
                d()
                ts(score[u][:], score[u][:], -40.0, 40.0, op0=ALU.max, op1=ALU.min).then_inc(score_ready, 1)
                if with_hist:
                    for q in range(4):
                        g4 = 8 * i + 4 * u + q
                        dve.wait_ge(hist_mm, g4 + 1)
                        for j in range(4):
                            t = bass.ds(16 * (2 * i + u) + 4 * q + j, 1)
                            ts(oh_lo[:, q % 2, j], laneI[0:ROW], part[:, t], None, op0=ALU.is_equal)
                            last = ts(oh_hi[:, q % 2, j], codeI[0:ROW], code[:, t], None, op0=ALU.is_equal)
                        last.then_inc(hist_oh, 1)
                dve.wait_ge(exp_ready, 2 * i + u + 1)
                e_ = weighted[:, :, C:C + HEADS]
                tt(e_, expd[u][:], bc(mask[:], HEADS), ALU.mult)
                d()
                tt(weighted[:, :, 0:C].rearrange("p s (h c) -> p s h c", h=HEADS),
                   G[u][:, :, C:].rearrange("p s (h c) -> p s h c", h=HEADS),
                   e_.unsqueeze(3).to_broadcast([P, SLOTS, HEADS, HD]), ALU.mult)
                d()
                red_(red[:, 0:C + HEADS], weighted.rearrange("p s c -> p c s"), X_AXIS, ALU.add)
                d()
                v_ = accV[:, bass.ds(blk, 1), :]
                tt(v_, v_, red[:, 0:C + HEADS].unsqueeze(1), ALU.add)
                d().then_inc(LOOP0.free, 1)

            pairs = dve.value_load(totI[0:1, 0:1], min_val=HI + 1, max_val=STEPS // 2 - 1)
            d().then_inc(hist_mm, 2)
            with dve.Fori(0, HI) as i:
                for u in range(2):
                    step0(i, u, True)
            with dve.Fori(HI, pairs) as i:
                for u in range(2):
                    step0(i, u, False)
            dve.wait_ge(LOOP0.rec_landed[0], 16 * (pairs + 1))
            dve.wait_ge(hist_mm, 8 * HI + 2)
            dve.tensor_copy(histo[:], hist[:, 0:NB * R]).then_inc(hist_done, 1)

            flat3 = lambda ap: ap.rearrange("p b c -> p (b c)")
            scr = prod.rearrange("p s c -> p (s c)")[:, 0:NB * C].rearrange("p (b c) -> p b c", c=C)

            def layernorm(dst, src, dfin=True):
                red_(S(MU_), src, X_AXIS, ALU.add)
                d()
                ts(S(MU_), S(MU_), 1.0 / C, None, op0=ALU.mult)
                d()
                tt(src, src, bc(S(MU_), C), ALU.subtract)
                d()
                tt(scr, src, src, ALU.mult)
                d()
                red_(S(VAR_), scr, X_AXIS, ALU.add)
                ask(d())
                dve.reciprocal(S(STD_), S(STD_))
                d()
                tt(dst, src, bc(S(STD_), C), ALU.mult)
                d()

            zp = small[:, ZP_:ZP_ + 4, :].rearrange("p a b -> p (a b)").rearrange("p (b h) -> p b h", h=HEADS)
            ts(zp, accV[:, :, C:], 1.0, None, op0=ALU.add)
            d()
            dve.reciprocal(zp, zp)
            d()
            tt(sR.rearrange("p b (h c) -> p b h c", h=HEADS), accV[:, :, 0:C].rearrange("p b (h c) -> p b h c", h=HEADS),
               zp.unsqueeze(3).to_broadcast([P, NB, HEADS, HD]), ALU.mult).then_inc(wv_done, 1)
            own = lambda k: ownR[:, :, k * C:(k + 1) * C]
            for g in GROUPS:
                n = len(g)
                mm_take(lambda bank: tt(own(1)[:, g[0]:g[-1] + 1], own(1)[:, g[0]:g[-1] + 1],
                                        bank[:, 0:C * n].rearrange("p (b c) -> p b c", c=C), ALU.add))
            d()
            dve.tensor_copy(x1R[:], own(1))
            d()
            layernorm(x1R[:], x1R[:])
            tt(x1R[:], x1R[:], bm(rowsB[:, 0], NB), ALU.mult)
            d()
            tt(x1R[:], x1R[:], bm(rowsB[:, 1], NB), ALU.add)
            d()
            tt(x1R[:], x1R[:], own(1), ALU.add)
            d()
            tt(x1R[:], x1R[:], own(2), ALU.add)
            d()
            layernorm(x1R[:], x1R[:])
            d().then_inc(x1_done, 1)
            reset_loop()
            for g in GROUPS:
                n = P * len(g)
                mm_take(lambda bank: dve.tensor_copy(T1[0:C, g[0] * P:g[0] * P + n], bank[0:C, 0:n]))
            dve.memset(accMx, -BIG)
            dve.memset(accMn, BIG)
            dve.memset(accS1, 0.0)
            dve.memset(accS2, 0.0)
            for pair in PAIRS:
                k = ring["mm"]
                dve.wait_ge(mm_full, k + 1)
                s = slice(pair[0], pair[-1] + 1)
                v = mm[:, k % 2].rearrange("p (b c) -> p b c", c=4 * C)[:, 0:len(pair)]
                tt(aR[:, s], v[:, :, 0:C], bm(edgeB[:, 0], len(pair)), ALU.add)
                dve.tensor_copy(sR[:, s], v[:, :, C:2 * C])
                dve.tensor_copy(mpR[:, s], v[:, :, 2 * C:3 * C]).then_inc(mm_evac, 1)
                ring["mm"] += 1
            d().then_inc(ab_done, 1)
            begin_loop(LOOP1)
            tmp = prod[:, :, 0:C]
            tmp2 = prod[:, :, C:]
            tmp3 = weighted[:, :, 0:C]
            pairs = dve.value_load(totI[0:1, 0:1], min_val=HI + 1, max_val=STEPS // 2 - 1)
            with dve.Fori(0, pairs) as i:
                for u in range(2):
                    blk = step_head(LOOP1, i, u)
                    ea = rec[u][:].bitcast(F32)
                    tt(ewm[:], ea[:, :, 4], mask[:], ALU.mult)
                    ts(neg[:], mask[:], 1.0, BIG, op0=ALU.subtract, op1=ALU.mult)
                    ts(pos[:], mask[:], 1.0, -BIG, op0=ALU.subtract, op1=ALU.mult)
                    d()
                    tt(eam[:], ea[:, :, 1:4].rearrange("p s k -> p k s"), bm(ewm[:], 3), ALU.mult)
                    d()
                    tt(tmp2, bc(eam[:, 0], C), bm(edgeB[:, 1], SLOTS), ALU.mult)
                    tt(tmp3, bc(eam[:, 1], C), bm(edgeB[:, 2], SLOTS), ALU.mult)
                    d()
                    tt(tmp2, tmp2, tmp3, ALU.add)
                    d()
                    tt(tmp3, bc(eam[:, 2], C), bm(edgeB[:, 3], SLOTS), ALU.mult)
                    d()
                    tt(tmp2, tmp2, tmp3, ALU.add)
                    wait_rows(LOOP1, i, u)
                    tt(tmp, G1[u], aR[:, bass.ds(blk, 1), :].to_broadcast([P, SLOTS, C]), ALU.add)
                    d()
                    tt(tmp, tmp, bc(ewm[:], C), ALU.mult)
                    d()
                    tt(tmp, tmp, tmp2, ALU.add)
                    d()
                    perc = lambda ap: ap.rearrange("p s c -> p c s")
                    red_(red[:, 0:C], perc(tmp), X_AXIS, ALU.add)
                    tt(tmp2, tmp, tmp, ALU.mult)
                    tt(tmp3, tmp, bc(neg[:], C), ALU.add)
                    d()
                    red_(red[:, C:2 * C], perc(tmp2), X_AXIS, ALU.add)
                    v_ = accS1[:, bass.ds(blk, 1), :]
                    tt(v_, v_, red[:, 0:C].unsqueeze(1), ALU.add)
                    d()
                    red_(red[:, 0:C], perc(tmp3), X_AXIS, ALU.max)
                    v_ = accS2[:, bass.ds(blk, 1), :]
                    tt(v_, v_, red[:, C:2 * C].unsqueeze(1), ALU.add)
                    tt(tmp2, tmp, bc(pos[:], C), ALU.add)
                    d()
                    red_(red[:, C:2 * C], perc(tmp2), X_AXIS, ALU.min)
                    v_ = accMx[:, bass.ds(blk, 1), :]
                    tt(v_, v_, red[:, 0:C].unsqueeze(1), ALU.max)
                    d()
                    v_ = accMn[:, bass.ds(blk, 1), :]
                    tt(v_, v_, red[:, C:2 * C].unsqueeze(1), ALU.min)
                    d().then_inc(LOOP1.free, 1)
            dve.wait_ge(LOOP1.rec_landed[0], 16 * (pairs + 1))
            ts(S(HAS_), S(DEGR_), 0.0, None, op0=ALU.is_gt)
            ts(S(LOGD_), S(DEGR_), 1.0, None, op0=ALU.max)
            d()
            dve.reciprocal(S(SAFE_), S(LOGD_))
            dve.reciprocal(lsum[:, 0:1], lsum[:, 1:2])
            ask(d())
            ts(S(RATIO_), S(LOGD_), lsum[:, 0:1], None, op0=ALU.mult)
            tt(accS1, accS1, bc(S(SAFE_), C), ALU.mult)
            tt(accS2, accS2, bc(S(SAFE_), C), ALU.mult)
            d()
            tt(scr, accS1, accS1, ALU.mult)
            d()
            tt(accS2, accS2, scr, ALU.subtract)
            d()
            ts(accS2, accS2, 0.0, None, op0=ALU.max)
            ask(d())
            for dst, src in ((0, accS1), (1, accMn), (2, accMx)):
                tt(agg[:, :, dst], src, bm(rowsB[:, 2], NB), ALU.add)
            d()
            for dst in range(3):
                tt(agg[:, :, dst], agg[:, :, dst], bc(S(HAS_), C), ALU.mult)
            d().then_inc(agg_done, 1)
            for g in GROUPS:
                k = ring["mm"]
                dve.wait_ge(mm_full, k + 1)
                s = slice(g[0], g[-1] + 1)
                v = mm[:, k % 2].rearrange("p (b c) -> p b c", c=2 * C)[:, 0:len(g)]
                tt(mpR[:, s], mpR[:, s], v[:, :, 0:C], ALU.add)
                tt(sR[:, s], v[:, :, C:2 * C], bc(S(RATIO_)[:, s], C), ALU.mult).then_inc(mm_evac, 1)
                ring["mm"] += 1
            d()
            tt(sR, sR, mpR, ALU.add)
            d().then_inc(out_done, 1)
            for pair in PAIRS:
                n = len(pair)
                mm_take(lambda bank: dve.tensor_copy(flat3(gates[:, pair[0]:pair[-1] + 1]), bank[:, 0:4 * C * n]))
            ask(d())
            gate = lambda k: gates[:, :, k * C:(k + 1) * C]
            tt(sR, gate(0), gate(3), ALU.mult)
            d()
            tt(sR, sR, gate(2), ALU.add)
            ask(d())
            tt(gate(0), x1R[:], sR, ALU.subtract)
            d()
            tt(gate(0), gate(0), gate(1), ALU.mult)
            d()
            tt(gate(0), gate(0), sR, ALU.add)
            d()
            tt(sR, gate(0), x1R[:], ALU.add)
            reset_loop()
            d()
            dve.tensor_copy(x1R[:], sR)
            d()
            layernorm(xN[:], x1R[:])
            d().then_inc(x2_done, 1)

            def sum_loop(L, buf, acc, w):
                for u in range(2):
                    dve.memset(buf[u], 0.0)
                dve.memset(acc, 0.0)
                begin_loop(L)
                pairs = dve.value_load(totI[0:1, 0:1], min_val=HI + 1, max_val=STEPS // 2 - 1)
                with dve.Fori(0, pairs) as i:
                    for u in range(2):
                        blk = step_head(L, i, u)
                        wait_rows(L, i, u)
                        tt(prod[:, :, 0:w], buf[u], bc(mask[:], w), ALU.mult)
                        d()
                        red_(red[:, 0:w], prod[:, :, 0:w].rearrange("p s c -> p c s"), X_AXIS, ALU.add)
                        d()
                        v_ = acc[:, bass.ds(blk, 1), :]
                        tt(v_, v_, red[:, 0:w].unsqueeze(1), ALU.add)
                        d().then_inc(L.free, 1)
                dve.wait_ge(L.rec_landed[0], 16 * (pairs + 1))

            sum_loop(LOOP2, G1, acc2, C)
            reset_loop()
            tt(sR, xN[:], acc2, ALU.add)
            d().then_inc(z_done, 1)
            ring["mm"] += 2 * len(GROUPS)
            dve.wait_ge(tp_evac, TP_H1)
            sum_loop(LOOP3, G, acc3, 2 * C)
            tt(h1R, h1R, acc3, ALU.add)
            d().then_inc(z_done, 1)
            ring["mm"] += 2 * len(GROUPS)
            for g in GROUPS:
                n = len(g)
                mm_take(lambda bank: tt(sR[:, g[0]:g[-1] + 1], xN[:, g[0]:g[-1] + 1],
                                        bank[:, 0:C * n].rearrange("p (b c) -> p b c", c=C), ALU.add))
            d()
            tt(sR, sR, bm(rowsB[:, 3], NB), ALU.add)
            d()
            layernorm(x1R[:], sR)
            dve.memset(T1[C:C + 1], 1.0)
            d().then_inc(x3_done, 1)
            dve.wait_ge(cnt_in, 16 * NB)
            dve.tensor_copy(cntR[:, :, 1], accT[:])
            d()
            cnts = cntR.rearrange("p b a r -> p b (a r)")
            red_(S(CNTT_), cnts, X_AXIS, ALU.add)
            d()
            ts(S(CNTT_), S(CNTT_), 1.0, None, op0=ALU.max)
            d()
            dve.reciprocal(S(CNTT_), S(CNTT_))
            for b in range(NB):
                dve.wait_ge(l3_full, b + 1)
                for j in range(3):
                    tt(prodL3[:, 6 * C * j:6 * C * (j + 1)].rearrange("p (r c) -> p r c", c=C),
                       l3[:, j, 0:6 * C].rearrange("p (r c) -> p r c", c=C),
                       bc(cnts[:, b, 6 * j:6 * j + 6], C), ALU.mult)
                d().then_inc(l3_used, 1)
                red_(sumL3[:, b], prodL3.rearrange("p (r c) -> p c r", c=C), X_AXIS, ALU.add)
                d()
            tt(sumL3, sumL3, bc(S(CNTT_), C), ALU.mult)
            d()
            tt(sumL3, sumL3, x1R[:], ALU.add)
            d()
            layernorm(sumL3, sumL3)
            d().then_inc(final_done, 1)


INPUTS = ["x", "src", "dst", "edge_attr_4", "edge_type_9", "node_vec",
          *("L0_gnn_" + k for k in ("Wq", "bq", "Wk", "bk", "Wv", "bv", "Wo", "bo", "Wf", "bf", "gamma", "beta")),
          *("L1_gnn_" + k for k in ("W", "We", "be", "Wpre", "bpre", "Wpost", "bpost", "Wih", "bih", "Whh", "bhh")),
          *("L2_gnn_" + k for k in ("W1a", "b1a", "W1b", "b1b", "W2a", "b2a", "W2b", "b2b", "Wlin", "blin")),
          "L3_gnn_weights", "L3_gnn_biases"]


def kernel(**inputs):
    import numpy as np
    import concourse.bacc as bacc
    from concourse import mybir as mb
    from concourse.bass_utils import run_bass_kernel_spmd

    nc = bacc.Bacc("TRN2", target_bir_lowering=False, num_devices=1)
    arrays, args = {}, {}
    for name in INPUTS:
        v = np.ascontiguousarray(inputs[name])
        arrays["in_" + name] = v
        args[name] = nc.dram_tensor("in_" + name, v.shape, mb.dt.from_np(v.dtype), kind="ExternalInput").ap()
    out = nc.dram_tensor("out_0", (N, C), mb.dt.float32, kind="ExternalOutput").ap()
    build(nc, args, out)
    r = run_bass_kernel_spmd(nc, [arrays], core_ids=[0])
    return r.results[0]["out_0"]
```

```python
from contextlib import ExitStack, nullcontext

import concourse.bass as bass
from concourse import mybir

F32 = mybir.dt.float32
BF16 = mybir.dt.bfloat16
I32 = mybir.dt.int32
I16 = mybir.dt.int16
U8 = mybir.dt.uint8
ALU = mybir.AluOpType
ACT = mybir.ActivationFunctionType
X_AXIS = mybir.AxisListType.X

P = 128
N, E, C, R = 3125, 100000, 64, 9
NB = 25
NP = NB * P
NV = N // NB
HEADS, HD = 4, 16
SLOTS = 16
SUB = 4
REC = 6
EP, EW = 80, 1250
ROW = 125
NROW = E // ROW
NSTAGE = 2
STEPS = 6400
SP_ = STEPS // P
HT, HI = 16, 25
GT = 9
GW = GT * P
KEY = 4096.0
BIG = 1.0e30
EPS = 1e-5
KV = 2 * C + 2
GROUPS = [list(range(g, min(g + 4, NB))) for g in range(0, NB, 4)]
PAIRS = [list(range(g, min(g + 2, NB))) for g in range(0, NB, 2)]


def build(nc, a, out):
    dram = lambda name, shape, dt=F32: nc.dram_tensor(name, shape, dt, kind="Internal").ap()
    rec_tab = dram("rec_tab", [E + SLOTS, REC], I32)
    tmin_tab = dram("tmin_tab", [NROW])
    start_tab = dram("start_tab", [NP + 1])
    key_tab = dram("key_tab", [NP])
    info_tab = dram("info_tab", [NP, 3], I32)
    step_tab = dram("step_tab", [STEPS], I16)
    kv_tab = dram("kv_tab", [NP, KV])
    at_tab = dram("at_tab", [NB, P, NP], BF16)
    own_tab = dram("own_tab", [NP, 3 * C])
    b_tab = dram("b_tab", [NP, C])
    x2_tab = dram("x2_tab", [NP, C])
    h1_tab = dram("h1_tab", [NP, 2 * C])
    cnt_tab = dram("cnt_tab", [NP, R])

    with ExitStack() as ctx:
        sb = lambda name, shape, dt=F32: ctx.enter_context(nc.sbuf_tensor(name, shape, dt))
        sem = lambda name: ctx.enter_context(nc.semaphore(name))

        arena = sb("arena", [P, 26600])

        def at(off, parts, *shape, dt=F32):
            n = 1
            for s in shape:
                n *= s
            v = arena[0:parts, off:off + n]
            if dt != F32:
                v = v.bitcast(dt)
            if len(shape) == 2:
                v = v.rearrange("p (a b) -> p a b", b=shape[1])
            if len(shape) == 3:
                v = v.rearrange("p (a b c) -> p a b c", b=shape[1], c=shape[2])
            return v

        rec_sb = at(0, EP, EW, REC, dt=I32)
        attr_sb = at(7500, EP, EW, 4)
        dst_sb = at(12500, EP, EW, dt=I32)
        src_sb = at(13750, EP, EW, dt=I32)
        typ_sb = at(15000, EP, EW, dt=I32)
        keyB = at(16250, P, NP)
        dstrow = at(19450, P, NB, ROW, dt=I32)
        junk_dve = at(22575, P, NP)
        tminB = at(25775, P, NROW)
        junk_act = at(12500, P, NP)
        ind3 = at(16250, P, SP_, NB)
        indw = at(17500, P, SP_, NB)
        G = [at(0, P, SLOTS, KV), at(2080, P, SLOTS, KV)]
        G1 = [at(0, P, SLOTS, C), at(2080, P, SLOTS, C)]
        G3 = [at(0, P, SLOTS, 2 * C), at(2080, P, SLOTS, 2 * C)]
        prod = at(4160, P, SLOTS, 2 * C)
        weighted = [at(6208, P, SLOTS, C + HEADS), at(21754, P, SLOTS, C + HEADS)]
        ownR = at(7296, P, NB, 3 * C)
        accV = at(12100, P, NB, C + HEADS)
        onehotA = at(19450, P, 4 * GW // 2, dt=BF16).rearrange("p (s c) -> p s c", s=4)
        onehot = at(13800, P, 4 * GW, dt=BF16).rearrange("p (r s c) -> p r s c", r=2, s=4)
        colI = at(18408, P, GW // 2, dt=I16)
        atS = at(23450, P, NP // 2, dt=BF16)
        packed = at(25050, P, GW, dt=I32)
        hsrc = at(19450, ROW, NROW, dt=I32)
        accMx = at(14100, P, NB, C)
        accMn = at(15700, P, NB, C)
        accS = at(17300, P, NB, 2 * C)
        accS1, accS2 = accS[:, :, 0:C], accS[:, :, C:]
        hh = [at(4160 + 4096 * u, P, SLOTS, 2 * C) for u in range(2)]
        hmax = [at(6208 + 4096 * u, P, SLOTS, C) for u in range(2)]
        hmin = [at(7232 + 4096 * u, P, SLOTS, C) for u in range(2)]
        aR = at(20500, P, NB, C)
        mpR = at(22100, P, NB, C)
        sR = at(23700, P, NB, C)
        agg = at(7296, P, NB, 4, C)
        aggT = [at(14100, P, NP), at(17300, P, NP)]
        gates = at(0, P, NB, 4 * C)
        atL = [at(NP // 2 * k, P, NP // 2, dt=BF16) for k in range(5)]
        h1R = at(8000, P, NB, 2 * C)
        acc3 = at(11200, P, NB, 2 * C)
        acc2 = at(11200, P, NB, C)
        hT = at(14400, P, NP)
        parts2 = at(17600, P, NB * 3 * C // 2, dt=BF16).rearrange("p (b k c) -> p b k c", b=NB, k=3)
        parts3 = at(17600, P, NB * 3 * C, dt=BF16).rearrange("p (b k c) -> p b k c", b=NB, k=3)
        cntR = at(22400, P, NB, 2, R)
        prodL3 = at(0, P, 2 * R * C)
        sumL3 = at(23700, P, NB, C)

        T1 = sb("T1", [P, NP])
        T2 = sb("T2", [P, NP])
        xN = sb("xN", [P, NB, C])
        x1R = sb("x1R", [P, NB, C])
        stepW = sb("step_word", [1, STEPS], I16)
        stage = T2[:, 0:NSTAGE * 8 * C].rearrange("p (s b c) -> p s b c", s=NSTAGE, b=2)
        accT = sb("accT", [P, NB, R])
        histo = sb("histo", [P, NB * R])
        rec = [sb(f"rec{u}", [P, SLOTS, REC], I32) for u in range(2)]
        win = [sb(f"win{u}", [P, 1], I32) for u in range(2)]
        digit = [sb(f"digit{u}", [P, SLOTS])[:] for u in range(2)]
        negdigit = [sb(f"negdigit{u}", [P, 4])[:] for u in range(2)]
        negcode = [sb(f"negcode{u}", [P, 4])[:] for u in range(2)]
        codes = sb("codes", [P, NB, 2])
        identB = sb("identB", [P, P], BF16)
        masks = [sb(f"mask{u}", [P, SLOTS])[:] for u in range(2)]
        neg = [sb(f"neg{u}", [P, SLOTS])[:] for u in range(2)]
        pos = [sb(f"pos{u}", [P, SLOTS])[:] for u in range(2)]
        ewm = [sb(f"ewm{u}", [P, SLOTS])[:] for u in range(2)]
        eam = [sb(f"eam{u}", [P, SLOTS, 3])[:] for u in range(2)]
        eaT = [sb(f"eaT{u}", [3 * SLOTS, P])[:] for u in range(2)]
        Wslots = sb("Wslots", [3 * SLOTS, SLOTS, C])
        WeR = sb("WeR", [C, SLOTS, 3])
        score = [sb(f"score{u}", [P, SLOTS, HEADS]) for u in range(2)]
        expd = [sb(f"expd{u}", [P, SLOTS, HEADS]) for u in range(2)]
        red = sb("red", [P, 2 * C + 4])
        eqt = sb("eqt", [P, R, SLOTS])
        redt = sb("redt", [P, R])
        oh_lo = sb("oh_lo", [ROW, 2, 4, P], BF16)
        oh_hi = sb("oh_hi", [ROW, 2, 4, NB * R], BF16)
        part = sb("hist_part", [ROW, NROW])[:]
        code = sb("hist_code", [ROW, NROW])[:]
        htyp = at(22650, ROW, NROW, dt=I32)
        zerosb = sb("zerosb", [P, GW // 3], BF16)

        ident = sb("ident", [P, P])
        nodeI = sb("nodeI", [P, NB], I32)
        nodeF = sb("nodeF", [P, NB])
        slotI = sb("slotI", [P, SLOTS], I32)
        slotF = sb("slotF", [P, SLOTS])
        relI = sb("relI", [P, R], I32)
        relF = sb("relF", [P, R])
        laneI = sb("laneI", [P, P], I16)
        codeI = sb("codeI", [P, NB * R], I16)
        gI = sb("gI", [P, SP_], I32)
        gF = sb("gF", [P, SP_])
        triI = sb("triI", [NB, NB])
        triE = sb("triE", [NB, NB])
        zrow = sb("zrow", [1, SLOTS * REC])
        small = sb("small", [P, 24, NB])
        smallI = sb("smallI", [P, 6, NB], I32)
        info = sb("info", [P, NB, 3], I32)
        infoR = sb("infoR", [P, NB, 3], I32)
        bcast = sb("bcast", [NB, 2, P])
        cum = sb("cum", [P, 3, NB])
        fval = sb("fval", [P, 2, NB])
        tabF = sb("tabF", [P, 3, SP_])
        tabI = sb("tabI", [P, SP_], I16)
        totI = sb("totI", [P, 3], I32)
        totF = sb("totF", [P, 2])
        nv = sb("nv", [P, NB])
        lsum = sb("lsum", [P, 2])
        ones = sb("ones", [P, P])
        epsb = sb("epsb", [P, 1])

        Wkvqf = sb("Wkvqf", [C + 1, 4 * C])
        Wo = sb("Wo", [C + 1, C])
        W1 = sb("W1", [C, C])
        Wabm = sb("Wabm", [C + 1, 3 * C])
        Wedge = sb("Wedge", [C, C])
        WeT = sb("WeT", [C, 4])
        WeB = at(16250, C, 4, P)
        edgeB = sb("edgeB", [P, 4, C])
        Wpost = sb("Wpost", [P, 3, 2, C])
        Wagg = sb("Wagg", [P, 2, 2, C])
        Wih = sb("Wih", [C + 1, 3 * C])
        Whh = sb("Whh", [C + 1, 3 * C])
        W1a = sb("W1a", [C, 2 * C])
        W1b = sb("W1b", [P, 2 * C])
        W2a = sb("W2a", [P, 2 * C])
        W2b = sb("W2b", [P, 2 * C])
        bcol = sb("bcol", [P, 4])
        Wlin = sb("Wlin", [P, C])
        rowsB = sb("rowsB", [P, 4, C])
        Wrel = sb("Wrel", [C + 1, 2 * R, C])

        tp = ctx.enter_context(nc.psum_tensor("tp", [P, 2, 512], F32))
        mm = ctx.enter_context(nc.psum_tensor("mm", [P, 2, 512], F32))
        l3 = ctx.enter_context(nc.psum_tensor("l3", [P, 3, 512], F32))
        hist = ctx.enter_context(nc.psum_tensor("hist", [P, 512], F32))

        consts = sem("consts")
        x_in = sem("x_in")
        edges_in, pads_clear = sem("edges_in"), sem("pads_clear")
        w_in = sem("w_in")
        tmin_cast, tmin_out, tmin_in = sem("tmin_cast"), sem("tmin_out"), sem("tmin_in")
        rec_built, rec_out = sem("rec_built"), sem("rec_out")
        row_index, row_in = sem("row_index"), sem("row_in")
        start_done, start_out, end_in = sem("start_done"), sem("start_out"), sem("end_in")
        key_done, key_out, key_in = sem("key_done"), sem("key_out"), sem("key_in")
        rank_act, rank_done = sem("rank_act"), sem("rank_done")
        info_out, info_in = sem("info_out"), sem("info_in")
        deg_done, degT_full, nit_done, cum_full = sem("deg_done"), sem("degT_full"), sem("nit_done"), sem("cum_full")
        steps_done, steps_out, steps_in = sem("steps_done"), sem("steps_out"), sem("steps_in")
        tp_full, tp_evac = sem("tp_full"), sem("tp_evac")
        mm_full, mm_evac = sem("mm_full"), sem("mm_evac")
        act_q, act_r = sem("act_q"), sem("act_r")
        stage_out = [sem(f"stage_out{k}") for k in range(NSTAGE)]
        stage_ready, own_x_out = sem("stage_ready"), sem("own_x_out")
        we_spread, row_cmp = sem("we_spread"), sem("row_cmp")
        own_in = sem("own_in")
        x1_done, x2_done, wv_done, ab_done, agg_done, out_done = (
            sem(n) for n in ("x1_done", "x2_done", "wv_done", "ab_done", "agg_done", "out_done"))
        b_out, x2_out, h1_done, h1_out = sem("b_out"), sem("x2_out"), sem("h1_done"), sem("h1_out")
        z_done = sem("z_done")
        edge_full = sem("edge_full")
        hist_in, hist_oh, hist_mm, hist_done, hist_out, hist_back = (
            sem(n) for n in ("hist_in", "hist_oh", "hist_mm", "hist_done", "hist_out", "hist_back"))
        cnt_in = sem("cnt_in")
        x3_done, l3_full, l3_used, final_done, final_out = (
            sem(n) for n in ("x3_done", "l3_full", "l3_used", "final_done", "final_out"))
        pool_steps = sem("pool_steps")
        codes_done, codes_out = sem("codes_done"), sem("codes_out")
        col_ready = sem("col_ready")
        oh_ready, oh_summed = sem("oh_ready"), sem("oh_summed")
        ohA_operands, ohA_ready, ohA_summed = sem("ohA_operands"), sem("ohA_ready"), sem("ohA_summed")
        weighted_ready, weighted_sums = sem("weighted_ready"), sem("weighted_sums")
        a_copied, a_bytes = sem("a_copied"), sem("a_bytes")
        at_full, at_ready, at_out = sem("at_full"), sem("at_ready"), sem("at_out")
        at_in = [sem(f"at_in{k}") for k in range(5)]
        parts_ready, conv_full, conv_evac = sem("parts_ready"), sem("conv_full"), sem("conv_evac")
        attrs_ready, attrsT_full, attrsT_ready, edge_terms = (
            sem(n) for n in ("attrs_ready", "attrsT_full", "attrsT_ready", "edge_terms"))
        h_ready, sq_ready, sums_full, hmax_ready, hmin_ready, sums_used = (
            sem(n) for n in ("h_ready", "sq_ready", "sums_full", "hmax_ready", "hmin_ready", "sums_used"))
        w_spread, w_diag = sem("w_spread"), sem("w_diag")
        score_ready, exp_ready = sem("score_ready"), sem("exp_ready")

        class Gather:

            def __init__(self, name):
                self.win_ready = sem(name + "_win_ready")
                self.rec_landed = [sem(f"{name}_rec_landed{u}") for u in range(2)]
                self.rows_landed = [sem(f"{name}_rows_landed{u}") for u in range(2)]
                self.rec_used = sem(name + "_rec_used")
                self.free = sem(name + "_free")

        LOOP0, LOOP1, LOOP2, LOOP3 = (Gather(f"loop{n}") for n in range(4))

        block = ctx.enter_context(nc.Block())
        NCONST = 11
        NW = 42
        RANK_DVE = 12
        TP_H1 = 8 * len(GROUPS)
        MM_MLP = [2 * len(GROUPS) + 1 + len(GROUPS) + 3 * len(PAIRS), 5 * len(GROUPS) + 1 + len(GROUPS) - len(GROUPS) + 3 * len(PAIRS)]
        tmin_small = at(26575, EP, 10)
        hsrc_q = at(20250, ROW, NROW, dt=I32)

        WMAX = 64 * (NB - 1) + 32 + SLOTS
        block_of = lambda word: nc.s_assert_within(word >> 6, 0, NB - 1)
        finished = lambda word: nc.s_assert_within(word >> 6, 1, NB - 1)
        at_banks = [tp[:, 0], tp[:, 1], mm[:, 0], mm[:, 1]]
        conv_banks = [l3[:, 0], l3[:, 1], l3[:, 2], hist[:], mm[:, 1]]
        distance = [T1[:, GW * k:GW * (k + 1)] for k in range(2)]
        wsum = [hist[:, 0:C + HEADS], hist[:, 256:256 + C + HEADS]]
        a_blk = T2[:, 0:3 * GW // 2].bitcast(BF16).rearrange("p (k c) -> p k c", k=3)

        K_, CNT_, START_, END_, DEG_, KEYN_, NKEY_, RANK_, RA_, RB_, DEGR_, PTR_, REM_, MAXD_, NIT_, ZP_, SAFE_, HAS_, RATIO_, MU_, VAR_, STD_, LOGD_, CNTT_ = range(24)
        S = lambda k: small[:, k, :]
        SI = lambda k: smallI[:, k, :]

        def bc(ap2, n):
            return ap2.unsqueeze(2).to_broadcast([ap2.shape[0], ap2.shape[1], n])

        def bm(ap2, n):
            return ap2.unsqueeze(1).to_broadcast([ap2.shape[0], n, ap2.shape[1]])

        @block.sync
        def _(sp):
            dma = sp.dma_start
            row = lambda v: v.rearrange("(a n) -> a n", a=1)
            dma(dst_sb, a["dst"].rearrange("(p n) -> p n", p=EP)).then_inc(edges_in, 16)
            dma(src_sb, a["src"].rearrange("(p n) -> p n", p=EP)).then_inc(edges_in, 16)
            dma(typ_sb, a["edge_type_9"].rearrange("(p n) -> p n", p=EP)).then_inc(edges_in, 16)
            dma(attr_sb, a["edge_attr_4"].rearrange("(p n) c -> p n c", p=EP)).then_inc(edges_in, 16)
            sp.wait_ge(pads_clear, 1)
            dma(xN[0:NV], a["x"].rearrange("(p b) c -> p b c", b=NB)).then_inc(x_in, 16)
            dma(nv[0:NV], a["node_vec"].rearrange("(p b) -> p b", b=NB)).then_inc(x_in, 16)
            sp.wait_ge(tmin_cast, 1)
            dma(tmin_tab.rearrange("(p n) -> p n", p=EP), tmin_small).then_inc(tmin_out, 16)
            sp.wait_ge(tmin_out, 16)
            dma(tminB, row(tmin_tab).to_broadcast([P, NROW])).then_inc(tmin_in, 16)
            sp.wait_ge(rec_built, 1)
            dma(rec_tab[0:E, :].rearrange("(p n) c -> p n c", p=EP), rec_sb).then_inc(rec_out, 16)
            dma(rec_tab[E:, :].rearrange("(a n) c -> a (n c)", a=1), zrow[:].bitcast(I32)).then_inc(rec_out, 16)
            kv_rows = kv_tab.rearrange("(p b) c -> p b c", b=NB)
            own_rows = own_tab.rearrange("(p b) c -> p b c", b=NB)
            dma(own_rows[:, :, 2 * C:], xN[:]).then_inc(own_x_out, 16)
            for k, pair in enumerate(PAIRS):
                s, b = k % NSTAGE, slice(pair[0], pair[-1] + 1)
                sp.wait_ge(stage_ready, k + 1)
                dma(kv_rows[:, b, 0:2 * C], stage[:, s, 0:len(pair), 0:2 * C]).then_inc(stage_out[s], 16)
                dma(own_rows[:, b, 0:2 * C], stage[:, s, 0:len(pair), 2 * C:]).then_inc(stage_out[s], 16)
            sp.wait_ge(start_done, 1)
            dma(start_tab[0:NP].rearrange("(p b) -> p b", b=NB), S(START_)).then_inc(start_out, 16)
            dma(start_tab[NP:].rearrange("(a n) -> a n", a=1), totF[0:1, 1:2]).then_inc(start_out, 16)
            sp.wait_ge(start_out, 32)
            dma(S(END_), start_tab[1:].rearrange("(p b) -> p b", b=NB)).then_inc(end_in, 16)
            sp.wait_ge(key_done, 1)
            dma(key_tab.rearrange("(p b) -> p b", b=NB), S(KEYN_)).then_inc(key_out, 16)
            sp.wait_ge(key_out, 16)
            dma(keyB, row(key_tab).to_broadcast([P, NP])).then_inc(key_in, 16)
            sp.wait_ge(codes_done, 1)
            dma(kv_rows[:, :, 2 * C:], codes[:]).then_inc(codes_out, 16)
            sp.wait_ge(info_out, 16 * NB)
            dma(infoR[:], info_tab.rearrange("(p b) c -> p b c", b=NB)).then_inc(info_in, 16)
            sp.wait_ge(steps_done, 1)
            dma(step_tab.rearrange("(p n) -> p n", p=P), tabI[:]).then_inc(steps_out, 16)
            sp.wait_ge(steps_out, 16)
            dma(stepW[:], row(step_tab)).then_inc(steps_in, 16)
            dma(hsrc, a["src"].rearrange("(p n) -> p n", p=ROW)).then_inc(hist_in, 16)
            dma(htyp, a["edge_type_9"].rearrange("(p n) -> p n", p=ROW)).then_inc(hist_in, 16)
            for b in range(NB):
                sp.wait_ge(at_ready, b + 2)
                dma(at_tab[b], atS).then_inc(at_out, 16)
            sp.wait_ge(hist_done, 1)
            dma(cnt_tab.rearrange("(p b) c -> p b c", b=NB),
                histo[:].rearrange("p (b c) -> p b c", c=R)).then_inc(hist_out, 16)
            sp.wait_ge(at_out, 16 * (NB + 1))
            sp.wait_ge(x2_done, 1)
            big = sp.value_load(totI[0:1, 2:3], min_val=0, max_val=1)
            with sp.If(big < 1):
                for s in range(2 * NB):
                    if s >= 5:
                        sp.wait_ge(conv_full, s - 4)
                    dma(atL[s % 5], at_tab[s % NB]).then_inc(at_in[s % 5], 16)

        @block.gpsimd
        def _(pool):
            pool.iota(nodeI[:], pattern=[[1, NB]], base=0, channel_multiplier=NB).then_inc(consts, 1)
            pool.iota(slotI[:], pattern=[[1, SLOTS]], base=0, channel_multiplier=0).then_inc(consts, 1)
            pool.iota(relI[:], pattern=[[1, R]], base=0, channel_multiplier=0).then_inc(consts, 1)
            pool.iota(gI[:], pattern=[[1, SP_]], base=0, channel_multiplier=SP_).then_inc(consts, 1)
            pool.iota(laneI[:], pattern=[[1, P]], base=0, channel_multiplier=0,
                      allow_small_or_imprecise_dtypes=True).then_inc(consts, 1)
            pool.iota(codeI[:], pattern=[[1, NB * R]], base=0, channel_multiplier=0,
                      allow_small_or_imprecise_dtypes=True).then_inc(consts, 1)
            pool.memset(ident[:], 0.0)
            pool.memset(ones[:], 1.0).then_inc(consts, 1)
            pool.memset(triI[:], 0.0)
            pool.memset(triE[:], 0.0)
            pool.memset(zrow[:], 0.0).then_inc(consts, 1)
            pool.wait_ge(consts, 8)
            pool.drain()
            pool.affine_select(out=ident[:], in_=ident[:], compare_op=ALU.not_equal, fill=1.0, base=0,
                               pattern=[[-1, P]], channel_multiplier=1).then_inc(consts, 1)
            pool.affine_select(out=triI[:], in_=triI[:], compare_op=ALU.is_gt, fill=1.0, base=0,
                               pattern=[[-1, NB]], channel_multiplier=1).then_inc(consts, 1)
            pool.affine_select(out=triE[:], in_=triE[:], compare_op=ALU.is_ge, fill=1.0, base=0,
                               pattern=[[-1, NB]], channel_multiplier=1).then_inc(consts, 1)

            offs = bass.IndirectOffsetOnAxis

            def gather(dst, table, index):
                return pool.indirect_dma_start(dst, None, table, offs(ap=index, axis=0))

            def scatter(table, index, src, **kw):
                return pool.indirect_dma_start(table, offs(ap=index, axis=0), src, None, **kw)

            pool.wait_ge(row_index, 1)
            dst_rows = a["dst"].rearrange("(t n) -> t n", n=ROW)
            for b in range(NB):
                gather(dstrow[:, b], dst_rows, SI(0)[:, b:b + 1]).then_inc(row_in, 16)
            pool.wait_ge(rank_done, 1)
            for b in range(NB):
                scatter(info_tab, SI(3)[:, b:b + 1], info[:, b]).then_inc(info_out, 16)
            pool.wait_ge(info_in, 16)
            for k in range(NSTAGE):
                pool.wait_ge(stage_out[k], 32 * len(PAIRS[k::NSTAGE]))
            pool.wait_ge(own_x_out, 16)
            pool.wait_ge(rec_out, 32)
            for b in range(NB):
                gather(ownR[:, b], own_tab, infoR[:, b, 0:1]).then_inc(own_in, 16)

            def gather_loop(L, buf, table):
                pairs = pool.value_load(totI[0:1, 0:1], min_val=HI + 1, max_val=STEPS // 2 - 8)
                pool.wait_ge(L.win_ready, 1)
                gather(rec[0][:].rearrange("p s c -> p (s c)"), rec_tab, win[0][:]).then_inc(L.rec_landed[0], 16)
                with pool.Fori(0, pairs) as i:
                    for u in range(2):
                        word = pool.value_load(stepW[0:1, bass.ds(2 * i + u, 1)], min_val=0, max_val=WMAX)
                        left = word & 31
                        pool.wait_ge(L.rec_landed[u], 16 * (i + 1))
                        pool.wait_ge(L.free, 2 * i + u + 1)
                        pool.sem_inc(pool_steps, 1)
                        for s in range(SLOTS // SUB):
                            if s == 2:
                                pool.wait_ge(L.win_ready, 2 * i + u + 2)
                                pool.wait_ge(L.rec_used, 2 * i + u + 1)
                                pool.sem_inc(pool_steps, 1)
                                gather(rec[1 - u][:].rearrange("p s c -> p (s c)"), rec_tab,
                                       win[1 - u][:]).then_inc(L.rec_landed[1 - u], 16)
                            with (pool.If(left >= s * SUB + 1) if s else nullcontext()):
                                for j in range(s * SUB, s * SUB + SUB):
                                    gather(buf[u][:, j], table, rec[u][:, j, 0:1]).then_inc(
                                        L.rows_landed[u], 16)
                pool.wait_ge(L.rec_landed[0], 16 * (pairs + 1))
                pool.sem_inc(pool_steps, 1)

            pool.wait_ge(steps_in, 16)
            pool.iota(colI, pattern=[[1, GW]], base=0, channel_multiplier=0,
                      allow_small_or_imprecise_dtypes=True).then_inc(col_ready, 1)
            pool.wait_ge(w_spread, 1)
            pool.affine_select(out=Wslots[:], in_=Wslots[:], compare_op=ALU.is_ge, fill=0.0, base=0,
                               pattern=[[-3, SLOTS], [0, C]], channel_multiplier=1)
            pool.drain()
            pool.affine_select(out=Wslots[:], in_=Wslots[:], compare_op=ALU.is_ge, fill=0.0, base=2,
                               pattern=[[3, SLOTS], [0, C]], channel_multiplier=-1).then_inc(w_diag, 1)
            pool.wait_ge(codes_out, 16)
            gather_loop(LOOP0, G, kv_tab)
            pool.wait_ge(ab_done, 1)
            for b in range(NB):
                scatter(b_tab, infoR[:, b, 0:1], sR[:, b]).then_inc(b_out, 16)
            pool.wait_ge(b_out, 16 * NB)
            gather_loop(LOOP1, G1, b_tab)
            pool.wait_ge(x2_done, 1)
            big = pool.value_load(totI[0:1, 2:3], min_val=0, max_val=1)
            with pool.If(big > 0):
                for b in range(NB):
                    scatter(x2_tab, infoR[:, b, 0:1], xN[:, b]).then_inc(x2_out, 16)
                pool.wait_ge(x2_out, 16 * NB)
                gather_loop(LOOP2, G1, x2_tab)
                pool.wait_ge(tp_evac, TP_H1)
                for b in range(NB):
                    scatter(h1_tab, infoR[:, b, 0:1], h1R[:, b]).then_inc(h1_out, 16)
                pool.wait_ge(h1_out, 16 * NB)
                gather_loop(LOOP3, G3, h1_tab)
            pool.wait_ge(hist_out, 16)
            pool.wait_ge(z_done, 2)
            for b in range(NB):
                gather(cntR[:, b, 0], cnt_tab, infoR[:, b, 0:1]).then_inc(cnt_in, 16)
            pool.wait_ge(final_done, 1)
            for b in range(NB):
                scatter(out, infoR[:, b, 0:1], sumL3[:, b], bounds_check=N - 1, oob_is_err=False).then_inc(
                    final_out, 16)
            pool.wait_ge(final_out, 16 * NB)

        @block.tensor
        def _(pe):
            ring = {"tp": 0, "mm": 0}

            def transpose_group(aps):
                k = ring["tp"]
                if k >= 2:
                    pe.wait_ge(tp_evac, k - 1)
                for j, ap in enumerate(aps):
                    last = pe.transpose(tp[0:ap.shape[1], k % 2, j * P:(j + 1) * P], ap, ident[:])
                last.then_inc(tp_full, 1)
                ring["tp"] = k + 1

            def transpose_all(src, w=None):
                for g in GROUPS:
                    transpose_group([src(b) for b in g])
                pe.wait_ge(tp_evac, ring["tp"])

            def product_group(parts):
                k = ring["mm"]
                if k >= 2:
                    pe.wait_ge(mm_evac, k - 1)
                for rows, cols, terms in parts:
                    for t, (l, r) in enumerate(terms):
                        last = pe.matmul(mm[0:rows, k % 2, cols[0]:cols[1]], l, r,
                                         start=(t == 0), stop=(t == len(terms) - 1))
                last.then_inc(mm_full, 1)
                ring["mm"] = k + 1

            cols = lambda b: slice(b * P, (b + 1) * P)

            pe.wait_ge(consts, NCONST)
            pe.wait_ge(pads_clear, 1)
            pe.wait_ge(x_in, 32)
            transpose_all(lambda b: xN[:, b])
            pe.wait_ge(w_in, 16 * NW)
            for pair in PAIRS:
                product_group([(P, (4 * C * j, 4 * C * (j + 1)), [(T1[0:C + 1, cols(b)], Wkvqf[:])])
                               for j, b in enumerate(pair)])
            pe.wait_ge(edge_full, 1)
            pe.wait_ge(we_spread, 1)
            product_group([(P, (C * j, C * (j + 1)), [(WeB[:, j], Wedge[:])]) for j in range(4)]
                          + [(P, (4 * C, 4 * C + 1), [(ones[0:NV, :], lsum[0:NV, 0:1])]),
                             (3 * SLOTS, (5 * C, 6 * C), [(WeR[:].rearrange("p s k -> p (s k)"), Wedge[:])])])
            pe.wait_ge(deg_done, 1)
            pe.transpose(l3[0:NB, 0, 0:P], S(DEGR_), ident[:]).then_inc(degT_full, 1)
            pe.wait_ge(nit_done, 1)
            pe.matmul(l3[:, 1, 0:NB], bcast[:, 0], triI[:], start=True, stop=True)
            pe.matmul(l3[:, 1, NB:2 * NB], bcast[:, 0], triE[:], start=True, stop=True)
            pe.matmul(l3[:, 1, 2 * NB:3 * NB], bcast[:, 1], ident[0:NB, 0:NB], start=True, stop=True).then_inc(
                cum_full, 1)
            def clear_counts():
                for j in range(3):
                    pe.matmul(l3[:, j, 0:GW // 3], zerosb[:, 0:P], zerosb[:], start=True, stop=True)

            def count_slots(hot):
                for j in range(4):
                    for b3 in range(3):
                        last = pe.matmul(l3[:, b3, 0:GW // 3], identB[:], hot[:, j, b3 * (GW // 3):(b3 + 1) * (GW // 3)],
                                         start=False, stop=True, skip_group_check=True)
                return last

            def transpose_counts(done):
                pe.wait_ge(at_ready, done)
                pe.wait_ge(a_bytes, done)
                for t in range(NB):
                    bank = at_banks[t // 8].bitcast(BF16)
                    k, c = divmod(t, GT)
                    last = pe.transpose(bank[:, (t % 8) * P:(t % 8 + 1) * P], a_blk[:, k, c * P:(c + 1) * P], identB[:])
                last.then_inc(at_full, 1)

            pe.wait_ge(tp_evac, ring["tp"])
            pe.wait_ge(mm_evac, ring["mm"])
            pe.wait_ge(steps_in, 16)
            pe.wait_ge(oh_ready, 1)
            clear_counts()
            pe.matmul(wsum[1], zerosb[:, 0:P], zerosb[:, 0:C + HEADS], start=True, stop=True)
            pe.drain().then_inc(weighted_sums, 1)
            pe.drain().then_inc(at_full, 1)
            pairs = pe.value_load(totI[0:1, 0:1], min_val=HI + 1, max_val=STEPS // 2 - 8)
            with pe.Fori(0, pairs) as i:
                for u in range(2):
                    word = pe.value_load(stepW[0:1, bass.ds(2 * i + u, 1)], min_val=0, max_val=WMAX)
                    new = word & 32
                    pe.wait_ge(ohA_ready, 2 * i + u + 1)
                    count_slots(onehotA).then_inc(ohA_summed, 1)
                    with pe.If(new > 0):
                        pe.wait_ge(a_copied, finished(word))
                        clear_counts()
                    for q in range(3):
                        pe.wait_ge(oh_ready, 6 * i + 3 * u + q + 2)
                        count_slots(onehot[:, (u + q) % 2]).then_inc(oh_summed, 1)
                    pe.wait_ge(weighted_ready, 2 * i + u + 1)
                    for s in range(SLOTS):
                        last = pe.matmul(wsum[u], ident[:], weighted[u][:, s], start=(s == 0), stop=(s == SLOTS - 1))
                    last.then_inc(weighted_sums, 1)
                    with pe.If(new > 0):
                        transpose_counts(finished(word))
            pe.wait_ge(ohA_ready, 2 * pairs + 1)
            count_slots(onehotA).then_inc(ohA_summed, 1)
            transpose_counts(NB)
            pe.wait_ge(at_ready, NB + 1)
            pe.wait_ge(wv_done, 1)
            transpose_all(lambda b: sR[:, b])
            for g in GROUPS:
                product_group([(P, (C * j, C * (j + 1)), [(T1[0:C + 1, cols(b)], Wo[:])])
                               for j, b in enumerate(g)])
            pe.wait_ge(x1_done, 1)
            transpose_all(lambda b: x1R[:, b])
            for g in GROUPS:
                product_group([(C, (0, P * len(g)), [(W1[:], T2[0:C, g[0] * P:(g[-1] + 1) * P])])])
            pe.wait_ge(mm_evac, ring["mm"])
            for pair in PAIRS:
                product_group([(P, (4 * C * j, 4 * C * j + 3 * C), [(T1[0:C + 1, cols(b)], Wabm[:])])
                               for j, b in enumerate(pair)])
            def step1(i, u, with_hist):
                pe.wait_ge(attrs_ready, 2 * i + u + 1)
                pe.matmul(tp[0:3 * SLOTS, u, 0:P], eam[u].rearrange("p s k -> p (s k)"), ident[:],
                          start=True, stop=True).then_inc(attrsT_full, 1)
                pe.wait_ge(attrsT_ready, 2 * i + u + 1)
                pe.wait_ge(h_ready, 2 * i + u + 1)
                for j in range(2):
                    last = pe.matmul(mm[:, j, :], eaT[u], Wslots[:, 8 * j:8 * j + 8].rearrange("p s c -> p (s c)"),
                                     start=True, stop=True)
                last.then_inc(edge_terms, 1)
                for q in range(4 if with_hist else 0):
                    pe.wait_ge(hist_oh, 8 * i + 4 * u + q + 2)
                    for j in range(4):
                        last = pe.matmul(hist[:, 0:NB * R], oh_lo[:, q % 2, j], oh_hi[:, q % 2, j],
                                         start=False, stop=True, skip_group_check=True)
                    last.then_inc(hist_mm, 1)
                pe.wait_ge(sq_ready, 2 * i + u + 1)
                pe.wait_ge(sums_used, 2 * i + u + 1)
                for s in range(SLOTS):
                    last = pe.matmul(l3[:, u, 0:2 * C], ident[:], hh[u][:, s], start=(s == 0), stop=(s == SLOTS - 1))
                last.then_inc(sums_full, 1)

            pe.wait_ge(mm_evac, ring["mm"])
            pe.wait_ge(w_diag, 1)
            pe.wait_ge(hist_oh, 1)
            pe.matmul(hist[:, 0:NB * R], zerosb[:, 0:P], zerosb[:, 0:NB * R], start=True, stop=True)
            pe.matmul(l3[:, 1, 0:2 * C], zerosb[:, 0:P], zerosb[:, 0:2 * C], start=True, stop=True).then_inc(sums_full, 1)
            pairs = pe.value_load(totI[0:1, 0:1], min_val=HI + 1, max_val=STEPS // 2 - 8)
            with pe.Fori(0, HI) as i:
                for u in range(2):
                    step1(i, u, True)
            with pe.Fori(HI, pairs) as i:
                for u in range(2):
                    step1(i, u, False)
            pe.wait_ge(agg_done, 1)
            for h in range(2):
                for g in GROUPS:
                    transpose_group([agg[:, b, 2 * h:2 * h + 2].rearrange("p a c -> p (a c)") for b in g])
            pe.wait_ge(tp_evac, ring["tp"])
            for g in GROUPS:
                product_group([(P, (P * j, P * (j + 1)),
                                [(aggT[h][:, cols(b)], Wagg[:, h].rearrange("p a c -> p (a c)")) for h in range(2)])
                               for j, b in enumerate(g)])
            pe.wait_ge(out_done, 1)
            transpose_all(lambda b: sR[:, b])
            for pair in PAIRS:
                parts = []
                for j, b in enumerate(pair):
                    o = 4 * C * j
                    xb, ob = T2[0:C + 1, cols(b)], T1[0:C + 1, cols(b)]
                    parts += [(P, (o, o + 2 * C), [(xb, Whh[:, 0:2 * C]), (ob, Wih[:, 0:2 * C])]),
                              (P, (o + 2 * C, o + 3 * C), [(ob, Wih[:, 2 * C:])]),
                              (P, (o + 3 * C, o + 4 * C), [(xb, Whh[:, 2 * C:])])]
                product_group(parts)

            def mlp(Wa, Wb, src, rows):
                transpose_all(src)
                for g in GROUPS:
                    product_group([(P, (0, P * len(g)), [(Wa[:], T1[0:rows, g[0] * P:(g[-1] + 1) * P])])])
                first = ring["mm"] - len(GROUPS)
                for n, g in enumerate(GROUPS):
                    pe.wait_ge(mm_evac, first + n + 1)
                    product_group([(P, (0, P * len(g)), [(Wb[:], T2[:, g[0] * P:(g[-1] + 1) * P])])])
                pe.wait_ge(mm_evac, ring["mm"])

            def conv(c, parts):
                pe.wait_ge(mm_evac, ring["mm"])
                pe.wait_ge(parts_ready, c + 1)
                w = parts.shape[2] * parts.shape[3]
                with pe.Fori(0, 5) as i:
                    for k in range(5):
                        pe.wait_ge(at_in[k], 16 * (i + 5 * c + 1))
                        pe.wait_ge(conv_evac, 5 * i + (k + 25 * c + 1))
                        for t in range(NB):
                            last = pe.matmul(conv_banks[k][:, 0:w], atL[k][:, cols(t)],
                                             parts[:, t].rearrange("p k c -> p (k c)"),
                                             start=(t == 0), stop=(t == NB - 1))
                        last.then_inc(conv_full, 1)

            pe.wait_ge(x2_done, 1)
            big = pe.value_load(totI[0:1, 2:3], min_val=0, max_val=1)
            with pe.If(big < 1):
                conv(0, parts2)
            pe.wait_ge(z_done, 1)
            mlp(W1a, W1b, lambda b: sR[:, b], C)
            transpose_all(lambda b: hT[:, cols(b)])
            with pe.If(big < 1):
                conv(1, parts3)
            pe.wait_ge(z_done, 2)
            mlp(W2a, W2b, lambda b: h1R[:, b], P)
            for g in GROUPS:
                product_group([(P, (C * j, C * (j + 1)), [(hT[:, cols(b)], Wlin[:])]) for j, b in enumerate(g)])
            pe.wait_ge(x3_done, 1)
            transpose_all(lambda b: x1R[:, b])
            for b in range(NB):
                if b:
                    pe.wait_ge(l3_used, b)
                for j in range(3):
                    last = pe.matmul(l3[:, j, 0:6 * C], T1[0:C + 1, cols(b)],
                                     Wrel[:, 6 * j:6 * j + 6].rearrange("k r n -> k (r n)"), start=True, stop=True)
                last.then_inc(l3_full, 1)

        @block.scalar
        def _(act):
            row = lambda v: v.rearrange("(a n) -> a n", a=1)
            ring = {"tp": 0, "mm": 0, "q": 0}

            def copy_transposed(dst, n, width):
                k = ring["tp"]
                act.wait_ge(tp_full, k + 1)
                act.activation(dst, tp[0:width, k % 2, 0:n], ACT.Copy).then_inc(tp_evac, 1)
                ring["tp"] = k + 1

            def copy_all(dst, width):
                for g in GROUPS:
                    copy_transposed(dst[0:width, g[0] * P:(g[-1] + 1) * P], P * len(g), width)

            def asked():
                act.wait_ge(act_q, ring["q"] + 1)
                ring["q"] += 1

            n = 0

            def w(dst, src):
                nonlocal n
                act.dma_start(dst, src).then_inc(w_in, 16)
                n += 1

            row = lambda v: v.rearrange("(a n) -> a n", a=1)
            for j, k in enumerate(("k", "v", "q", "f")):
                w(Wkvqf[0:C, j * C:(j + 1) * C], a["L0_gnn_W" + k])
                w(Wkvqf[C:C + 1, j * C:(j + 1) * C], row(a["L0_gnn_b" + k]))
            w(Wo[0:C], a["L0_gnn_Wo"])
            w(Wo[C:C + 1], row(a["L0_gnn_bo"]))
            w(W1[:], a["L1_gnn_W"])
            for j in range(2):
                w(Wabm[0:C, j * C:(j + 1) * C], a["L1_gnn_Wpre"][j * C:(j + 1) * C, :])
            w(Wabm[0:C, 2 * C:], a["L1_gnn_Wpost"][0:C, :])
            w(Wabm[C:C + 1, 2 * C:], row(a["L1_gnn_bpost"]))
            w(Wedge[:], a["L1_gnn_Wpre"][2 * C:, :])
            for k in range(3):
                w(WeT[:, 1 + k:2 + k], a["L1_gnn_We"][k, :].rearrange("(n a) -> n a", a=1))
            w(WeT[:, 0:1], a["L1_gnn_be"].rearrange("(n a) -> n a", a=1))
            for j in range(3):
                w(Wpost[:, j], a["L1_gnn_Wpost"][(1 + 4 * j) * C:(5 + 4 * j) * C, :].rearrange(
                    "(h p) n -> p h n", p=P))
            for t, k in ((Wih, "ih"), (Whh, "hh")):
                w(t[0:C], a["L1_gnn_W" + k])
                w(t[C:C + 1], row(a["L1_gnn_b" + k]))
            for t, k in ((W1a, "1a"), (W1b, "1b"), (W2a, "2a"), (W2b, "2b"), (Wlin, "lin")):
                w(t[:], a["L2_gnn_W" + k])
            for j, k in enumerate(("b1a", "b1b", "b2a", "b2b")):
                w(bcol[:, j:j + 1], a["L2_gnn_" + k].rearrange("(n a) -> n a", a=1))
            for j, k in enumerate(("L0_gnn_gamma", "L0_gnn_beta", "L1_gnn_bpre", "L2_gnn_blin")):
                w(rowsB[:, j], row(a[k]).to_broadcast([P, C]))
            w(Wrel[0:C], a["L3_gnn_weights"][2].rearrange("r k n -> k r n"))
            w(Wrel[C:C + 1], a["L3_gnn_biases"][2:3])
            assert n == NW
            copy_all(T1, C)
            act.wait_ge(x_in, 32)
            act.activation(nv[:], nv[:], ACT.Ln, bias=ones[:, 0:1], accum_out=lsum[:, 0:1]).then_inc(edge_full, 1)
            act.wait_ge(key_in, 16)
            for b in range(RANK_DVE, NB):
                act.activation(junk_act, keyB, ACT.Sign, bias=S(NKEY_)[:, b:b + 1], accum_out=S(RANK_)[:, b:b + 1])
                last = act.drain()
            last.then_inc(rank_act, 1)
            def copy_counts(done):
                act.activation(packed.rearrange("p (a c) -> p a c", a=3), l3[:, :, 0:GW // 3], ACT.Copy)
                act.drain().then_inc(a_copied, 1)
                act.wait_ge(at_full, done)
                act.activation(a_blk, packed.bitcast(U8).rearrange("p (c k) -> p k c", k=4)[:, 0:3],
                               ACT.Copy).then_inc(a_bytes, 1)

            def copy_tiles(done):
                act.wait_ge(at_out, 16 * done)
                act.wait_ge(at_full, done + 1)
                for j, bank in enumerate(at_banks):
                    n = min(8 * P, NP - 8 * P * j)
                    last = act.activation(atS[:, 8 * P * j:8 * P * j + n], bank[:, 0:n // 2].bitcast(BF16), ACT.Copy)
                last.then_inc(at_ready, 1)

            act.wait_ge(steps_in, 16)
            act.drain().then_inc(at_ready, 1)
            act.drain().then_inc(at_out, 16)
            pairs = act.value_load(totI[0:1, 0:1], min_val=HI + 1, max_val=STEPS // 2 - 8)
            with act.Fori(0, pairs) as i:
                for u in range(2):
                    word = act.value_load(stepW[0:1, bass.ds(2 * i + u, 1)], min_val=0, max_val=WMAX)
                    new = word & 32
                    with act.If(new > 0):
                        act.wait_ge(ohA_summed, 2 * i + u + 1)
                        copy_counts(finished(word))
                    act.wait_ge(score_ready, 2 * i + u + 1)
                    act.activation(expd[u][:], score[u][:], ACT.Exp, scale=1.0 / 8.0).then_inc(exp_ready, 1)
                    act.wait_ge(ohA_operands, 2 * i + u + 1)
                    act.wait_ge(ohA_summed, 2 * i + u + 1)
                    for j in range(0, 4, 2):
                        for k in range(2):
                            act.activation(distance[k], colI, ACT.Abs, bias=negcode[u][:, j + k:j + k + 1])
                        act.drain()
                        for k in range(2):
                            last = act.activation(onehotA[:, j + k], distance[k], ACT.Relu,
                                                  scale=negdigit[u][:, j + k:j + k + 1],
                                                  bias=digit[u][:, SLOTS - 4 + j + k:SLOTS - 3 + j + k])
                        if j == 0:
                            act.drain()
                    last.then_inc(ohA_ready, 1)
                    with act.If(new > 0):
                        copy_tiles(finished(word))
            act.wait_ge(ohA_summed, 2 * pairs + 1)
            copy_counts(NB)
            copy_tiles(NB)
            copy_all(T1, C)

            def std(first=True):
                asked()
                act.activation(S(STD_), S(VAR_), ACT.Sqrt, bias=epsb[:], scale=1.0 / C).then_inc(act_r, 1)

            std()
            std()
            copy_all(T2, C)
            pairs = act.value_load(totI[0:1, 0:1], min_val=HI + 1, max_val=STEPS // 2 - 8)
            with act.Fori(0, pairs) as i:
                for u in range(2):
                    act.wait_ge(attrsT_full, 2 * i + u + 1)
                    act.activation(eaT[u], tp[0:3 * SLOTS, u, 0:P], ACT.Copy).then_inc(attrsT_ready, 1)
                    act.wait_ge(h_ready, 2 * i + u + 2)
                    act.activation(hh[u][:, :, C:], hh[u][:, :, 0:C], ACT.Square).then_inc(sq_ready, 1)
                    for dst, bias, ready in ((hmax[u], neg[u], hmax_ready), (hmin[u], pos[u], hmin_ready)):
                        for s in range(SLOTS):
                            last = act.activation(dst[:, s], hh[u][:, s, 0:C], ACT.Identity, bias=bias[:, s:s + 1])
                        last.then_inc(ready, 1)
            asked()
            act.activation(S(LOGD_), S(LOGD_), ACT.Ln, bias=ones[:, 0:1]).then_inc(act_r, 1)
            asked()
            act.activation(agg[:, :, 3], accS2, ACT.Sqrt, bias=epsb[:]).then_inc(act_r, 1)
            for h in range(2):
                copy_all(aggT[h], P)
            copy_all(T1, C)
            asked()
            act.activation(gates[:, :, 0:2 * C], gates[:, :, 0:2 * C], ACT.Sigmoid).then_inc(act_r, 1)
            asked()
            act.activation(sR, sR, ACT.Tanh).then_inc(act_r, 1)
            std()
            for first in (True, False):
                copy_all(T1, C if first else P)
                for layer in range(2):
                    for g in GROUPS:
                        k = MM_MLP[0 if first else 1] + layer * 7 + g[0] // 4
                        n = P * len(g)
                        act.wait_ge(mm_full, k + 1)
                        act.activation((T2 if layer == 0 else hT)[:, g[0] * P:g[0] * P + n], mm[:, k % 2, 0:n], ACT.Relu,
                                       bias=bcol[:, (0 if first else 2) + layer:(0 if first else 2) + layer + 1]).then_inc(
                                           mm_evac, 1)
                if first:
                    for g in GROUPS:
                        copy_transposed(h1R[:, g[0]:g[-1] + 1].rearrange("p b c -> p (b c)"), P * len(g), P)
            std()
            copy_all(T1, C)
            std()

        @block.vector
        def _(dve):
            ring = {"mm": 0, "q": 0, "stage": 0}
            tt, ts, stt, red_ = dve.tensor_tensor, dve.tensor_scalar, dve.scalar_tensor_tensor, dve.tensor_reduce
            d = dve.drain

            def mm_take(fn):
                k = ring["mm"]
                dve.wait_ge(mm_full, k + 1)
                fn(mm[:, k % 2]).then_inc(mm_evac, 1)
                ring["mm"] = k + 1

            def ask(ins):
                ins.then_inc(act_q, 1)
                ring["q"] += 1
                dve.wait_ge(act_r, ring["q"])

            dve.memset(xN[96:P], 0.0)
            dve.memset(nv[96:P], 0.0)
            dve.memset(T1[C:C + 1], 1.0)
            dve.memset(Wabm[C:C + 1, 0:2 * C], 0.0)
            dve.memset(zerosb[:], 0.0)
            dve.memset(codes[:], 1.0)
            dve.memset(totF[:, 1:2], float(E))
            dve.memset(epsb[:], EPS)
            dve.memset(accT[:], 0.0)
            d().then_inc(pads_clear, 1)
            dve.wait_ge(consts, NCONST)
            dve.tensor_copy(nodeF[:], nodeI[:])
            dve.tensor_copy(slotF[:], slotI[:])
            dve.tensor_copy(relF[:], relI[:])
            dve.tensor_copy(gF[:], gI[:])
            dve.tensor_copy(identB[:], ident[:])
            dve.wait_ge(edges_in, 64)
            dve.tensor_copy(tmin_small, dst_sb[:, 0:EW:ROW]).then_inc(tmin_cast, 1)
            dve.tensor_copy(rec_sb[:, :, 0], src_sb)
            dve.tensor_copy(rec_sb[:, :, 5], typ_sb)
            dve.tensor_copy(rec_sb[:, :, 1:5], attr_sb.bitcast(I32)).then_inc(rec_built, 1)
            dve.wait_ge(tmin_in, 16)
            d()
            for b in range(NB):
                ts(junk_dve[:, 0:NROW], tminB, nodeF[:, b:b + 1], None, op0=ALU.is_lt, op1=ALU.add,
                   accum_out=S(K_)[:, b:b + 1])
                d()
            ts(S(K_), S(K_), -1.0, 0.0, op0=ALU.add, op1=ALU.max)
            d()
            dve.tensor_copy(SI(0), S(K_)).then_inc(row_index, 1)
            dve.wait_ge(w_in, 16 * NW)
            dve.tensor_copy(WeB, bc(WeT[:], P))
            dve.tensor_copy(WeR[:], bm(WeT[:, 1:4], SLOTS))
            tt(Wagg[:, :, 0], Wpost[:, 0], Wpost[:, 2], ALU.add)
            dve.tensor_copy(Wagg[:, :, 1], Wpost[:, 1])
            d().then_inc(we_spread, 1)
            for pair in PAIRS:
                s = ring["stage"] % NSTAGE
                if ring["stage"] >= NSTAGE:
                    dve.wait_ge(stage_out[s], 32 * (ring["stage"] // NSTAGE))
                n = len(pair)
                mm_take(lambda bank: dve.tensor_copy(stage[:, s, 0:n].rearrange("p a c -> p (a c)"),
                                                     bank[:, 0:4 * C * n]))
                d().then_inc(stage_ready, 1)
                ring["stage"] += 1
            dve.wait_ge(mm_full, ring["mm"] + 1)
            dve.tensor_copy(edgeB[:].rearrange("p a c -> p (a c)"), mm[:, ring["mm"] % 2, 0:4 * C])
            dve.tensor_copy(Wslots[:], bm(mm[0:3 * SLOTS, ring["mm"] % 2, 5 * C:6 * C], SLOTS)).then_inc(w_spread, 1)
            ts(lsum[:, 1:2], mm[:, ring["mm"] % 2, 4 * C:4 * C + 1], 1.0 / N, None, op0=ALU.mult).then_inc(mm_evac, 1)
            ring["mm"] += 1
            dve.wait_ge(row_in, 16 * NB)
            cmp_row = junk_dve[:, 0:NB * ROW].rearrange("p (b n) -> p b n", n=ROW)
            tt(cmp_row, dstrow, bc(nodeF[:], ROW), ALU.is_lt)
            d()
            red_(S(CNT_), cmp_row, X_AXIS, ALU.add)
            d()
            stt(out=S(START_), in0=S(K_), scalar=float(ROW), in1=S(CNT_), op0=ALU.mult, op1=ALU.add).then_inc(start_done, 1)
            dve.wait_ge(end_in, 16)
            tt(S(DEG_), S(END_), S(START_), ALU.subtract)
            d()
            ts(S(KEYN_), S(DEG_), 4000.0, KEY, op0=ALU.min, op1=ALU.mult)
            d()
            tt(S(KEYN_), S(KEYN_), nodeF[:], ALU.add)
            d()
            ts(S(NKEY_), S(KEYN_), -1.0, None, op0=ALU.mult)
            dve.tensor_copy(info[:, :, 0], nodeI[:])
            dve.tensor_copy(info[:, :, 1], S(START_))
            dve.tensor_copy(info[:, :, 2], S(END_))
            d().then_inc(key_done, 1)
            dve.wait_ge(key_in, 16)
            for b in range(RANK_DVE):
                ts(junk_dve, keyB, S(KEYN_)[:, b:b + 1], None, op0=ALU.is_gt, op1=ALU.add,
                   accum_out=S(RANK_)[:, b:b + 1])
                d()
            dve.wait_ge(rank_act, 1)
            ts(S(RANK_)[:, RANK_DVE:], S(RANK_)[:, RANK_DVE:], float(NP - 1), 0.5, op0=ALU.add, op1=ALU.mult)
            d()
            dve.tensor_copy(SI(1), S(RANK_))
            ts(S(RA_), S(RANK_), float(GW), None, op0=ALU.is_ge)
            ts(S(RB_), S(RANK_), float(2 * GW), None, op0=ALU.is_ge)
            d()
            ts(S(ZP_), S(RB_), 65280.0, 1.0, op0=ALU.mult, op1=ALU.add)
            tt(S(RB_), S(RA_), S(RB_), ALU.add)
            d()
            stt(out=codes[:, :, 0], in0=S(RB_), scalar=-float(GW), in1=S(RANK_), op0=ALU.mult, op1=ALU.add)
            stt(out=codes[:, :, 1], in0=S(RA_), scalar=255.0, in1=S(ZP_), op0=ALU.mult, op1=ALU.add)
            d().then_inc(codes_done, 1)
            ts(SI(2), SI(1), 7, None, op0=ALU.logical_shift_right)
            ts(SI(4), SI(1), 127, None, op0=ALU.bitwise_and)
            d()
            stt(out=SI(3), in0=SI(4), scalar=float(NB), in1=SI(2), op0=ALU.mult, op1=ALU.add).then_inc(rank_done, 1)
            dve.wait_ge(info_in, 16)
            dve.tensor_copy(S(PTR_), infoR[:, :, 1])
            dve.tensor_copy(S(END_), infoR[:, :, 2])
            d()
            tt(S(DEGR_), S(END_), S(PTR_), ALU.subtract)
            d()
            dve.tensor_copy(S(REM_), S(DEGR_)).then_inc(deg_done, 1)
            dve.wait_ge(degT_full, 1)
            red_(S(MAXD_)[0:NB, 0:1], l3[0:NB, 0, 0:P], X_AXIS, ALU.max)
            d()
            ts(SI(5)[0:NB, 0:1], S(MAXD_)[0:NB, 0:1], 1.0, float(SLOTS - 1), op0=ALU.max, op1=ALU.add)
            d()
            ts(SI(5)[0:NB, 1:2], SI(5)[0:NB, 0:1], 4, None, op0=ALU.logical_shift_right)
            d()
            dve.tensor_copy(S(NIT_)[0:NB, 0:1], SI(5)[0:NB, 1:2])
            d()
            dve.tensor_copy(bcast[:, 0], S(NIT_)[0:NB, 0:1].to_broadcast([NB, P]))
            dve.tensor_copy(bcast[:, 1], S(MAXD_)[0:NB, 0:1].to_broadcast([NB, P]))
            d().then_inc(nit_done, 1)
            dve.wait_ge(cum_full, 1)
            dve.tensor_copy(cum[:].rearrange("p a b -> p (a b)"), l3[:, 1, 0:3 * NB])
            d()
            stt(out=fval[:, 0], in0=cum[:, 1], scalar=float(SLOTS), in1=cum[:, 2], op0=ALU.mult, op1=ALU.add)
            tt(ind3, bc(gF[:], NB), bm(cum[:, 0], SP_), ALU.is_ge)
            ts(totI[:, 1:2], cum[:, 0, NB - 1:NB], 1.0, None, op0=ALU.add)
            d()
            tt(fval[:, 1, 0:NB - 1], fval[:, 0, 1:NB], fval[:, 0, 0:NB - 1], ALU.subtract)
            red_(tabF[:, 0], ind3, X_AXIS, ALU.add)
            d()
            tt(ind3, bc(gF[:], NB), bm(cum[:, 0], SP_), ALU.is_equal)
            ts(totI[:, 2:3], cum[:, 2, 0:1], 255.0, None, op0=ALU.is_gt)
            d()
            red_(tabF[:, 2], ind3[:, :, 0:NB - 1], X_AXIS, ALU.add)
            d()
            tt(ind3, bc(gF[:], NB), bm(cum[:, 0], SP_), ALU.is_ge)
            ts(totI[:, 0:1], totI[:, 1:2], 1, None, op0=ALU.logical_shift_right)
            d()
            tt(indw[:, :, 0:NB - 1], ind3[:, :, 0:NB - 1], bm(fval[:, 1, 0:NB - 1], SP_), ALU.mult)
            ts(totI[:, 0:1], totI[:, 0:1], float(HI + 1), None, op0=ALU.max)
            d()
            red_(tabF[:, 1], indw[:, :, 0:NB - 1], X_AXIS, ALU.add)
            d()
            ts(tabF[:, 1], tabF[:, 1], fval[:, 0, 0:1], None, op0=ALU.add)
            d()
            stt(out=tabF[:, 1], in0=gF[:], scalar=-float(SLOTS), in1=tabF[:, 1], op0=ALU.mult, op1=ALU.add)
            ts(tabF[:, 0], tabF[:, 0], float(NB - 1), 64.0, op0=ALU.min, op1=ALU.mult)
            d()
            ts(tabF[:, 1], tabF[:, 1], 0.0, float(SLOTS), op0=ALU.max, op1=ALU.min)
            stt(out=tabF[:, 0], in0=tabF[:, 2], scalar=32.0, in1=tabF[:, 0], op0=ALU.mult, op1=ALU.add)
            d()
            tt(tabI[:], tabF[:, 0], tabF[:, 1], ALU.add)
            d().then_inc(steps_done, 1)

            dve.wait_ge(hist_in, 32)
            ts(hsrc_q, hsrc, 5243.0, None, op0=ALU.mult)
            d()
            ts(hsrc_q, hsrc_q, 17, None, op0=ALU.logical_shift_right)
            d()
            dve.tensor_copy(part, hsrc_q)
            d()
            stt(out=code, in0=part, scalar=-float(NB), in1=hsrc, op0=ALU.mult, op1=ALU.add)
            d()
            stt(out=code, in0=code, scalar=float(R), in1=htyp, op0=ALU.mult, op1=ALU.add)
            d().then_inc(hist_oh, 1)

            landed = [dve.alloc_register(f"rows_expected{u}") for u in range(2)]

            before = dve.alloc_register("word_before")
            word = [dve.alloc_register(f"word{u}") for u in range(2)]
            ahead = [dve.alloc_register(f"word_ahead{u}") for u in range(2)]
            block_in = lambda reg: nc.s_assert_within(dve.snap(reg) >> 6, 0, NB - 1)

            def load_word(reg, g):
                w = dve.value_load(stepW[0:1, bass.ds(g, 1)], min_val=0, max_val=WMAX)
                dve.reg_mov(reg, dve.snap(w))

            def expect_rows(u):
                left = dve.snap(word[u]) & 31
                fours = dve.snap(((left + 3) >> 2) + (left < 1))
                dve.reg_add(landed[u], landed[u], dve.snap(fours * 64))

            def wait_rows(L, u):
                dve.wait_ge(L.rows_landed[u], dve.snap(landed[u]))

            def prepare_step(g, u):
                load_word(ahead[u], g + 2)
                expect_rows(u)

            def end_step(u):
                dve.reg_mov(before, word[u])
                dve.reg_mov(word[u], ahead[u])

            def begin_loop(L):
                dve.reg_mov(before, 0)
                for u in range(2):
                    dve.reg_mov(landed[u], 0)
                    load_word(word[u], u)
                    next_window(L, u, block_in(word[u]))
                prepare_step(0, 0)
                d().then_inc(L.rec_used, 1)
                d().then_inc(L.free, 2)

            def next_window(L, u, blk):
                p_ = small[:, PTR_, bass.ds(blk, 1)]
                ts(win[u][:], p_, float(E), None, op0=ALU.min)
                d()
                ts(p_, p_, float(SLOTS), None, op0=ALU.add)
                d().then_inc(L.win_ready, 1)

            def step_head(L, i, u):
                blk = block_in(word[u])
                dve.wait_ge(L.rec_landed[u], 16 * (i + 1))
                next_window(L, u, block_in(ahead[u]))
                r_ = small[:, REM_, bass.ds(blk, 1)]
                ts(masks[u], slotF[:], r_, None, op0=ALU.is_lt)
                d()
                ts(r_, r_, -float(SLOTS), None, op0=ALU.add)
                return blk

            def reset_loop():
                dve.tensor_copy(S(PTR_), infoR[:, :, 1])
                dve.tensor_copy(S(REM_), S(DEGR_))

            flat = lambda ap: ap.rearrange("p s c -> p (s c)")

            dve.wait_ge(steps_in, 16)
            dve.wait_ge(own_in, 16 * NB)
            dve.memset(accV, 0.0)
            dve.wait_ge(rec_out, 32)
            for u in range(2):
                dve.memset(G[u], 0.0)
            begin_loop(LOOP0)
            dve.wait_ge(steps_in, 16)

            dve.wait_ge(col_ready, 1)
            d().then_inc(oh_summed, 2)
            dve.memset(onehotA, 0.0)
            d().then_inc(ohA_ready, 1)
            d().then_inc(oh_ready, 1)

            def step0(i, u):
                blk = step_head(LOOP0, i, u)
                tt(eqt[:], bm(rec[u][:, :, 5], R), bc(relF[:], SLOTS), ALU.is_equal)
                d()
                tt(eqt[:], eqt[:], bm(masks[u], R), ALU.mult)
                d()
                red_(redt[:], eqt[:], X_AXIS, ALU.add)
                d()
                t_ = accT[:, bass.ds(blk, 1), :]
                tt(t_, t_, redt[:].unsqueeze(1), ALU.add)
                wait_rows(LOOP0, u)
                q_ = ownR[:, bass.ds(blk, 1), 0:C].to_broadcast([P, SLOTS, C])
                tt(prod[:, :, 0:C], G[u][:, :, 0:C], q_, ALU.mult).then_inc(LOOP0.rec_used, 1)
                prepare_step(2 * i + u + 1, 1 - u)
                d()
                red_(score[u][:], prod[:, :, 0:C].rearrange("p s (h c) -> p s h c", h=HEADS), X_AXIS, ALU.add)
                d()
                ts(score[u][:], score[u][:], -40.0, 40.0, op0=ALU.max, op1=ALU.min).then_inc(score_ready, 1)
                tt(digit[u], G[u][:, :, 2 * C + 1], masks[u], ALU.mult)
                ts(negcode[u], G[u][:, SLOTS - 4:, 2 * C], -1.0, None, op0=ALU.mult)
                d()
                ts(negdigit[u], digit[u][:, SLOTS - 4:], -1.0, None, op0=ALU.mult).then_inc(ohA_operands, 1)
                for q in range(3):
                    dve.wait_ge(oh_summed, 6 * i + 3 * u + q + 1)
                    for j in range(4):
                        s = 4 * q + j
                        last = ts(onehot[:, (u + q) % 2, j], colI, G[u][:, s, 2 * C:2 * C + 1], digit[u][:, s:s + 1],
                                  op0=ALU.is_equal, op1=ALU.mult)
                    last.then_inc(oh_ready, 1)
                dve.wait_ge(exp_ready, 2 * i + u + 1)
                e_ = weighted[u][:, :, C:C + HEADS]
                tt(e_, expd[u][:], bc(masks[u], HEADS), ALU.mult)
                add_weighted(2 * i + u, 1 - u)
                d()
                tt(weighted[u][:, :, 0:C].rearrange("p s (h c) -> p s h c", h=HEADS),
                   G[u][:, :, C:2 * C].rearrange("p s (h c) -> p s h c", h=HEADS),
                   e_.unsqueeze(3).to_broadcast([P, SLOTS, HEADS, HD]), ALU.mult).then_inc(weighted_ready, 1)
                end_step(u)
                d().then_inc(LOOP0.free, 1)

            def add_weighted(g, u):
                dve.wait_ge(weighted_sums, g + 1)
                v_ = accV[:, bass.ds(block_in(before), 1), :]
                tt(v_, v_, wsum[u].unsqueeze(1), ALU.add)

            pairs = dve.value_load(totI[0:1, 0:1], min_val=HI + 1, max_val=STEPS // 2 - 8)
            with dve.Fori(0, pairs) as i:
                for u in range(2):
                    step0(i, u)
            dve.wait_ge(LOOP0.rec_landed[0], 16 * (pairs + 1))
            add_weighted(2 * pairs, 1)
            d()
            dve.wait_ge(at_full, NB + 1)
            dve.wait_ge(at_out, 16 * (NB + 1))
            dve.memset(T1[C:C + 1], 1.0)
            dve.memset(T2[C:C + 1], 1.0)

            flat3 = lambda ap: ap.rearrange("p b c -> p (b c)")
            scr = prod.rearrange("p s c -> p (s c)")[:, 0:NB * C].rearrange("p (b c) -> p b c", c=C)

            def layernorm(dst, src, dfin=True):
                red_(S(MU_), src, X_AXIS, ALU.add)
                d()
                ts(S(MU_), S(MU_), 1.0 / C, None, op0=ALU.mult)
                d()
                tt(src, src, bc(S(MU_), C), ALU.subtract)
                d()
                tt(scr, src, src, ALU.mult)
                d()
                red_(S(VAR_), scr, X_AXIS, ALU.add)
                ask(d())
                dve.reciprocal(S(STD_), S(STD_))
                d()
                tt(dst, src, bc(S(STD_), C), ALU.mult)
                d()

            zp = small[:, ZP_:ZP_ + 4, :].rearrange("p a b -> p (a b)").rearrange("p (b h) -> p b h", h=HEADS)
            ts(zp, accV[:, :, C:], 1.0, None, op0=ALU.add)
            d()
            dve.reciprocal(zp, zp)
            d()
            tt(sR.rearrange("p b (h c) -> p b h c", h=HEADS), accV[:, :, 0:C].rearrange("p b (h c) -> p b h c", h=HEADS),
               zp.unsqueeze(3).to_broadcast([P, NB, HEADS, HD]), ALU.mult).then_inc(wv_done, 1)
            own = lambda k: ownR[:, :, k * C:(k + 1) * C]
            for g in GROUPS:
                n = len(g)
                mm_take(lambda bank: tt(own(1)[:, g[0]:g[-1] + 1], own(1)[:, g[0]:g[-1] + 1],
                                        bank[:, 0:C * n].rearrange("p (b c) -> p b c", c=C), ALU.add))
            d()
            dve.tensor_copy(x1R[:], own(1))
            d()
            layernorm(x1R[:], x1R[:])
            tt(x1R[:], x1R[:], bm(rowsB[:, 0], NB), ALU.mult)
            d()
            tt(x1R[:], x1R[:], bm(rowsB[:, 1], NB), ALU.add)
            d()
            tt(x1R[:], x1R[:], own(1), ALU.add)
            d()
            tt(x1R[:], x1R[:], own(2), ALU.add)
            d()
            layernorm(x1R[:], x1R[:])
            d().then_inc(x1_done, 1)
            reset_loop()
            for g in GROUPS:
                n = P * len(g)
                mm_take(lambda bank: dve.tensor_copy(T1[0:C, g[0] * P:g[0] * P + n], bank[0:C, 0:n]))
            dve.memset(accMx, -BIG)
            dve.memset(accMn, BIG)
            dve.memset(accS, 0.0)
            for pair in PAIRS:
                k = ring["mm"]
                dve.wait_ge(mm_full, k + 1)
                s = slice(pair[0], pair[-1] + 1)
                v = mm[:, k % 2].rearrange("p (b c) -> p b c", c=4 * C)[:, 0:len(pair)]
                tt(aR[:, s], v[:, :, 0:C], bm(edgeB[:, 0], len(pair)), ALU.add)
                dve.tensor_copy(sR[:, s], v[:, :, C:2 * C])
                dve.tensor_copy(mpR[:, s], v[:, :, 2 * C:3 * C]).then_inc(mm_evac, 1)
                ring["mm"] += 1
            d().then_inc(ab_done, 1)
            begin_loop(LOOP1)
            dve.memset(hmax[1], -BIG)
            dve.memset(hmin[1], BIG)
            d().then_inc(hmax_ready, 1)
            d().then_inc(hmin_ready, 1)
            d().then_inc(hist_mm, 2)
            d().then_inc(h_ready, 1)
            d().then_inc(sums_used, 1)

            def add_step(g, u):
                blk = block_in(before)
                row_of = lambda acc: acc[:, bass.ds(blk, 1), :]
                dve.wait_ge(sums_full, g + 1)
                v_ = row_of(accS)
                tt(v_, v_, l3[:, u:u + 1, 0:2 * C], ALU.add).then_inc(sums_used, 1)
                dve.wait_ge(hmax_ready, g + 1)
                red_(red[:, 0:C], hmax[u].rearrange("p s c -> p c s"), X_AXIS, ALU.max)
                dve.wait_ge(hmin_ready, g + 1)
                red_(red[:, C:2 * C], hmin[u].rearrange("p s c -> p c s"), X_AXIS, ALU.min)
                d()
                v_ = row_of(accMx)
                tt(v_, v_, red[:, 0:C].unsqueeze(1), ALU.max)
                v_ = row_of(accMn)
                tt(v_, v_, red[:, C:2 * C].unsqueeze(1), ALU.min)

            def step1(i, u, with_hist):
                blk = step_head(LOOP1, i, u)
                ea = rec[u][:].bitcast(F32)
                tt(ewm[u], ea[:, :, 4], masks[u], ALU.mult)
                ts(neg[u], masks[u], 1.0, BIG, op0=ALU.subtract, op1=ALU.mult)
                ts(pos[u], masks[u], 1.0, -BIG, op0=ALU.subtract, op1=ALU.mult)
                d()
                tt(eam[u], ea[:, :, 1:4], bc(ewm[u], 3), ALU.mult).then_inc(attrs_ready, 1)
                h = hh[u][:, :, 0:C]
                wait_rows(LOOP1, u)
                tt(h, G1[u], aR[:, bass.ds(blk, 1), :].to_broadcast([P, SLOTS, C]), ALU.add).then_inc(
                    LOOP1.rec_used, 1)
                prepare_step(2 * i + u + 1, 1 - u)
                d().then_inc(LOOP1.free, 1)
                tt(h, h, bc(ewm[u], C), ALU.mult)
                d()
                dve.wait_ge(edge_terms, 2 * i + u + 1)
                tt(h, h, mm[:].rearrange("p a (s c) -> p (a s) c", c=C), ALU.add).then_inc(h_ready, 1)
                for q in range(4 if with_hist else 0):
                    dve.wait_ge(hist_mm, 8 * i + 4 * u + q + 1)
                    for j in range(4):
                        t = bass.ds(16 * (2 * i + u) + 4 * q + j, 1)
                        ts(oh_lo[:, q % 2, j], laneI[0:ROW], part[:, t], None, op0=ALU.is_equal)
                        last = ts(oh_hi[:, q % 2, j], codeI[0:ROW], code[:, t], None, op0=ALU.is_equal)
                    last.then_inc(hist_oh, 1)
                add_step(2 * i + u, 1 - u)
                end_step(u)

            with dve.Fori(0, HI) as i:
                for u in range(2):
                    step1(i, u, True)
            with dve.Fori(HI, pairs) as i:
                for u in range(2):
                    step1(i, u, False)
            d()
            add_step(2 * pairs, 1)
            dve.wait_ge(hist_mm, 8 * HI + 2)
            dve.tensor_copy(histo[:], hist[:, 0:NB * R]).then_inc(hist_done, 1)
            dve.wait_ge(LOOP1.rec_landed[0], 16 * (pairs + 1))
            ts(S(HAS_), S(DEGR_), 0.0, None, op0=ALU.is_gt)
            ts(S(LOGD_), S(DEGR_), 1.0, None, op0=ALU.max)
            d()
            dve.reciprocal(S(SAFE_), S(LOGD_))
            dve.reciprocal(lsum[:, 0:1], lsum[:, 1:2])
            ask(d())
            ts(S(RATIO_), S(LOGD_), lsum[:, 0:1], None, op0=ALU.mult)
            tt(accS1, accS1, bc(S(SAFE_), C), ALU.mult)
            tt(accS2, accS2, bc(S(SAFE_), C), ALU.mult)
            d()
            tt(scr, accS1, accS1, ALU.mult)
            d()
            tt(accS2, accS2, scr, ALU.subtract)
            d()
            ts(accS2, accS2, 0.0, None, op0=ALU.max)
            ask(d())
            for dst, src in ((0, accS1), (1, accMn), (2, accMx)):
                tt(agg[:, :, dst], src, bm(rowsB[:, 2], NB), ALU.add)
            d()
            for dst in range(3):
                tt(agg[:, :, dst], agg[:, :, dst], bc(S(HAS_), C), ALU.mult)
            d().then_inc(agg_done, 1)
            for g in GROUPS:
                k = ring["mm"]
                dve.wait_ge(mm_full, k + 1)
                s = slice(g[0], g[-1] + 1)
                v = mm[:, k % 2].rearrange("p (b c) -> p b c", c=2 * C)[:, 0:len(g)]
                tt(mpR[:, s], mpR[:, s], v[:, :, 0:C], ALU.add)
                tt(sR[:, s], v[:, :, C:2 * C], bc(S(RATIO_)[:, s], C), ALU.mult).then_inc(mm_evac, 1)
                ring["mm"] += 1
            d()
            tt(sR, sR, mpR, ALU.add)
            d().then_inc(out_done, 1)
            for pair in PAIRS:
                n = len(pair)
                mm_take(lambda bank: dve.tensor_copy(flat3(gates[:, pair[0]:pair[-1] + 1]), bank[:, 0:4 * C * n]))
            ask(d())
            gate = lambda k: gates[:, :, k * C:(k + 1) * C]
            tt(sR, gate(0), gate(3), ALU.mult)
            d()
            tt(sR, sR, gate(2), ALU.add)
            ask(d())
            tt(gate(0), x1R[:], sR, ALU.subtract)
            d()
            tt(gate(0), gate(0), gate(1), ALU.mult)
            d()
            tt(gate(0), gate(0), sR, ALU.add)
            d()
            tt(sR, gate(0), x1R[:], ALU.add)
            reset_loop()
            d()
            dve.tensor_copy(x1R[:], sR)
            d()
            layernorm(xN[:], x1R[:])
            d().then_inc(x2_done, 1)

            def sum_loop(L, buf, acc, w):
                for u in range(2):
                    dve.memset(buf[u], 0.0)
                dve.memset(acc, 0.0)
                begin_loop(L)
                pairs = dve.value_load(totI[0:1, 0:1], min_val=HI + 1, max_val=STEPS // 2 - 8)
                with dve.Fori(0, pairs) as i:
                    for u in range(2):
                        blk = step_head(L, i, u)
                        wait_rows(L, u)
                        tt(prod[:, :, 0:w], buf[u], bc(masks[u], w), ALU.mult).then_inc(L.rec_used, 1)
                        prepare_step(2 * i + u + 1, 1 - u)
                        d()
                        red_(red[:, 0:w], prod[:, :, 0:w].rearrange("p s c -> p c s"), X_AXIS, ALU.add)
                        d()
                        v_ = acc[:, bass.ds(blk, 1), :]
                        tt(v_, v_, red[:, 0:w].unsqueeze(1), ALU.add)
                        end_step(u)
                        d().then_inc(L.free, 1)
                dve.wait_ge(L.rec_landed[0], 16 * (pairs + 1))
                reset_loop()

            def conv_sums(c, src, parts, acc, w):
                dve.tensor_copy(parts[:, :, 0], src)
                d()
                tt(acc, src, parts[:, :, 0], ALU.subtract)
                d()
                dve.tensor_copy(parts[:, :, 1], acc)
                d()
                tt(acc, acc, parts[:, :, 1], ALU.subtract)
                d()
                dve.tensor_copy(parts[:, :, 2], acc)
                d().then_inc(parts_ready, 1)
                if c == 0:
                    d().then_inc(conv_evac, 5)
                with dve.Fori(0, 5) as i:
                    for k in range(5):
                        dve.wait_ge(conv_full, 5 * i + (k + 25 * c + 1))
                        red_(acc[:, bass.ds(5 * i + k, 1), :].rearrange("p a c -> p (a c)"),
                             conv_banks[k][:, 0:3 * w].rearrange("p (k c) -> p c k", k=3), X_AXIS,
                             ALU.add).then_inc(conv_evac, 1)
                d()

            big = dve.value_load(totI[0:1, 2:3], min_val=0, max_val=1)
            with dve.If(big < 1):
                conv_sums(0, xN[:], parts2, acc2, C)
            with dve.If(big > 0):
                sum_loop(LOOP2, G1, acc2, C)
            tt(sR, xN[:], acc2, ALU.add)
            d().then_inc(z_done, 1)
            ring["mm"] += 2 * len(GROUPS)
            dve.wait_ge(tp_evac, TP_H1)
            with dve.If(big < 1):
                conv_sums(1, h1R, parts3, acc3, 2 * C)
            with dve.If(big > 0):
                sum_loop(LOOP3, G3, acc3, 2 * C)
            tt(h1R, h1R, acc3, ALU.add)
            d().then_inc(z_done, 1)
            ring["mm"] += 2 * len(GROUPS)
            for g in GROUPS:
                n = len(g)
                mm_take(lambda bank: tt(sR[:, g[0]:g[-1] + 1], xN[:, g[0]:g[-1] + 1],
                                        bank[:, 0:C * n].rearrange("p (b c) -> p b c", c=C), ALU.add))
            d()
            tt(sR, sR, bm(rowsB[:, 3], NB), ALU.add)
            d()
            layernorm(x1R[:], sR)
            dve.memset(T1[C:C + 1], 1.0)
            d().then_inc(x3_done, 1)
            dve.wait_ge(cnt_in, 16 * NB)
            dve.tensor_copy(cntR[:, :, 1], accT[:])
            d()
            cnts = cntR.rearrange("p b a r -> p b (a r)")
            red_(S(CNTT_), cnts, X_AXIS, ALU.add)
            d()
            ts(S(CNTT_), S(CNTT_), 1.0, None, op0=ALU.max)
            d()
            dve.reciprocal(S(CNTT_), S(CNTT_))
            for b in range(NB):
                dve.wait_ge(l3_full, b + 1)
                for j in range(3):
                    tt(prodL3[:, 6 * C * j:6 * C * (j + 1)].rearrange("p (r c) -> p r c", c=C),
                       l3[:, j, 0:6 * C].rearrange("p (r c) -> p r c", c=C),
                       bc(cnts[:, b, 6 * j:6 * j + 6], C), ALU.mult)
                d().then_inc(l3_used, 1)
                red_(sumL3[:, b], prodL3.rearrange("p (r c) -> p c r", c=C), X_AXIS, ALU.add)
                d()
            tt(sumL3, sumL3, bc(S(CNTT_), C), ALU.mult)
            d()
            tt(sumL3, sumL3, x1R[:], ALU.add)
            d()
            layernorm(sumL3, sumL3)
            d().then_inc(final_done, 1)


INPUTS = ["x", "src", "dst", "edge_attr_4", "edge_type_9", "node_vec",
          *("L0_gnn_" + k for k in ("Wq", "bq", "Wk", "bk", "Wv", "bv", "Wo", "bo", "Wf", "bf", "gamma", "beta")),
          *("L1_gnn_" + k for k in ("W", "We", "be", "Wpre", "bpre", "Wpost", "bpost", "Wih", "bih", "Whh", "bhh")),
          *("L2_gnn_" + k for k in ("W1a", "b1a", "W1b", "b1b", "W2a", "b2a", "W2b", "b2b", "Wlin", "blin")),
          "L3_gnn_weights", "L3_gnn_biases"]


def kernel(**inputs):
    import numpy as np
    import concourse.bacc as bacc
    from concourse import mybir as mb
    from concourse.bass_utils import run_bass_kernel_spmd

    nc = bacc.Bacc("TRN2", target_bir_lowering=False, num_devices=1)
    arrays, args = {}, {}
    for name in INPUTS:
        v = np.ascontiguousarray(inputs[name])
        arrays["in_" + name] = v
        args[name] = nc.dram_tensor("in_" + name, v.shape, mb.dt.from_np(v.dtype), kind="ExternalInput").ap()
    out = nc.dram_tensor("out_0", (N, C), mb.dt.float32, kind="ExternalOutput").ap()
    build(nc, args, out)
    r = run_bass_kernel_spmd(nc, [arrays], core_ids=[0])
    return r.results[0]["out_0"]
```

```python
from contextlib import ExitStack, nullcontext

import concourse.bass as bass
from concourse import mybir

F32 = mybir.dt.float32
BF16 = mybir.dt.bfloat16
I32 = mybir.dt.int32
I16 = mybir.dt.int16
U8 = mybir.dt.uint8
ALU = mybir.AluOpType
ACT = mybir.ActivationFunctionType
X_AXIS = mybir.AxisListType.X

P = 128
N, E, C, R = 3125, 100000, 64, 9
NB = 25
NP = NB * P
NV = N // NB
HEADS, HD = 4, 16
SLOTS = 16
SUB = 2
REC = 6
EP, EW = 80, 1250
ROW = 125
NROW = E // ROW
NSTAGE = 2
STEPS = 6400
SP_ = STEPS // P
HI = 25
GT = 9
GW = GT * P
KEY = 4096.0
BIG = 1.0e30
EPS = 1e-5
KV = 2 * C + 2
OWN = 3 * C + 3
GROUPS = [list(range(g, min(g + 4, NB))) for g in range(0, NB, 4)]
PARTS = [(0, 17), (17, 25)]
PAIRS = [list(range(g, min(g + 2, NB))) for g in range(0, NB, 2)]


def build(nc, a, out):
    dram = lambda name, shape, dt=F32: nc.dram_tensor(name, shape, dt, kind="Internal").ap()
    rec_tab = dram("rec_tab", [E + SLOTS, REC], I32)
    dst_tab = dram("dst_tab", [E], I32)
    ptr_tab = dram("ptr_tab", [NP])
    sorted_dst = dram("sorted_dst", [E, 1], I32)
    sorted_rec = dram("sorted_rec", [E, REC], I32)
    tmin_tab = dram("tmin_tab", [NROW], I16)
    start_tab = dram("start_tab", [NP + 1])
    key_tab = dram("key_tab", [NP], I16)
    step_tab = dram("step_tab", [STEPS], I16)
    kv_tab = dram("kv_tab", [NP, KV])
    at_tab = dram("at_tab", [NB, P, NP], BF16)
    own_tab = dram("own_tab", [NP, OWN])
    b_tab = dram("b_tab", [NP, C])
    x2_tab = dram("x2_tab", [NP, C])
    h1_tab = dram("h1_tab", [NP, 2 * C])
    cnt_tab = dram("cnt_tab", [NP, R])

    with ExitStack() as ctx:
        sb = lambda name, shape, dt=F32: ctx.enter_context(nc.sbuf_tensor(name, shape, dt))
        sem = lambda name: ctx.enter_context(nc.semaphore(name))

        arena = sb("arena", [P, 26600])

        def at(off, parts, *shape, dt=F32):
            n = 1
            for s in shape:
                n *= s
            v = arena[0:parts, off:off + n]
            if dt != F32:
                v = v.bitcast(dt)
            if len(shape) == 2:
                v = v.rearrange("p (a b) -> p a b", b=shape[1])
            if len(shape) == 3:
                v = v.rearrange("p (a b c) -> p a b c", b=shape[1], c=shape[2])
            return v

        rec_sb = at(0, EP, EW, REC, dt=I32)
        attr_sb = at(7500, EP, EW, 4)
        dst_sb = at(12500, EP, EW, dt=I32)
        src_sb = at(13750, EP, EW, dt=I32)
        typ_sb = at(15000, EP, EW, dt=I32)
        ownN = at(7500, P, NB, OWN)
        keyB = at(16250, P, NP // 2, dt=I16)
        dstrow = at(19450, P, NB, ROW, dt=I32)
        junk_dve = at(22575, P, NP)
        junk16 = at(22575, P, NP, dt=BF16).rearrange("p (k n) -> p k n", k=2)
        tminB = at(25775, P, NROW // 2, dt=I16)
        junk_act = at(12500, P, NP)
        ind3 = at(16250, P, SP_, NB)
        indw = at(23450, P, SP_, NB)
        G = [at(0, P, SLOTS, KV), at(2080, P, SLOTS, KV)]
        G1 = [at(0, P, SLOTS, C), at(2080, P, SLOTS, C)]
        G3 = [at(0, P, SLOTS, 2 * C), at(2080, P, SLOTS, 2 * C)]
        prod = at(4160, P, SLOTS, 2 * C)
        weighted = [at(6208, P, SLOTS, C + HEADS), at(21754, P, SLOTS, C + HEADS)]
        ownR = at(7296, P, NB, 3 * C)
        accV = at(12100, P, NB, C + HEADS)
        onehotA = at(19450, P, 4 * GW // 2, dt=BF16).rearrange("p (s c) -> p s c", s=4)
        onehot = at(13800, P, 4 * GW, dt=BF16).rearrange("p (r s c) -> p r s c", r=2, s=4)
        colI = at(18408, P, GW // 2, dt=I16)
        atS = at(23450, P, NP // 2, dt=BF16)
        packed = at(25050, P, GW, dt=I32)
        hsrc = at(19450, ROW, NROW, dt=I32)
        accMx = at(14100, P, NB, C)
        accMn = at(15700, P, NB, C)
        accS = at(17300, P, NB, 2 * C)
        accS1, accS2 = accS[:, :, 0:C], accS[:, :, C:]
        hh = [at(4160 + 4240 * u, P, SLOTS, 2 * C + R) for u in range(2)]
        hmax = [at(6352 + 4240 * u, P, SLOTS, C) for u in range(2)]
        hmin = [at(7376 + 4240 * u, P, SLOTS, C) for u in range(2)]
        aR = at(20500, P, NB, C)
        mpR = at(22100, P, NB, C)
        sR = at(23700, P, NB, C)
        agg = at(7296, P, NB, 4, C)
        aggT = [at(14100, P, NP), at(17300, P, NP)]
        gates = at(0, P, NB, 4 * C)
        atL = [at(NP // 2 * k, P, NP // 2, dt=BF16) for k in range(5)]
        h1R = at(8000, P, NB, 2 * C)
        acc3 = at(11200, P, NB, 2 * C)
        acc2 = at(11200, P, NB, C)
        hT = at(14400, P, NP)
        parts2 = at(17600, P, NB * 3 * C // 2, dt=BF16).rearrange("p (b k c) -> p b k c", b=NB, k=3)
        parts3 = at(17600, P, NB * 3 * C, dt=BF16).rearrange("p (b k c) -> p b k c", b=NB, k=3)
        cntR = at(22400, P, NB, 2, R)
        prodL3 = [at(2 * R * C * k, P, 2 * R * C) for k in range(2)]
        sumL3 = at(23700, P, NB, C)

        T1 = sb("T1", [P, NP])
        T2 = sb("T2", [P, NP])
        xN = sb("xN", [P, NB, C])
        x1R = sb("x1R", [P, NB, C])
        stepW = sb("step_word", [1, STEPS], I16)
        stage = T2[:, 0:NSTAGE * 4 * C].rearrange("p (s b c) -> p s b c", s=NSTAGE, b=2)
        accT = sb("accT", [P, NB, R])
        histo = sb("histo", [P, NB * R])
        rec = [sb(f"rec{u}", [P, SLOTS, REC], I32) for u in range(2)]
        win = [sb(f"win{u}", [P, 1], I32) for u in range(2)]
        slotOK = sb("slotOK", [P, NB, SLOTS])
        nitB = sb("nitB", [P, NB])
        digit = [sb(f"digit{u}", [P, SLOTS])[:] for u in range(2)]
        negdigit = [sb(f"negdigit{u}", [P, 4])[:] for u in range(2)]
        negcode = [sb(f"negcode{u}", [P, 4])[:] for u in range(2)]
        codes = sb("codes", [P, NB, 2])
        identB = sb("identB", [P, P], BF16)
        masks = [sb(f"mask{u}", [P, SLOTS])[:] for u in range(2)]
        neg = [sb(f"neg{u}", [P, SLOTS])[:] for u in range(2)]
        pos = [sb(f"pos{u}", [P, SLOTS])[:] for u in range(2)]
        ewm = [sb(f"ewm{u}", [P, SLOTS])[:] for u in range(2)]
        eam = [sb(f"eam{u}", [P, SLOTS, 3])[:] for u in range(2)]
        eaT = [sb(f"eaT{u}", [3 * SLOTS, P])[:] for u in range(2)]
        Wslots = sb("Wslots", [3 * SLOTS, SLOTS, C])
        WeR = sb("WeR", [C, SLOTS, 3])
        score = [sb(f"score{u}", [P, SLOTS, HEADS]) for u in range(2)]
        expd = [sb(f"expd{u}", [P, SLOTS, HEADS]) for u in range(2)]
        red = sb("red", [P, 2 * C + 4])
        relation = [sb(f"relation{u}", [P, SLOTS])[:] for u in range(2)]
        rel_off = sb("rel_off", [P, R, SLOTS])
        negrel = sb("negrel", [P, R])
        oh_lo = sb("oh_lo", [ROW, 2, 4, P], BF16)
        oh_hi = sb("oh_hi", [ROW, 2, 4, NB * R], BF16)
        part = sb("hist_part", [ROW, NROW])[:]
        code = sb("hist_code", [ROW, NROW])[:]
        htyp = at(22650, ROW, NROW, dt=I32)
        zerosb = sb("zerosb", [P, GW // 3], BF16)

        ident = sb("ident", [P, P])
        nodeI = sb("nodeI", [P, NB], I32)
        nodeF = sb("nodeF", [P, NB])
        slotI = sb("slotI", [P, SLOTS], I32)
        slotF = sb("slotF", [P, SLOTS])
        relI = sb("relI", [P, R], I32)
        laneI = sb("laneI", [P, P], I16)
        codeI = sb("codeI", [P, NB * R], I16)
        gI = sb("gI", [P, SP_], I32)
        gF = sb("gF", [P, SP_])
        triI = sb("triI", [NB, NB])
        triE = sb("triE", [NB, NB])
        zrow = sb("zrow", [1, SLOTS * REC])
        small = sb("small", [P, 24, NB])
        smallI = sb("smallI", [P, 6, NB], I32)
        key16 = sb("key16", [P, NB], I16)
        infoR = sb("infoR", [P, NB, 3], I32)
        bcast = sb("bcast", [NB, 2, P])
        cum = sb("cum", [P, 3, NB])
        fval = sb("fval", [P, 2, NB])
        tabF = sb("tabF", [P, 3, SP_])
        tabI = sb("tabI", [P, SP_], I16)
        totI = sb("totI", [P, 3], I32)
        totF = sb("totF", [P, 2])
        nv = sb("nv", [P, NB])
        lsum = sb("lsum", [P, 2])
        ones = sb("ones", [P, P])
        epsb = sb("epsb", [P, 1])

        Wkvqf = sb("Wkvqf", [C + 1, 4 * C])
        Wo = sb("Wo", [C + 1, C])
        W1 = sb("W1", [C, C])
        Wabm = sb("Wabm", [C + 1, 3 * C])
        Wedge = sb("Wedge", [C, C])
        WeT = sb("WeT", [C, 4])
        WeB = at(16250, C, 4, P)
        edgeB = sb("edgeB", [P, 4, C])
        Wpost = sb("Wpost", [P, 3, 2, C])
        Wagg = sb("Wagg", [P, 2, 2, C])
        Wih = sb("Wih", [C + 1, 3 * C])
        Whh = sb("Whh", [C + 1, 3 * C])
        W1a = sb("W1a", [C, 2 * C])
        W1b = sb("W1b", [P, 2 * C])
        W2a = sb("W2a", [P, 2 * C])
        W2b = sb("W2b", [P, 2 * C])
        bcol = sb("bcol", [P, 4])
        Wlin = sb("Wlin", [P, C])
        rowsB = sb("rowsB", [P, 4, C])
        Wrel = sb("Wrel", [C + 1, 2 * R, C])

        tp = ctx.enter_context(nc.psum_tensor("tp", [P, 2, 512], F32))
        mm = ctx.enter_context(nc.psum_tensor("mm", [P, 2, 512], F32))
        l3 = ctx.enter_context(nc.psum_tensor("l3", [P, 3, 512], F32))
        hist = ctx.enter_context(nc.psum_tensor("hist", [P, 512], F32))

        consts = sem("consts")
        x_in = sem("x_in")
        edges_in, pads_clear = sem("edges_in"), sem("pads_clear")
        w_in = sem("w_in")
        tmin_cast, tmin_out, tmin_in = sem("tmin_cast"), sem("tmin_out"), sem("tmin_in")
        rec_built, rec_out = sem("rec_built"), sem("rec_out")
        row_index, row_in = sem("row_index"), [sem(f"row_in{k}") for k in range(5)]
        start_done, start_out, end_in = sem("start_done"), sem("start_out"), sem("end_in")
        key_done, key_out, key_in = sem("key_done"), sem("key_out"), sem("key_in")
        rank_act, rank_done = sem("rank_act"), sem("rank_done")
        info_out, info_in = sem("info_out"), sem("info_in")
        deg_done, degT_full, nit_done, cum_full = sem("deg_done"), sem("degT_full"), sem("nit_done"), sem("cum_full")
        steps_done, steps_out, steps_in = sem("steps_done"), sem("steps_out"), sem("steps_in")
        tp_full, tp_evac = sem("tp_full"), sem("tp_evac")
        mm_full, mm_evac = sem("mm_full"), sem("mm_evac")
        act_q, act_r = sem("act_q"), sem("act_r")
        stage_out = [sem(f"stage_out{k}") for k in range(NSTAGE)]
        stage_ready, we_spread = sem("stage_ready"), sem("we_spread")
        own_in = sem("own_in")
        x1_done, x2_done, wv_done, ab_done, agg_done, out_done = (
            sem(n) for n in ("x1_done", "x2_done", "wv_done", "ab_done", "agg_done", "out_done"))
        b_out, x2_out, h1_out = sem("b_out"), sem("x2_out"), sem("h1_out")
        z_done = sem("z_done")
        edge_full = sem("edge_full")
        hist_in, hist_oh, hist_mm, hist_done, hist_out, hist_back = (
            sem(n) for n in ("hist_in", "hist_oh", "hist_mm", "hist_done", "hist_out", "hist_back"))
        cnt_in = sem("cnt_in")
        x3_done, l3_full, l3_used, final_done, final_out = (
            sem(n) for n in ("x3_done", "l3_full", "l3_used", "final_done", "final_out"))
        ones_back = sem("ones_back")
        l3_usedA, counts_ready, prod_summed = sem("l3_usedA"), sem("counts_ready"), sem("prod_summed")
        pool_steps = sem("pool_steps")
        codes_done, codes_out = sem("codes_done"), sem("codes_out")
        col_ready = sem("col_ready")
        oh_ready, oh_summed = sem("oh_ready"), sem("oh_summed")
        ohA_operands, ohA_ready, ohA_summed = sem("ohA_operands"), sem("ohA_ready"), sem("ohA_summed")
        weighted_ready, weighted_sums = sem("weighted_ready"), sem("weighted_sums")
        a_copied, a_bytes = sem("a_copied"), sem("a_bytes")
        at_full, at_ready, at_out = sem("at_full"), sem("at_ready"), sem("at_out")
        at_in = [sem(f"at_in{k}") for k in range(5)]
        parts_ready, conv_full, conv_evac = sem("parts_ready"), sem("conv_full"), sem("conv_evac")
        attrs_ready, attrsT_full, attrsT_ready, edge_terms = (
            sem(n) for n in ("attrs_ready", "attrsT_full", "attrsT_ready", "edge_terms"))
        h_ready, sq_ready, sums_full, hmax_ready, hmin_ready, sums_used = (
            sem(n) for n in ("h_ready", "sq_ready", "sums_full", "hmax_ready", "hmin_ready", "sums_used"))
        descents_found, descents_summed, unsorted_known = (
            sem(n) for n in ("descents_found", "descents_summed", "unsorted_known"))
        chunk_in = [sem(f"chunk_in{u}") for u in range(2)]
        chunk_used, counts_done, ptr_set, sort_masks = (
            sem(n) for n in ("chunk_used", "counts_done", "ptr_set", "sort_masks"))
        column_ready, column_spread, ptr_in, pos_ready, sort_out, resorted = (
            sem(n) for n in ("column_ready", "column_spread", "ptr_in", "pos_ready", "sort_out", "resorted"))
        dst_final, dst_out = sem("dst_final"), sem("dst_out")
        w_spread, w_diag = sem("w_spread"), sem("w_diag")
        score_ready, exp_ready = sem("score_ready"), sem("exp_ready")

        class Gather:

            def __init__(self, name):
                self.win_ready = sem(name + "_win_ready")
                self.rec_landed = [sem(f"{name}_rec_landed{u}") for u in range(2)]
                self.rows_landed = [sem(f"{name}_rows_landed{u}") for u in range(2)]
                self.rec_used = sem(name + "_rec_used")
                self.free = sem(name + "_free")

        LOOP0, LOOP1, LOOP2, LOOP3 = (Gather(f"loop{n}") for n in range(4))

        block = ctx.enter_context(nc.Block())
        NCONST = 11
        NW = 42
        RANK_DVE = 15
        TP_H1 = 8 * len(GROUPS)
        MM_MLP = [1 + k * len(GROUPS) + 3 * len(PAIRS) for k in (3, 5)]
        tmin_small = at(26575, EP, 5, dt=I16)
        dst_next = at(26585, EP, 1, dt=I32)
        descents = at(26586, EP, 2)
        chunk = [at(16250 + 1250 * u, P, EW, dt=I32) for u in range(2)]
        junk_sort = at(18750, P, EW)
        before_m, behind_m, same, same2 = (at(20000 + EP * k, EP, EP) for k in range(4))
        colD, pos_i, ptr_i = (at(20320 + k, EP, 1, dt=I32) for k in range(3))
        colF, ptr_f, rank_f, behind_f, pos_f, next_f, ptr_to = (at(20323 + k, P, 1) for k in range(7))
        recC = at(20330, EP, REC, dt=I32)
        unsorted = sb("unsorted", [P, 1], I32)
        hsrc_q = at(20250, ROW, NROW, dt=I32)

        WMAX = 64 * (NB - 1) + 32 + SLOTS
        finished = lambda word: nc.s_assert_within(word >> 6, 1, NB - 1)
        at_banks = [tp[:, 0], tp[:, 1], mm[:, 0], mm[:, 1]]
        rel_banks = [[l3[:, 0], l3[:, 1], l3[:, 2]], [mm[:, 0], mm[:, 1], hist[:]]]
        conv_banks = [l3[:, 0], l3[:, 1], l3[:, 2], hist[:], mm[:, 1]]
        distance = [T1[:, GW * k:GW * (k + 1)] for k in range(2)]
        wsum = [hist[:, 0:C + HEADS], hist[:, 256:256 + C + HEADS]]
        a_blk = T2[:, 0:3 * GW // 2].bitcast(BF16).rearrange("p (k c) -> p k c", k=3)

        (K_, CNT_, START_, END_, DEG_, KEYN_, NKEY_, RANK_, PER_, RB_, DEGR_, PTR_, REM_, MAXD_, NIT_, ZP_,
         SAFE_, HAS_, RATIO_, MU_, VAR_, STD_, LOGD_, CNTT_) = range(24)
        S = lambda k: small[:, k, :]
        SI = lambda k: smallI[:, k, :]

        def bc(ap2, n):
            return ap2.unsqueeze(2).to_broadcast([ap2.shape[0], ap2.shape[1], n])

        def bm(ap2, n):
            return ap2.unsqueeze(1).to_broadcast([ap2.shape[0], n, ap2.shape[1]])

        @block.sync
        def _(sp):
            dma = sp.dma_start
            row = lambda v: v.rearrange("(a n) -> a n", a=1)
            dma(dst_sb, a["dst"].rearrange("(p n) -> p n", p=EP)).then_inc(edges_in, 16)
            dst_rows = a["dst"].rearrange("(p n) -> p n", p=EP)
            dma(dst_next[0:EP - 1], dst_rows[1:, 0:1], allow_slow_non_contiguous=True).then_inc(edges_in, 16)
            dma(dst_next[EP - 1:], dst_rows[EP - 1:, EW - 1:]).then_inc(edges_in, 16)
            dma(src_sb, a["src"].rearrange("(p n) -> p n", p=EP)).then_inc(edges_in, 16)
            dma(typ_sb, a["edge_type_9"].rearrange("(p n) -> p n", p=EP)).then_inc(edges_in, 16)
            dma(attr_sb, a["edge_attr_4"].rearrange("(p n) c -> p n c", p=EP)).then_inc(edges_in, 16)
            sp.wait_ge(pads_clear, 1)
            dma(xN[0:NV], a["x"].rearrange("(p b) c -> p b c", b=NB)).then_inc(x_in, 16)
            dma(nv[0:NV], a["node_vec"].rearrange("(p b) -> p b", b=NB)).then_inc(x_in, 16)
            sp.wait_ge(unsorted_known, 1)
            flag = sp.value_load(unsorted[0:1, 0:1], min_val=0, max_val=1)
            with sp.If(flag > 0):
                with sp.Fori(0, EP // 2) as i:
                    for u in range(2):
                        sp.wait_ge(chunk_used, 2 * i + u + 1)
                        dma(chunk[u], dst_rows[bass.ds(2 * i + u, 1)].to_broadcast([P, EW])).then_inc(chunk_in[u], 16)
                sp.wait_ge(counts_done, 1)
                dma(ptr_tab.rearrange("(p b) -> p b", b=NB), S(START_)).then_inc(ptr_set, 16)
                sp.wait_ge(sort_out, 48 * EW)
                dma(dst_sb, sorted_dst.rearrange("(p n) a -> p (n a)", p=EP)).then_inc(resorted, 16)
                dma(rec_sb, sorted_rec.rearrange("(p n) c -> p n c", p=EP)).then_inc(resorted, 16)
            sp.wait_ge(dst_final, 1)
            dma(dst_tab.rearrange("(p n) -> p n", p=EP), dst_sb).then_inc(dst_out, 16)
            sp.wait_ge(tmin_cast, 1)
            dma(tmin_tab.rearrange("(p n) -> p n", p=EP), tmin_small).then_inc(tmin_out, 16)
            sp.wait_ge(tmin_out, 16)
            dma(tminB, row(tmin_tab).to_broadcast([P, NROW])).then_inc(tmin_in, 16)
            sp.wait_ge(rec_built, 1)
            dma(rec_tab[0:E, :].rearrange("(p n) c -> p n c", p=EP), rec_sb).then_inc(rec_out, 16)
            dma(rec_tab[E:, :].rearrange("(a n) c -> a (n c)", a=1), zrow[:].bitcast(I32)).then_inc(rec_out, 16)
            kv_rows = kv_tab.rearrange("(p b) c -> p b c", b=NB)
            for k, pair in enumerate(PAIRS):
                s, b = k % NSTAGE, slice(pair[0], pair[-1] + 1)
                sp.wait_ge(stage_ready, k + 1)
                dma(kv_rows[:, b, 0:2 * C], stage[:, s, 0:len(pair)]).then_inc(stage_out[s], 16)
            sp.wait_ge(start_done, 1)
            dma(start_tab[0:NP].rearrange("(p b) -> p b", b=NB), S(START_)).then_inc(start_out, 16)
            dma(start_tab[NP:].rearrange("(a n) -> a n", a=1), totF[0:1, 1:2]).then_inc(start_out, 16)
            sp.wait_ge(start_out, 32)
            dma(S(END_), start_tab[1:].rearrange("(p b) -> p b", b=NB)).then_inc(end_in, 16)
            sp.wait_ge(key_done, 1)
            dma(key_tab.rearrange("(p b) -> p b", b=NB), key16[:]).then_inc(key_out, 16)
            sp.wait_ge(key_out, 16)
            dma(keyB, row(key_tab).to_broadcast([P, NP])).then_inc(key_in, 16)
            sp.wait_ge(rank_done, 1)
            dma(hsrc, a["src"].rearrange("(p n) -> p n", p=ROW)).then_inc(hist_in, 16)
            dma(htyp, a["edge_type_9"].rearrange("(p n) -> p n", p=ROW)).then_inc(hist_in, 16)
            sp.wait_ge(codes_done, 1)
            dma(kv_rows[:, :, 2 * C:], codes[:]).then_inc(codes_out, 16)
            sp.wait_ge(info_out, 16 * NB)
            own_rows = own_tab.rearrange("(p b) c -> p b c", b=NB)
            dma(infoR[:].bitcast(F32), own_rows[:, :, 3 * C:]).then_inc(info_in, 16)
            dma(ownR, own_rows[:, :, 0:3 * C]).then_inc(own_in, 16)
            sp.wait_ge(steps_done, 1)
            dma(step_tab.rearrange("(p n) -> p n", p=P), tabI[:]).then_inc(steps_out, 16)
            sp.wait_ge(steps_out, 16)
            dma(stepW[:], row(step_tab)).then_inc(steps_in, 16)
            for b in range(NB):
                sp.wait_ge(at_ready, b + 2)
                dma(at_tab[b], atS).then_inc(at_out, 16)
            sp.wait_ge(hist_done, 1)
            dma(cnt_tab.rearrange("(p b) c -> p b c", b=NB),
                histo[:].rearrange("p (b c) -> p b c", c=R)).then_inc(hist_out, 16)
            sp.wait_ge(at_out, 16 * (NB + 1))
            sp.wait_ge(x2_done, 1)
            big = sp.value_load(totI[0:1, 2:3], min_val=0, max_val=1)
            with sp.If(big < 1):
                for s in range(2 * NB):
                    if s >= 5:
                        sp.wait_ge(conv_full, s - 4)
                    dma(atL[s % 5], at_tab[s % NB]).then_inc(at_in[s % 5], 16)

        @block.gpsimd
        def _(pool):
            pool.iota(nodeI[:], pattern=[[1, NB]], base=0, channel_multiplier=NB).then_inc(consts, 1)
            pool.iota(slotI[:], pattern=[[1, SLOTS]], base=0, channel_multiplier=0).then_inc(consts, 1)
            pool.iota(relI[:], pattern=[[1, R]], base=0, channel_multiplier=0).then_inc(consts, 1)
            pool.iota(gI[:], pattern=[[1, SP_]], base=0, channel_multiplier=SP_).then_inc(consts, 1)
            pool.iota(laneI[:], pattern=[[1, P]], base=0, channel_multiplier=0,
                      allow_small_or_imprecise_dtypes=True).then_inc(consts, 1)
            pool.iota(codeI[:], pattern=[[1, NB * R]], base=0, channel_multiplier=0,
                      allow_small_or_imprecise_dtypes=True).then_inc(consts, 1)
            pool.memset(ident[:], 0.0)
            pool.memset(ones[:], 1.0).then_inc(consts, 1)
            pool.memset(triI[:], 0.0)
            pool.memset(triE[:], 0.0)
            pool.memset(zrow[:], 0.0).then_inc(consts, 1)
            pool.wait_ge(consts, 8)
            pool.drain()
            pool.affine_select(out=ident[:], in_=ident[:], compare_op=ALU.not_equal, fill=1.0, base=0,
                               pattern=[[-1, P]], channel_multiplier=1).then_inc(consts, 1)
            pool.affine_select(out=triI[:], in_=triI[:], compare_op=ALU.is_gt, fill=1.0, base=0,
                               pattern=[[-1, NB]], channel_multiplier=1).then_inc(consts, 1)
            pool.affine_select(out=triE[:], in_=triE[:], compare_op=ALU.is_ge, fill=1.0, base=0,
                               pattern=[[-1, NB]], channel_multiplier=1).then_inc(consts, 1)

            offs = bass.IndirectOffsetOnAxis

            def gather(dst, table, index):
                return pool.indirect_dma_start(dst, None, table, offs(ap=index, axis=0))

            def scatter(table, index, src, **kw):
                return pool.indirect_dma_start(table, offs(ap=index, axis=0), src, None, **kw)

            pool.wait_ge(unsorted_known, 1)
            flag = pool.value_load(unsorted[0:1, 0:1], min_val=0, max_val=1)
            with pool.If(flag > 0):
                pool.wait_ge(ptr_set, 16)
                for m, step in ((behind_m, -1), (before_m, 1)):
                    pool.affine_select(out=m, in_=m, compare_op=ALU.is_ge, fill=1.0, base=0,
                                       pattern=[[step, EP]], channel_multiplier=-step).then_inc(sort_masks, 1)
                ptr_rows = ptr_tab.rearrange("(n a) -> n a", a=1)
                with pool.Fori(0, EW) as i:
                    pool.wait_ge(column_ready, i + 1)
                    pool.sem_inc(pool_steps, 1)
                    gather(ptr_f[0:EP], ptr_rows, colD).then_inc(ptr_in, 16)
                    pool.wait_ge(pos_ready, i + 1)
                    pool.sem_inc(pool_steps, 1)
                    scatter(ptr_rows, ptr_i, next_f[0:EP], bounds_check=NP - 1, oob_is_err=False).then_inc(sort_out, 16)
                    scatter(sorted_dst, pos_i, colD).then_inc(sort_out, 16)
                    scatter(sorted_rec, pos_i, recC).then_inc(sort_out, 16)
            pool.wait_ge(dst_out, 16)
            dst_rows = dst_tab.rearrange("(t n) -> t n", n=ROW)
            for b in range(NB):
                pool.wait_ge(row_index, b // 5 + 1)
                gather(dstrow[:, b], dst_rows, SI(0)[:, b:b + 1]).then_inc(row_in[b // 5], 16)
            pool.iota(colI, pattern=[[1, GW]], base=0, channel_multiplier=0,
                      allow_small_or_imprecise_dtypes=True).then_inc(col_ready, 1)
            pool.wait_ge(w_spread, 1)
            pool.affine_select(out=Wslots[:], in_=Wslots[:], compare_op=ALU.is_ge, fill=0.0, base=0,
                               pattern=[[-3, SLOTS], [0, C]], channel_multiplier=1)
            pool.drain()
            pool.affine_select(out=Wslots[:], in_=Wslots[:], compare_op=ALU.is_ge, fill=0.0, base=2,
                               pattern=[[3, SLOTS], [0, C]], channel_multiplier=-1).then_inc(w_diag, 1)
            pool.wait_ge(rank_done, 1)
            for b in range(NB):
                scatter(own_tab, SI(3)[:, b:b + 1], ownN[:, b]).then_inc(info_out, 16)
            for k in range(NSTAGE):
                pool.wait_ge(stage_out[k], 16 * len(PAIRS[k::NSTAGE]))
            pool.wait_ge(rec_out, 32)

            def gather_loop(L, buf, table):
                pairs = pool.value_load(totI[0:1, 0:1], min_val=HI + 1, max_val=STEPS // 2 - 8)
                pool.wait_ge(L.win_ready, 1)
                gather(rec[0][:].rearrange("p s c -> p (s c)"), rec_tab, win[0][:]).then_inc(L.rec_landed[0], 16)
                with pool.Fori(0, pairs) as i:
                    for u in range(2):
                        word = pool.value_load(stepW[0:1, bass.ds(2 * i + u, 1)], min_val=0, max_val=WMAX)
                        left = word & 31
                        pool.wait_ge(L.rec_landed[u], 16 * (i + 1))
                        pool.wait_ge(L.free, 2 * i + u + 1)
                        pool.sem_inc(pool_steps, 1)
                        for s in range(SLOTS // SUB):
                            if s == SLOTS // SUB // 2:
                                pool.wait_ge(L.win_ready, 2 * i + u + 2)
                                pool.wait_ge(L.rec_used, 2 * i + u + 1)
                                pool.sem_inc(pool_steps, 1)
                                gather(rec[1 - u][:].rearrange("p s c -> p (s c)"), rec_tab,
                                       win[1 - u][:]).then_inc(L.rec_landed[1 - u], 16)
                            with (pool.If(left >= s * SUB + 1) if s else nullcontext()):
                                for j in range(s * SUB, s * SUB + SUB):
                                    gather(buf[u][:, j], table, rec[u][:, j, 0:1]).then_inc(
                                        L.rows_landed[u], 16)
                pool.wait_ge(L.rec_landed[0], 16 * (pairs + 1))
                pool.sem_inc(pool_steps, 1)

            pool.wait_ge(steps_in, 16)
            pool.wait_ge(codes_out, 16)
            gather_loop(LOOP0, G, kv_tab)
            for b in range(NB):
                pool.wait_ge(ab_done, b // 2 + 1)
                scatter(b_tab, infoR[:, b, 0:1], sR[:, b]).then_inc(b_out, 16)
            pool.wait_ge(b_out, 16 * NB)
            gather_loop(LOOP1, G1, b_tab)
            pool.wait_ge(x2_done, 1)
            big = pool.value_load(totI[0:1, 2:3], min_val=0, max_val=1)
            with pool.If(big > 0):
                for b in range(NB):
                    scatter(x2_tab, infoR[:, b, 0:1], xN[:, b]).then_inc(x2_out, 16)
                pool.wait_ge(x2_out, 16 * NB)
                gather_loop(LOOP2, G1, x2_tab)
                pool.wait_ge(tp_evac, TP_H1)
                for b in range(NB):
                    scatter(h1_tab, infoR[:, b, 0:1], h1R[:, b]).then_inc(h1_out, 16)
                pool.wait_ge(h1_out, 16 * NB)
                gather_loop(LOOP3, G3, h1_tab)
            pool.wait_ge(hist_out, 16)
            pool.wait_ge(z_done, 2)
            for b in range(NB):
                gather(cntR[:, b, 0], cnt_tab, infoR[:, b, 0:1]).then_inc(cnt_in, 16)
            for b in range(NB):
                pool.wait_ge(final_done, 1 + sum(hi <= b for _, hi in PARTS))
                scatter(out, infoR[:, b, 0:1], sumL3[:, b], bounds_check=N - 1, oob_is_err=False).then_inc(
                    final_out, 16)
            pool.wait_ge(final_out, 16 * NB)

        @block.tensor
        def _(pe):
            ring = {"tp": 0, "mm": 0}

            def transpose_group(aps):
                k = ring["tp"]
                if k >= 2:
                    pe.wait_ge(tp_evac, k - 1)
                for j, ap in enumerate(aps):
                    last = pe.transpose(tp[0:ap.shape[1], k % 2, j * P:(j + 1) * P], ap, ident[:])
                last.then_inc(tp_full, 1)
                ring["tp"] = k + 1

            def transpose_all(src, w=None):
                for g in GROUPS:
                    transpose_group([src(b) for b in g])
                pe.wait_ge(tp_evac, ring["tp"])

            def product_group(parts):
                k = ring["mm"]
                if k >= 2:
                    pe.wait_ge(mm_evac, k - 1)
                for rows, cols, terms in parts:
                    for t, (l, r) in enumerate(terms):
                        last = pe.matmul(mm[0:rows, k % 2, cols[0]:cols[1]], l, r,
                                         start=(t == 0), stop=(t == len(terms) - 1))
                last.then_inc(mm_full, 1)
                ring["mm"] = k + 1

            cols = lambda b: slice(b * P, (b + 1) * P)

            pe.wait_ge(consts, NCONST)
            pe.wait_ge(descents_found, 1)
            pe.matmul(l3[:, 2, 0:2], ones[0:EP, :], descents, start=True, stop=True).then_inc(descents_summed, 1)
            pe.wait_ge(unsorted_known, 1)
            flag = pe.value_load(unsorted[0:1, 0:1], min_val=0, max_val=1)
            with pe.If(flag > 0):
                with pe.Fori(0, EW) as i:
                    pe.wait_ge(column_ready, i + 1)
                    pe.matmul(l3[:, 2, 0:P], colF.to_broadcast([P, P]), ident[:], start=True, stop=True).then_inc(
                        column_spread, 1)
            pe.wait_ge(consts, NCONST)
            pe.wait_ge(pads_clear, 1)
            pe.wait_ge(x_in, 32)
            transpose_all(lambda b: xN[:, b])
            pe.wait_ge(w_in, 16 * NW)
            for pair in PAIRS:
                product_group([(P, (4 * C * j, 4 * C * (j + 1)), [(T1[0:C + 1, cols(b)], Wkvqf[:])])
                               for j, b in enumerate(pair)])
            pe.wait_ge(edge_full, 1)
            pe.wait_ge(we_spread, 1)
            product_group([(P, (C * j, C * (j + 1)), [(WeB[:, j], Wedge[:])]) for j in range(4)]
                          + [(P, (4 * C, 4 * C + 1), [(ones[0:NV, :], lsum[0:NV, 0:1])]),
                             (3 * SLOTS, (5 * C, 6 * C), [(WeR[:].rearrange("p s k -> p (s k)"), Wedge[:])])])
            pe.wait_ge(deg_done, 1)
            pe.transpose(l3[0:NB, 0, 0:P], S(DEGR_), ident[:]).then_inc(degT_full, 1)
            pe.wait_ge(nit_done, 1)
            pe.matmul(l3[:, 1, 0:NB], bcast[:, 0], triI[:], start=True, stop=True)
            pe.matmul(l3[:, 1, NB:2 * NB], bcast[:, 0], triE[:], start=True, stop=True)
            pe.matmul(l3[:, 1, 2 * NB:3 * NB], bcast[:, 1], ident[0:NB, 0:NB], start=True, stop=True).then_inc(
                cum_full, 1)
            def clear_counts():
                for j in range(3):
                    pe.matmul(l3[:, j, 0:GW // 3], zerosb[:, 0:P], zerosb[:], start=True, stop=True)

            def count_slots(hot):
                for j in range(4):
                    for b3 in range(3):
                        last = pe.matmul(l3[:, b3, 0:GW // 3], identB[:], hot[:, j, b3 * (GW // 3):(b3 + 1) * (GW // 3)],
                                         start=False, stop=True, skip_group_check=True)
                return last

            def transpose_counts(done):
                pe.wait_ge(at_ready, done)
                pe.wait_ge(a_bytes, done)
                for t in range(NB):
                    bank = at_banks[t // 8].bitcast(BF16)
                    k, c = divmod(t, GT)
                    last = pe.transpose(bank[:, (t % 8) * P:(t % 8 + 1) * P], a_blk[:, k, c * P:(c + 1) * P], identB[:])
                last.then_inc(at_full, 1)

            pe.wait_ge(tp_evac, ring["tp"])
            pe.wait_ge(mm_evac, ring["mm"])
            pe.wait_ge(steps_in, 16)
            pe.wait_ge(oh_ready, 1)
            clear_counts()
            pe.matmul(wsum[1], zerosb[:, 0:P], zerosb[:, 0:C + HEADS], start=True, stop=True)
            pe.drain().then_inc(weighted_sums, 1)
            pe.drain().then_inc(at_full, 1)
            pairs = pe.value_load(totI[0:1, 0:1], min_val=HI + 1, max_val=STEPS // 2 - 8)
            with pe.Fori(0, pairs) as i:
                for u in range(2):
                    word = pe.value_load(stepW[0:1, bass.ds(2 * i + u, 1)], min_val=0, max_val=WMAX)
                    new = word & 32
                    pe.wait_ge(ohA_ready, 2 * i + u + 1)
                    count_slots(onehotA).then_inc(ohA_summed, 1)
                    with pe.If(new > 0):
                        pe.wait_ge(a_copied, finished(word))
                        clear_counts()
                    for q in range(3):
                        pe.wait_ge(oh_ready, 6 * i + 3 * u + q + 2)
                        count_slots(onehot[:, (u + q) % 2]).then_inc(oh_summed, 1)
                    pe.wait_ge(weighted_ready, 2 * i + u + 1)
                    for s in range(SLOTS):
                        last = pe.matmul(wsum[u], ident[:], weighted[u][:, s], start=(s == 0), stop=(s == SLOTS - 1))
                    last.then_inc(weighted_sums, 1)
                    with pe.If(new > 0):
                        transpose_counts(finished(word))
            pe.wait_ge(ohA_ready, 2 * pairs + 1)
            count_slots(onehotA).then_inc(ohA_summed, 1)
            transpose_counts(NB)
            pe.wait_ge(at_ready, NB + 1)
            pe.wait_ge(wv_done, 1)
            transpose_all(lambda b: sR[:, b])
            pe.wait_ge(ones_back, 1)
            for g in GROUPS:
                product_group([(P, (C * j, C * (j + 1)), [(T1[0:C + 1, cols(b)], Wo[:])])
                               for j, b in enumerate(g)])
            pe.wait_ge(x1_done, 1)
            transpose_all(lambda b: x1R[:, b])
            for g in GROUPS:
                product_group([(C, (0, P * len(g)), [(W1[:], T2[0:C, g[0] * P:(g[-1] + 1) * P])])])
            pe.wait_ge(mm_evac, ring["mm"])
            for pair in PAIRS:
                product_group([(P, (4 * C * j, 4 * C * j + 3 * C), [(T1[0:C + 1, cols(b)], Wabm[:])])
                               for j, b in enumerate(pair)])
            def step1(i, u, with_hist):
                pe.wait_ge(attrs_ready, 2 * i + u + 1)
                pe.matmul(tp[0:3 * SLOTS, u, 0:P], eam[u].rearrange("p s k -> p (s k)"), ident[:],
                          start=True, stop=True).then_inc(attrsT_full, 1)
                pe.wait_ge(attrsT_ready, 2 * i + u + 1)
                pe.wait_ge(h_ready, 2 * i + u + 1)
                for j in range(2):
                    last = pe.matmul(mm[:, j, :], eaT[u], Wslots[:, 8 * j:8 * j + 8].rearrange("p s c -> p (s c)"),
                                     start=True, stop=True)
                last.then_inc(edge_terms, 1)
                for q in range(4 if with_hist else 0):
                    pe.wait_ge(hist_oh, 8 * i + 4 * u + q + 2)
                    for j in range(4):
                        last = pe.matmul(hist[:, 0:NB * R], oh_lo[:, q % 2, j], oh_hi[:, q % 2, j],
                                         start=False, stop=True, skip_group_check=True)
                    last.then_inc(hist_mm, 1)
                pe.wait_ge(sq_ready, 2 * i + u + 1)
                pe.wait_ge(sums_used, 2 * i + u + 1)
                for s in range(SLOTS):
                    last = pe.matmul(l3[:, u, 0:2 * C + R], ident[:], hh[u][:, s], start=(s == 0), stop=(s == SLOTS - 1))
                last.then_inc(sums_full, 1)

            pe.wait_ge(mm_evac, ring["mm"])
            pe.wait_ge(w_diag, 1)
            pe.wait_ge(hist_oh, 1)
            pe.matmul(hist[:, 0:NB * R], zerosb[:, 0:P], zerosb[:, 0:NB * R], start=True, stop=True)
            pe.matmul(l3[:, 1, 0:2 * C + R], zerosb[:, 0:P], zerosb[:, 0:2 * C + R], start=True, stop=True).then_inc(
                sums_full, 1)
            pairs = pe.value_load(totI[0:1, 0:1], min_val=HI + 1, max_val=STEPS // 2 - 8)
            with pe.Fori(0, HI) as i:
                for u in range(2):
                    step1(i, u, True)
            with pe.Fori(HI, pairs) as i:
                for u in range(2):
                    step1(i, u, False)
            pe.wait_ge(agg_done, 1)
            for h in range(2):
                for g in GROUPS:
                    transpose_group([agg[:, b, 2 * h:2 * h + 2].rearrange("p a c -> p (a c)") for b in g])
            pe.wait_ge(tp_evac, ring["tp"])
            for g in GROUPS:
                product_group([(P, (P * j, P * (j + 1)),
                                [(aggT[h][:, cols(b)], Wagg[:, h].rearrange("p a c -> p (a c)")) for h in range(2)])
                               for j, b in enumerate(g)])
            pe.wait_ge(out_done, 1)
            transpose_all(lambda b: sR[:, b])
            for pair in PAIRS:
                parts = []
                for j, b in enumerate(pair):
                    o = 4 * C * j
                    xb, ob = T2[0:C + 1, cols(b)], T1[0:C + 1, cols(b)]
                    parts += [(P, (o, o + 2 * C), [(xb, Whh[:, 0:2 * C]), (ob, Wih[:, 0:2 * C])]),
                              (P, (o + 2 * C, o + 3 * C), [(ob, Wih[:, 2 * C:])]),
                              (P, (o + 3 * C, o + 4 * C), [(xb, Whh[:, 2 * C:])])]
                product_group(parts)

            def mlp(Wa, Wb, src, rows):
                transpose_all(src)
                for g in GROUPS:
                    product_group([(P, (0, P * len(g)), [(Wa[:], T1[0:rows, g[0] * P:(g[-1] + 1) * P])])])
                first = ring["mm"] - len(GROUPS)
                for n, g in enumerate(GROUPS):
                    pe.wait_ge(mm_evac, first + n + 1)
                    product_group([(P, (0, P * len(g)), [(Wb[:], T2[:, g[0] * P:(g[-1] + 1) * P])])])
                pe.wait_ge(mm_evac, ring["mm"])

            def conv(c, parts):
                pe.wait_ge(mm_evac, ring["mm"])
                pe.wait_ge(parts_ready, c + 1)
                w = parts.shape[2] * parts.shape[3]
                with pe.Fori(0, 5) as i:
                    for k in range(5):
                        pe.wait_ge(at_in[k], 16 * (i + 5 * c + 1))
                        pe.wait_ge(conv_evac, 5 * i + (k + 25 * c + 1))
                        for t in range(NB):
                            last = pe.matmul(conv_banks[k][:, 0:w], atL[k][:, cols(t)],
                                             parts[:, t].rearrange("p k c -> p (k c)"),
                                             start=(t == 0), stop=(t == NB - 1))
                        last.then_inc(conv_full, 1)

            pe.wait_ge(x2_done, 1)
            big = pe.value_load(totI[0:1, 2:3], min_val=0, max_val=1)
            with pe.If(big < 1):
                conv(0, parts2)
            pe.wait_ge(z_done, 1)
            mlp(W1a, W1b, lambda b: sR[:, b], C)
            transpose_all(lambda b: hT[:, cols(b)])
            with pe.If(big < 1):
                conv(1, parts3)
            pe.wait_ge(z_done, 2)
            mlp(W2a, W2b, lambda b: h1R[:, b], P)
            for g in GROUPS:
                product_group([(P, (C * j, C * (j + 1)), [(hT[:, cols(b)], Wlin[:])]) for j, b in enumerate(g)])
            pe.wait_ge(x3_done, 1)
            transpose_all(lambda b: x1R[:, b])
            for b in range(NB):
                if b >= 2:
                    pe.wait_ge(l3_used, b - 1)
                    pe.wait_ge(l3_usedA, b - 1)
                for j in range(3):
                    last = pe.matmul(rel_banks[b % 2][j][:, 0:6 * C], T1[0:C + 1, cols(b)],
                                     Wrel[:, 6 * j:6 * j + 6].rearrange("k r n -> k (r n)"), start=True, stop=True)
                last.then_inc(l3_full, 1)

        @block.scalar
        def _(act):
            row = lambda v: v.rearrange("(a n) -> a n", a=1)
            ring = {"tp": 0, "mm": 0, "q": 0}

            def copy_transposed(dst, n, width):
                k = ring["tp"]
                act.wait_ge(tp_full, k + 1)
                act.activation(dst, tp[0:width, k % 2, 0:n], ACT.Copy).then_inc(tp_evac, 1)
                ring["tp"] = k + 1

            def copy_all(dst, width):
                for g in GROUPS:
                    copy_transposed(dst[0:width, g[0] * P:(g[-1] + 1) * P], P * len(g), width)

            def asked():
                act.wait_ge(act_q, ring["q"] + 1)
                ring["q"] += 1

            n = 0

            def w(dst, src):
                nonlocal n
                act.dma_start(dst, src).then_inc(w_in, 16)
                n += 1

            row = lambda v: v.rearrange("(a n) -> a n", a=1)
            for j, k in enumerate(("k", "v", "q", "f")):
                w(Wkvqf[0:C, j * C:(j + 1) * C], a["L0_gnn_W" + k])
                w(Wkvqf[C:C + 1, j * C:(j + 1) * C], row(a["L0_gnn_b" + k]))
            w(Wo[0:C], a["L0_gnn_Wo"])
            w(Wo[C:C + 1], row(a["L0_gnn_bo"]))
            w(W1[:], a["L1_gnn_W"])
            for j in range(2):
                w(Wabm[0:C, j * C:(j + 1) * C], a["L1_gnn_Wpre"][j * C:(j + 1) * C, :])
            w(Wabm[0:C, 2 * C:], a["L1_gnn_Wpost"][0:C, :])
            w(Wabm[C:C + 1, 2 * C:], row(a["L1_gnn_bpost"]))
            w(Wedge[:], a["L1_gnn_Wpre"][2 * C:, :])
            for k in range(3):
                w(WeT[:, 1 + k:2 + k], a["L1_gnn_We"][k, :].rearrange("(n a) -> n a", a=1))
            w(WeT[:, 0:1], a["L1_gnn_be"].rearrange("(n a) -> n a", a=1))
            for j in range(3):
                w(Wpost[:, j], a["L1_gnn_Wpost"][(1 + 4 * j) * C:(5 + 4 * j) * C, :].rearrange(
                    "(h p) n -> p h n", p=P))
            for t, k in ((Wih, "ih"), (Whh, "hh")):
                w(t[0:C], a["L1_gnn_W" + k])
                w(t[C:C + 1], row(a["L1_gnn_b" + k]))
            for t, k in ((W1a, "1a"), (W1b, "1b"), (W2a, "2a"), (W2b, "2b"), (Wlin, "lin")):
                w(t[:], a["L2_gnn_W" + k])
            for j, k in enumerate(("b1a", "b1b", "b2a", "b2b")):
                w(bcol[:, j:j + 1], a["L2_gnn_" + k].rearrange("(n a) -> n a", a=1))
            for j, k in enumerate(("L0_gnn_gamma", "L0_gnn_beta", "L1_gnn_bpre", "L2_gnn_blin")):
                w(rowsB[:, j], row(a[k]).to_broadcast([P, C]))
            w(Wrel[0:C], a["L3_gnn_weights"][2].rearrange("r k n -> k r n"))
            w(Wrel[C:C + 1], a["L3_gnn_biases"][2:3])
            assert n == NW
            copy_all(T1, C)
            act.wait_ge(x_in, 32)
            act.activation(nv[:], nv[:], ACT.Ln, bias=ones[:, 0:1], accum_out=lsum[:, 0:1]).then_inc(edge_full, 1)
            act.wait_ge(key_in, 16)
            for b in range(RANK_DVE, NB):
                act.activation(junk_act, keyB, ACT.Sign, bias=S(NKEY_)[:, b:b + 1], accum_out=S(RANK_)[:, b:b + 1])
                last = act.drain()
            last.then_inc(rank_act, 1)
            def copy_counts(done):
                act.activation(packed.rearrange("p (a c) -> p a c", a=3), l3[:, :, 0:GW // 3], ACT.Copy)
                act.drain().then_inc(a_copied, 1)
                act.wait_ge(at_full, done)
                act.activation(a_blk, packed.bitcast(U8).rearrange("p (c k) -> p k c", k=4)[:, 0:3],
                               ACT.Copy).then_inc(a_bytes, 1)

            def copy_tiles(done):
                act.wait_ge(at_out, 16 * done)
                act.wait_ge(at_full, done + 1)
                for j, bank in enumerate(at_banks):
                    n = min(8 * P, NP - 8 * P * j)
                    last = act.activation(atS[:, 8 * P * j:8 * P * j + n], bank[:, 0:n // 2].bitcast(BF16), ACT.Copy)
                last.then_inc(at_ready, 1)

            act.wait_ge(steps_in, 16)
            act.drain().then_inc(at_ready, 1)
            act.drain().then_inc(at_out, 16)
            pairs = act.value_load(totI[0:1, 0:1], min_val=HI + 1, max_val=STEPS // 2 - 8)
            with act.Fori(0, pairs) as i:
                for u in range(2):
                    word = act.value_load(stepW[0:1, bass.ds(2 * i + u, 1)], min_val=0, max_val=WMAX)
                    new = word & 32
                    with act.If(new > 0):
                        act.wait_ge(ohA_summed, 2 * i + u + 1)
                        copy_counts(finished(word))
                    act.wait_ge(score_ready, 2 * i + u + 1)
                    act.activation(expd[u][:], score[u][:], ACT.Exp, scale=1.0 / 8.0).then_inc(exp_ready, 1)
                    act.wait_ge(ohA_operands, 2 * i + u + 1)
                    act.wait_ge(ohA_summed, 2 * i + u + 1)
                    for j in range(0, 4, 2):
                        for k in range(2):
                            act.activation(distance[k], colI, ACT.Abs, bias=negcode[u][:, j + k:j + k + 1])
                        act.drain()
                        for k in range(2):
                            last = act.activation(onehotA[:, j + k], distance[k], ACT.Relu,
                                                  scale=negdigit[u][:, j + k:j + k + 1],
                                                  bias=digit[u][:, SLOTS - 4 + j + k:SLOTS - 3 + j + k])
                        if j == 0:
                            act.drain()
                    last.then_inc(ohA_ready, 1)
                    with act.If(new > 0):
                        copy_tiles(finished(word))
            act.wait_ge(ohA_summed, 2 * pairs + 1)
            copy_counts(NB)
            copy_tiles(NB)
            copy_all(T1, C)

            def std(lo=0, hi=NB):
                asked()
                act.activation(S(STD_)[:, lo:hi], S(VAR_)[:, lo:hi], ACT.Sqrt, bias=epsb[:], scale=1.0 / C).then_inc(
                    act_r, 1)

            std()
            std()
            copy_all(T2, C)
            pairs = act.value_load(totI[0:1, 0:1], min_val=HI + 1, max_val=STEPS // 2 - 8)
            with act.Fori(0, pairs) as i:
                for u in range(2):
                    act.wait_ge(attrsT_full, 2 * i + u + 1)
                    act.activation(eaT[u], tp[0:3 * SLOTS, u, 0:P], ACT.Copy).then_inc(attrsT_ready, 1)
                    for r in range(R):
                        act.activation(rel_off[:, r], relation[u], ACT.Abs, bias=negrel[:, r:r + 1])
                    act.drain()
                    act.activation(hh[u][:, :, 2 * C:].rearrange("p s r -> p r s"), rel_off[:], ACT.Relu, scale=-1.0,
                                   bias=ones[:, 0:1])
                    act.wait_ge(h_ready, 2 * i + u + 2)
                    act.activation(hh[u][:, :, C:2 * C], hh[u][:, :, 0:C], ACT.Square).then_inc(sq_ready, 1)
                    for dst, bias, ready in ((hmax[u], neg[u], hmax_ready), (hmin[u], pos[u], hmin_ready)):
                        for s in range(SLOTS):
                            last = act.activation(dst[:, s], hh[u][:, s, 0:C], ACT.Identity, bias=bias[:, s:s + 1])
                        last.then_inc(ready, 1)
            asked()
            act.activation(S(LOGD_), S(LOGD_), ACT.Ln, bias=ones[:, 0:1]).then_inc(act_r, 1)
            asked()
            act.activation(agg[:, :, 3], accS2, ACT.Sqrt, bias=epsb[:]).then_inc(act_r, 1)
            for h in range(2):
                copy_all(aggT[h], P)
            copy_all(T1, C)
            asked()
            act.activation(gates[:, :, 0:2 * C], gates[:, :, 0:2 * C], ACT.Sigmoid).then_inc(act_r, 1)
            asked()
            act.activation(sR, sR, ACT.Tanh).then_inc(act_r, 1)
            std()
            for first in (True, False):
                copy_all(T1, C if first else P)
                for layer in range(2):
                    for g in GROUPS:
                        k = MM_MLP[0 if first else 1] + layer * 7 + g[0] // 4
                        n = P * len(g)
                        act.wait_ge(mm_full, k + 1)
                        act.activation((T2 if layer == 0 else hT)[:, g[0] * P:g[0] * P + n], mm[:, k % 2, 0:n], ACT.Relu,
                                       bias=bcol[:, (0 if first else 2) + layer:(0 if first else 2) + layer + 1]).then_inc(
                                           mm_evac, 1)
                if first:
                    for g in GROUPS:
                        copy_transposed(h1R[:, g[0]:g[-1] + 1].rearrange("p b c -> p (b c)"), P * len(g), P)
            std()
            copy_all(T1, C)
            act.wait_ge(counts_ready, 1)
            for lo, hi, b in ((lo, hi, b) for lo, hi in PARTS for b in range(lo, hi)):
                act.wait_ge(l3_full, b + 1)
                if b >= 2:
                    act.wait_ge(prod_summed, b - 1)
                for k in range(6):
                    r = 12 + k
                    last = act.activation(prodL3[b % 2][:, r * C:(r + 1) * C], rel_banks[b % 2][2][:, k * C:(k + 1) * C],
                                          ACT.Copy, scale=cntR[:, b].rearrange("p a r -> p (a r)")[:, r:r + 1])
                last.then_inc(l3_usedA, 1)
                if b == hi - 1:
                    std(lo, hi)

        @block.vector
        def _(dve):
            ring = {"mm": 0, "q": 0, "stage": 0}
            tt, ts, stt, red_ = dve.tensor_tensor, dve.tensor_scalar, dve.scalar_tensor_tensor, dve.tensor_reduce
            d = dve.drain

            def mm_take(fn):
                k = ring["mm"]
                dve.wait_ge(mm_full, k + 1)
                fn(mm[:, k % 2]).then_inc(mm_evac, 1)
                ring["mm"] = k + 1

            def ask(ins):
                ins.then_inc(act_q, 1)
                ring["q"] += 1
                dve.wait_ge(act_r, ring["q"])

            dve.memset(xN[96:P], 0.0)
            dve.memset(nv[96:P], 0.0)
            dve.memset(T1[C:C + 1], 1.0)
            dve.memset(Wabm[C:C + 1, 0:2 * C], 0.0)
            dve.memset(zerosb[:], 0.0)
            dve.memset(codes[:], 1.0)
            dve.memset(totF[:, 1:2], float(E))
            dve.memset(epsb[:], EPS)
            dve.memset(accT[:], 0.0)
            d().then_inc(pads_clear, 1)
            dve.wait_ge(consts, NCONST)
            dve.tensor_copy(nodeF[:], nodeI[:])
            dve.tensor_copy(slotF[:], slotI[:])
            dve.tensor_copy(gF[:], gI[:])
            ts(negrel[:], relI[:], -1.0, -1.0, op0=ALU.mult, op1=ALU.add)
            dve.tensor_copy(identB[:], ident[:])
            dve.wait_ge(edges_in, 96)
            descending = at(18750, EP, EW - 1)
            tt(descending, dst_sb[:, 1:], dst_sb[:, 0:EW - 1], ALU.is_lt)
            tt(descents[:, 1:2], dst_next, dst_sb[:, EW - 1:], ALU.is_lt)
            d()
            red_(descents[:, 0:1], descending, X_AXIS, ALU.add)
            d().then_inc(descents_found, 1)

            def build_records():
                dve.tensor_copy(rec_sb[:, :, 0], src_sb)
                dve.tensor_copy(rec_sb[:, :, 5], typ_sb)
                dve.tensor_copy(rec_sb[:, :, 1:5], attr_sb.bitcast(I32))
                d()

            dve.wait_ge(descents_summed, 1)
            red_(totF[:, 0:1], l3[:, 2, 0:2], X_AXIS, ALU.add)
            d()
            ts(unsorted[:], totF[:, 0:1], 1.0, None, op0=ALU.min)
            d().then_inc(unsorted_known, 1)
            flag = dve.value_load(unsorted[0:1, 0:1], min_val=0, max_val=1)
            with dve.If(flag > 0):
                build_records()
                dve.memset(S(START_), 0.0)
                dve.memset(before_m, 0.0)
                dve.memset(behind_m, 0.0)
                dve.memset(colF, 0.0)
                d().then_inc(chunk_used, 2)
                with dve.Fori(0, EP // 2) as i:
                    for u in range(2):
                        dve.wait_ge(chunk_in[u], 16 * (i + 1))
                        for b in range(NB):
                            ts(junk_sort, chunk[u], nodeF[:, b:b + 1], None, op0=ALU.is_lt, op1=ALU.add,
                               accum_out=S(K_)[:, b:b + 1])
                            d()
                        tt(S(START_), S(START_), S(K_), ALU.add)
                        d().then_inc(chunk_used, 1)
                d().then_inc(counts_done, 1)
                dve.wait_ge(sort_masks, 2)

                def load_column(i):
                    dve.tensor_copy(colD, dst_sb[:, bass.ds(i, 1)])
                    dve.tensor_copy(colF[0:EP], dst_sb[:, bass.ds(i, 1)])
                    dve.tensor_copy(recC.unsqueeze(1), rec_sb[:, bass.ds(i, 1), :])
                    d().then_inc(column_ready, 1)

                def place_column(i):
                    dve.wait_ge(column_spread, i + 1)
                    ts(same, l3[0:EP, 2, 0:EP], colF[0:EP], None, op0=ALU.is_equal)
                    d()
                    tt(same2, same, before_m, ALU.mult)
                    d()
                    tt(same, same, behind_m, ALU.mult)
                    d()
                    red_(rank_f[0:EP], same2, X_AXIS, ALU.add)
                    red_(behind_f[0:EP], same, X_AXIS, ALU.add)
                    d()
                    dve.wait_ge(ptr_in, 16 * (i + 1))
                    tt(pos_f[0:EP], ptr_f[0:EP], rank_f[0:EP], ALU.add)
                    ts(ptr_to[0:EP], behind_f[0:EP], float(NP), None, op0=ALU.mult)
                    d()
                    tt(ptr_i, ptr_to[0:EP], colF[0:EP], ALU.add)
                    ts(next_f[0:EP], pos_f[0:EP], 1.0, None, op0=ALU.add)
                    dve.tensor_copy(pos_i, pos_f[0:EP])
                    d().then_inc(pos_ready, 1)

                load_column(0)
                with dve.Fori(0, EW - 1) as i:
                    place_column(i)
                    dve.wait_ge(sort_out, 48 * (i + 1))
                    load_column(i + 1)
                place_column(EW - 1)
                dve.wait_ge(resorted, 32)
                d()
            d().then_inc(dst_final, 1)
            dve.tensor_copy(tmin_small, dst_sb[:, 0:EW:ROW]).then_inc(tmin_cast, 1)
            with dve.If(flag < 1):
                build_records()
            d().then_inc(rec_built, 1)
            dve.wait_ge(tmin_in, 16)
            d()
            for g in range(0, NB, 5):
                for b in range(g, g + 5):
                    ts(junk16[:, b % 5 // 3, NROW * (b % 5 % 3):NROW * (b % 5 % 3 + 1)], tminB, nodeF[:, b:b + 1], None,
                       op0=ALU.is_lt, op1=ALU.add, accum_out=S(K_)[:, b:b + 1])
                d()
                ts(S(K_)[:, g:g + 5], S(K_)[:, g:g + 5], -1.0, 0.0, op0=ALU.add, op1=ALU.max)
                d()
                dve.tensor_copy(SI(0)[:, g:g + 5], S(K_)[:, g:g + 5]).then_inc(row_index, 1)
            dve.wait_ge(w_in, 16 * NW)
            dve.tensor_copy(WeB, bc(WeT[:], P))
            dve.tensor_copy(WeR[:], bm(WeT[:, 1:4], SLOTS))
            tt(Wagg[:, :, 0], Wpost[:, 0], Wpost[:, 2], ALU.add)
            dve.tensor_copy(Wagg[:, :, 1], Wpost[:, 1])
            d().then_inc(we_spread, 1)
            for pair in PAIRS:
                s = ring["stage"] % NSTAGE
                if ring["stage"] >= NSTAGE:
                    dve.wait_ge(stage_out[s], 16 * (ring["stage"] // NSTAGE))
                n = len(pair)
                k = ring["mm"]
                dve.wait_ge(mm_full, k + 1)
                bank = mm[:, k % 2].rearrange("p (b c) -> p b c", c=4 * C)[:, 0:n]
                dve.tensor_copy(stage[:, s, 0:n], bank[:, :, 0:2 * C]).then_inc(stage_ready, 1)
                dve.tensor_copy(ownN[:, pair[0]:pair[-1] + 1, 0:2 * C], bank[:, :, 2 * C:]).then_inc(mm_evac, 1)
                ring["mm"] = k + 1
                ring["stage"] += 1
            dve.wait_ge(mm_full, ring["mm"] + 1)
            dve.tensor_copy(edgeB[:].rearrange("p a c -> p (a c)"), mm[:, ring["mm"] % 2, 0:4 * C])
            dve.tensor_copy(Wslots[:], bm(mm[0:3 * SLOTS, ring["mm"] % 2, 5 * C:6 * C], SLOTS)).then_inc(w_spread, 1)
            ts(lsum[:, 1:2], mm[:, ring["mm"] % 2, 4 * C:4 * C + 1], 1.0 / N, None, op0=ALU.mult).then_inc(mm_evac, 1)
            ring["mm"] += 1
            dve.tensor_copy(ownN[:, :, 2 * C:3 * C], xN[:])
            cmp_row = junk_dve[:, 0:NB * ROW].rearrange("p (b n) -> p b n", n=ROW)
            for g in range(0, NB, 5):
                dve.wait_ge(row_in[g // 5], 16 * 5)
                tt(cmp_row[:, g:g + 5], dstrow[:, g:g + 5], bc(nodeF[:, g:g + 5], ROW), ALU.is_lt)
                d()
                red_(S(CNT_)[:, g:g + 5], cmp_row[:, g:g + 5], X_AXIS, ALU.add)
            d()
            stt(out=S(START_), in0=S(K_), scalar=float(ROW), in1=S(CNT_), op0=ALU.mult, op1=ALU.add).then_inc(start_done, 1)
            dve.wait_ge(end_in, 16)
            tt(S(DEG_), S(END_), S(START_), ALU.subtract)
            d()
            ts(SI(1), S(DEG_), 3.0, 60.0, op0=ALU.add, op1=ALU.min)
            d()
            ts(SI(2), SI(1), 2, None, op0=ALU.logical_shift_right)
            d()
            ts(S(KEYN_), SI(2), -8.0, KEY, op0=ALU.add, op1=ALU.mult)
            d()
            tt(S(KEYN_), S(KEYN_), nodeF[:], ALU.add)
            d()
            dve.tensor_copy(key16[:], S(KEYN_))
            ts(S(NKEY_), S(KEYN_), -1.0, None, op0=ALU.mult)
            infoN = ownN[:, :, 3 * C:].bitcast(I32)
            dve.tensor_copy(infoN[:, :, 0], nodeI[:])
            dve.tensor_copy(infoN[:, :, 1], S(START_))
            dve.tensor_copy(infoN[:, :, 2], S(END_))
            d().then_inc(key_done, 1)
            dve.wait_ge(key_in, 16)
            for b in range(RANK_DVE):
                ts(junk16[:, b % 2], keyB, S(KEYN_)[:, b:b + 1], None, op0=ALU.is_gt, op1=ALU.add,
                   accum_out=S(RANK_)[:, b:b + 1])
                if b % 2:
                    d()
            dve.wait_ge(rank_act, 1)
            ts(S(RANK_)[:, RANK_DVE:], S(RANK_)[:, RANK_DVE:], float(NP - 1), 0.5, op0=ALU.add, op1=ALU.mult)
            d()
            dve.tensor_copy(SI(1), S(RANK_))
            ts(S(PER_), S(RANK_), float(GW), None, op0=ALU.is_ge)
            ts(S(RB_), S(RANK_), float(2 * GW), None, op0=ALU.is_ge)
            d()
            ts(S(ZP_), S(RB_), 65280.0, 1.0, op0=ALU.mult, op1=ALU.add)
            tt(S(RB_), S(PER_), S(RB_), ALU.add)
            d()
            stt(out=codes[:, :, 0], in0=S(RB_), scalar=-float(GW), in1=S(RANK_), op0=ALU.mult, op1=ALU.add)
            stt(out=codes[:, :, 1], in0=S(PER_), scalar=255.0, in1=S(ZP_), op0=ALU.mult, op1=ALU.add)
            d().then_inc(codes_done, 1)
            ts(SI(2), SI(1), 7, None, op0=ALU.logical_shift_right)
            ts(SI(4), SI(1), 127, None, op0=ALU.bitwise_and)
            d()
            stt(out=SI(3), in0=SI(4), scalar=float(NB), in1=SI(2), op0=ALU.mult, op1=ALU.add).then_inc(rank_done, 1)
            dve.wait_ge(rec_out, 32)
            for u in range(2):
                dve.memset(G[u], 0.0)
            dve.wait_ge(hist_in, 32)
            ts(hsrc_q, hsrc, 5243.0, None, op0=ALU.mult)
            d()
            ts(hsrc_q, hsrc_q, 17, None, op0=ALU.logical_shift_right)
            d()
            dve.tensor_copy(part, hsrc_q)
            d()
            stt(out=code, in0=part, scalar=-float(NB), in1=hsrc, op0=ALU.mult, op1=ALU.add)
            d()
            stt(out=code, in0=code, scalar=float(R), in1=htyp, op0=ALU.mult, op1=ALU.add)
            d().then_inc(hist_oh, 1)

            dve.memset(onehotA, 0.0)
            dve.wait_ge(info_in, 16)
            dve.tensor_copy(S(PTR_), infoR[:, :, 1])
            dve.tensor_copy(S(END_), infoR[:, :, 2])
            d()
            tt(S(DEGR_), S(END_), S(PTR_), ALU.subtract)
            d()
            dve.tensor_copy(S(REM_), S(DEGR_)).then_inc(deg_done, 1)
            dve.memset(accV, 0.0)
            dve.wait_ge(degT_full, 1)
            red_(S(MAXD_)[0:NB, 0:1], l3[0:NB, 0, 0:P], X_AXIS, ALU.max)
            d()
            ts(SI(5)[0:NB, 0:1], S(MAXD_)[0:NB, 0:1], 1.0, float(SLOTS - 1), op0=ALU.max, op1=ALU.add)
            d()
            ts(SI(5)[0:NB, 1:2], SI(5)[0:NB, 0:1], 4, None, op0=ALU.logical_shift_right)
            d()
            dve.tensor_copy(S(NIT_)[0:NB, 0:1], SI(5)[0:NB, 1:2])
            d()
            dve.tensor_copy(bcast[:, 0], S(NIT_)[0:NB, 0:1].to_broadcast([NB, P]))
            dve.tensor_copy(bcast[:, 1], S(MAXD_)[0:NB, 0:1].to_broadcast([NB, P]))
            d().then_inc(nit_done, 1)
            dve.wait_ge(cum_full, 1)
            dve.tensor_copy(cum[:].rearrange("p a b -> p (a b)"), l3[:, 1, 0:3 * NB])
            d()
            red_(totF[:, 0:1], cum[:, 2], X_AXIS, ALU.max)
            tt(nitB[:], cum[:, 0], cum[:, 1], ALU.subtract)
            dve.memset(fval[:, 0], float(SUB))
            d()
            for m in range(SUB, SLOTS, SUB):
                stt(out=fval[:, 1], in0=nitB[:], scalar=float(m), in1=cum[:, 2], op0=ALU.mult, op1=ALU.is_lt)
                d()
                stt(out=fval[:, 0], in0=fval[:, 1], scalar=float(SUB), in1=fval[:, 0], op0=ALU.mult, op1=ALU.add)
                d()
            dve.tensor_copy(S(PER_), fval[:, 0])
            tt(slotOK[:], bm(slotF[:], NB), bc(fval[:, 0], SLOTS), ALU.is_lt)
            tt(ind3, bc(gF[:], NB), bm(cum[:, 0], SP_), ALU.is_ge)
            ts(totI[:, 1:2], cum[:, 0, NB - 1:NB], 1.0, None, op0=ALU.add)
            d()
            tt(fval[:, 1, 0:NB - 1], fval[:, 0, 1:NB], fval[:, 0, 0:NB - 1], ALU.subtract)
            red_(tabF[:, 0], ind3, X_AXIS, ALU.add)
            d()
            tt(ind3, bc(gF[:], NB), bm(cum[:, 0], SP_), ALU.is_equal)
            ts(totI[:, 2:3], totF[:, 0:1], 255.0, None, op0=ALU.is_gt)
            d()
            red_(tabF[:, 2], ind3[:, :, 0:NB - 1], X_AXIS, ALU.add)
            d()
            tt(ind3, bc(gF[:], NB), bm(cum[:, 0], SP_), ALU.is_ge)
            ts(totI[:, 0:1], totI[:, 1:2], 1, None, op0=ALU.logical_shift_right)
            d()
            tt(indw[:, :, 0:NB - 1], ind3[:, :, 0:NB - 1], bm(fval[:, 1, 0:NB - 1], SP_), ALU.mult)
            ts(totI[:, 0:1], totI[:, 0:1], float(HI + 1), None, op0=ALU.max)
            d()
            red_(tabF[:, 1], indw[:, :, 0:NB - 1], X_AXIS, ALU.add)
            d()
            ts(tabF[:, 1], tabF[:, 1], fval[:, 0, 0:1], None, op0=ALU.add)
            d()
            ts(tabF[:, 0], tabF[:, 0], float(NB - 1), 64.0, op0=ALU.min, op1=ALU.mult)
            d()
            ts(tabF[:, 1], tabF[:, 1], 0.0, float(SLOTS), op0=ALU.max, op1=ALU.min)
            stt(out=tabF[:, 0], in0=tabF[:, 2], scalar=32.0, in1=tabF[:, 0], op0=ALU.mult, op1=ALU.add)
            d()
            tt(tabI[:], tabF[:, 0], tabF[:, 1], ALU.add)
            d().then_inc(steps_done, 1)

            landed = [dve.alloc_register(f"rows_expected{u}") for u in range(2)]

            before = dve.alloc_register("word_before")
            word = [dve.alloc_register(f"word{u}") for u in range(2)]
            ahead = [dve.alloc_register(f"word_ahead{u}") for u in range(2)]
            block_in = lambda reg: nc.s_assert_within(dve.snap(reg) >> 6, 0, NB - 1)

            def load_word(reg, g):
                w = dve.value_load(stepW[0:1, bass.ds(g, 1)], min_val=0, max_val=WMAX)
                dve.reg_mov(reg, dve.snap(w))

            def expect_rows(u):
                left = dve.snap(word[u]) & 31
                dve.reg_add(landed[u], landed[u], dve.snap(left * 16))

            def wait_rows(L, u):
                dve.wait_ge(L.rows_landed[u], dve.snap(landed[u]))

            def prepare_step(g, u):
                load_word(ahead[u], g + 2)
                expect_rows(u)

            def end_step(u):
                dve.reg_mov(before, word[u])
                dve.reg_mov(word[u], ahead[u])

            def begin_loop(L):
                dve.reg_mov(before, 0)
                for u in range(2):
                    dve.reg_mov(landed[u], 0)
                    load_word(word[u], u)
                    next_window(L, u, block_in(word[u]))
                prepare_step(0, 0)
                d().then_inc(L.rec_used, 1)
                d().then_inc(L.free, 2)

            def next_window(L, u, blk):
                p_ = small[:, PTR_, bass.ds(blk, 1)]
                ts(win[u][:], p_, float(E), None, op0=ALU.min)
                d()
                tt(p_, p_, small[:, PER_, bass.ds(blk, 1)], ALU.add)
                d().then_inc(L.win_ready, 1)

            def step_head(L, i, u):
                blk = block_in(word[u])
                dve.wait_ge(L.rec_landed[u], 16 * (i + 1))
                next_window(L, u, block_in(ahead[u]))
                r_ = small[:, REM_, bass.ds(blk, 1)]
                stt(out=masks[u], in0=slotF[:], scalar=r_, in1=slotOK[:, bass.ds(blk, 1), :].rearrange("p a s -> p (a s)"),
                    op0=ALU.is_lt, op1=ALU.mult)
                d()
                tt(r_, r_, small[:, PER_, bass.ds(blk, 1)], ALU.subtract)
                return blk

            def reset_loop():
                dve.tensor_copy(S(PTR_), infoR[:, :, 1])
                dve.tensor_copy(S(REM_), S(DEGR_))


            dve.wait_ge(steps_in, 16)
            dve.wait_ge(own_in, 16)
            begin_loop(LOOP0)
            dve.wait_ge(steps_in, 16)

            dve.wait_ge(col_ready, 1)
            d().then_inc(oh_summed, 2)
            d().then_inc(ohA_ready, 1)
            d().then_inc(oh_ready, 1)

            def step0(i, u):
                blk = step_head(LOOP0, i, u)
                wait_rows(LOOP0, u)
                q_ = ownR[:, bass.ds(blk, 1), 0:C].to_broadcast([P, SLOTS, C])
                tt(prod[:, :, 0:C], G[u][:, :, 0:C], q_, ALU.mult).then_inc(LOOP0.rec_used, 1)
                prepare_step(2 * i + u + 1, 1 - u)
                d()
                red_(score[u][:], prod[:, :, 0:C].rearrange("p s (h c) -> p s h c", h=HEADS), X_AXIS, ALU.add)
                d()
                ts(score[u][:], score[u][:], -40.0, 40.0, op0=ALU.max, op1=ALU.min).then_inc(score_ready, 1)
                tt(digit[u], G[u][:, :, 2 * C + 1], masks[u], ALU.mult)
                ts(negcode[u], G[u][:, SLOTS - 4:, 2 * C], -1.0, None, op0=ALU.mult)
                d()
                ts(negdigit[u], digit[u][:, SLOTS - 4:], -1.0, None, op0=ALU.mult).then_inc(ohA_operands, 1)
                for q in range(3):
                    dve.wait_ge(oh_summed, 6 * i + 3 * u + q + 1)
                    for j in range(4):
                        s = 4 * q + j
                        last = ts(onehot[:, (u + q) % 2, j], colI, G[u][:, s, 2 * C:2 * C + 1], digit[u][:, s:s + 1],
                                  op0=ALU.is_equal, op1=ALU.mult)
                    last.then_inc(oh_ready, 1)
                dve.wait_ge(exp_ready, 2 * i + u + 1)
                e_ = weighted[u][:, :, C:C + HEADS]
                tt(e_, expd[u][:], bc(masks[u], HEADS), ALU.mult)
                add_weighted(2 * i + u, 1 - u)
                d()
                tt(weighted[u][:, :, 0:C].rearrange("p s (h c) -> p s h c", h=HEADS),
                   G[u][:, :, C:2 * C].rearrange("p s (h c) -> p s h c", h=HEADS),
                   e_.unsqueeze(3).to_broadcast([P, SLOTS, HEADS, HD]), ALU.mult).then_inc(weighted_ready, 1)
                end_step(u)
                d().then_inc(LOOP0.free, 1)

            def add_weighted(g, u):
                dve.wait_ge(weighted_sums, g + 1)
                v_ = accV[:, bass.ds(block_in(before), 1), :]
                tt(v_, v_, wsum[u].unsqueeze(1), ALU.add)

            pairs = dve.value_load(totI[0:1, 0:1], min_val=HI + 1, max_val=STEPS // 2 - 8)
            with dve.Fori(0, pairs) as i:
                for u in range(2):
                    step0(i, u)
            dve.wait_ge(LOOP0.rec_landed[0], 16 * (pairs + 1))
            add_weighted(2 * pairs, 1)
            d()
            dve.wait_ge(at_full, NB + 1)
            dve.wait_ge(at_out, 16 * (NB + 1))

            flat3 = lambda ap: ap.rearrange("p b c -> p (b c)")
            scr = prod.rearrange("p s c -> p (s c)")[:, 0:NB * C].rearrange("p (b c) -> p b c", c=C)

            def layernorm(dst, src, lo=0, hi=NB):
                dst, src, tmp = dst[:, lo:hi], src[:, lo:hi], scr[:, lo:hi]
                mu, var, std = (S(k)[:, lo:hi] for k in (MU_, VAR_, STD_))
                red_(mu, src, X_AXIS, ALU.add)
                d()
                ts(mu, mu, 1.0 / C, None, op0=ALU.mult)
                d()
                tt(src, src, bc(mu, C), ALU.subtract)
                d()
                tt(tmp, src, src, ALU.mult)
                d()
                red_(var, tmp, X_AXIS, ALU.add)
                ask(d())
                dve.reciprocal(std, std)
                d()
                tt(dst, src, bc(std, C), ALU.mult)
                d()

            zp = small[:, ZP_:ZP_ + 4, :].rearrange("p a b -> p (a b)").rearrange("p (b h) -> p b h", h=HEADS)
            ts(zp, accV[:, :, C:], 1.0, None, op0=ALU.add)
            d()
            dve.reciprocal(zp, zp)
            d()
            tt(sR.rearrange("p b (h c) -> p b h c", h=HEADS), accV[:, :, 0:C].rearrange("p b (h c) -> p b h c", h=HEADS),
               zp.unsqueeze(3).to_broadcast([P, NB, HEADS, HD]), ALU.mult).then_inc(wv_done, 1)
            dve.memset(T1[C:C + 1], 1.0)
            dve.memset(T2[C:C + 1], 1.0).then_inc(ones_back, 1)
            own = lambda k: ownR[:, :, k * C:(k + 1) * C]
            for g in GROUPS:
                n = len(g)
                mm_take(lambda bank: tt(own(1)[:, g[0]:g[-1] + 1], own(1)[:, g[0]:g[-1] + 1],
                                        bank[:, 0:C * n].rearrange("p (b c) -> p b c", c=C), ALU.add))
            d()
            dve.tensor_copy(x1R[:], own(1))
            d()
            layernorm(x1R[:], x1R[:])
            tt(x1R[:], x1R[:], bm(rowsB[:, 0], NB), ALU.mult)
            d()
            tt(x1R[:], x1R[:], bm(rowsB[:, 1], NB), ALU.add)
            d()
            tt(x1R[:], x1R[:], own(1), ALU.add)
            d()
            tt(x1R[:], x1R[:], own(2), ALU.add)
            d()
            layernorm(x1R[:], x1R[:])
            d().then_inc(x1_done, 1)
            reset_loop()
            for g in GROUPS:
                n = P * len(g)
                mm_take(lambda bank: dve.tensor_copy(T1[0:C, g[0] * P:g[0] * P + n], bank[0:C, 0:n]))
            for pair in PAIRS:
                k = ring["mm"]
                dve.wait_ge(mm_full, k + 1)
                s = slice(pair[0], pair[-1] + 1)
                v = mm[:, k % 2].rearrange("p (b c) -> p b c", c=4 * C)[:, 0:len(pair)]
                tt(aR[:, s], v[:, :, 0:C], bm(edgeB[:, 0], len(pair)), ALU.add)
                dve.tensor_copy(sR[:, s], v[:, :, C:2 * C]).then_inc(ab_done, 1)
                dve.tensor_copy(mpR[:, s], v[:, :, 2 * C:3 * C]).then_inc(mm_evac, 1)
                ring["mm"] += 1
            dve.memset(accMx, -BIG)
            dve.memset(accMn, BIG)
            dve.memset(accS, 0.0)
            begin_loop(LOOP1)
            dve.memset(hmax[1], -BIG)
            dve.memset(hmin[1], BIG)
            d().then_inc(hmax_ready, 1)
            d().then_inc(hmin_ready, 1)
            d().then_inc(hist_mm, 2)
            d().then_inc(h_ready, 1)
            d().then_inc(sums_used, 1)

            def add_step(g, u):
                blk = block_in(before)
                row_of = lambda acc: acc[:, bass.ds(blk, 1), :]
                dve.wait_ge(sums_full, g + 1)
                v_ = row_of(accS)
                tt(v_, v_, l3[:, u:u + 1, 0:2 * C], ALU.add)
                v_ = row_of(accT)
                tt(v_, v_, l3[:, u:u + 1, 2 * C:2 * C + R], ALU.add).then_inc(sums_used, 1)
                dve.wait_ge(hmax_ready, g + 1)
                red_(red[:, 0:C], hmax[u].rearrange("p s c -> p c s"), X_AXIS, ALU.max)
                dve.wait_ge(hmin_ready, g + 1)
                red_(red[:, C:2 * C], hmin[u].rearrange("p s c -> p c s"), X_AXIS, ALU.min)
                d()
                v_ = row_of(accMx)
                tt(v_, v_, red[:, 0:C].unsqueeze(1), ALU.max)
                v_ = row_of(accMn)
                tt(v_, v_, red[:, C:2 * C].unsqueeze(1), ALU.min)

            def step1(i, u, with_hist):
                blk = step_head(LOOP1, i, u)
                ea = rec[u][:].bitcast(F32)
                tt(ewm[u], ea[:, :, 4], masks[u], ALU.mult)
                stt(out=relation[u], in0=rec[u][:, :, 5], scalar=1.0, in1=masks[u], op0=ALU.add, op1=ALU.mult)
                ts(neg[u], masks[u], 1.0, BIG, op0=ALU.subtract, op1=ALU.mult)
                ts(pos[u], masks[u], 1.0, -BIG, op0=ALU.subtract, op1=ALU.mult)
                d()
                tt(eam[u], ea[:, :, 1:4], bc(ewm[u], 3), ALU.mult).then_inc(attrs_ready, 1)
                h = hh[u][:, :, 0:C]
                wait_rows(LOOP1, u)
                tt(h, G1[u], aR[:, bass.ds(blk, 1), :].to_broadcast([P, SLOTS, C]), ALU.add).then_inc(
                    LOOP1.rec_used, 1)
                prepare_step(2 * i + u + 1, 1 - u)
                d().then_inc(LOOP1.free, 1)
                tt(h, h, bc(ewm[u], C), ALU.mult)
                d()
                dve.wait_ge(edge_terms, 2 * i + u + 1)
                tt(h, h, mm[:].rearrange("p a (s c) -> p (a s) c", c=C), ALU.add).then_inc(h_ready, 1)
                for q in range(4 if with_hist else 0):
                    dve.wait_ge(hist_mm, 8 * i + 4 * u + q + 1)
                    for j in range(4):
                        t = bass.ds(16 * (2 * i + u) + 4 * q + j, 1)
                        ts(oh_lo[:, q % 2, j], laneI[0:ROW], part[:, t], None, op0=ALU.is_equal)
                        last = ts(oh_hi[:, q % 2, j], codeI[0:ROW], code[:, t], None, op0=ALU.is_equal)
                    last.then_inc(hist_oh, 1)
                add_step(2 * i + u, 1 - u)
                end_step(u)

            with dve.Fori(0, HI) as i:
                for u in range(2):
                    step1(i, u, True)
            with dve.Fori(HI, pairs) as i:
                for u in range(2):
                    step1(i, u, False)
            d()
            add_step(2 * pairs, 1)
            dve.wait_ge(hist_mm, 8 * HI + 2)
            dve.tensor_copy(histo[:], hist[:, 0:NB * R]).then_inc(hist_done, 1)
            dve.wait_ge(LOOP1.rec_landed[0], 16 * (pairs + 1))
            ts(S(HAS_), S(DEGR_), 0.0, None, op0=ALU.is_gt)
            ts(S(LOGD_), S(DEGR_), 1.0, None, op0=ALU.max)
            d()
            dve.reciprocal(S(SAFE_), S(LOGD_))
            dve.reciprocal(lsum[:, 0:1], lsum[:, 1:2])
            ask(d())
            ts(S(RATIO_), S(LOGD_), lsum[:, 0:1], None, op0=ALU.mult)
            tt(accS1, accS1, bc(S(SAFE_), C), ALU.mult)
            tt(accS2, accS2, bc(S(SAFE_), C), ALU.mult)
            d()
            tt(scr, accS1, accS1, ALU.mult)
            d()
            tt(accS2, accS2, scr, ALU.subtract)
            d()
            ts(accS2, accS2, 0.0, None, op0=ALU.max)
            ask(d())
            for dst, src in ((0, accS1), (1, accMn), (2, accMx)):
                tt(agg[:, :, dst], src, bm(rowsB[:, 2], NB), ALU.add)
            d()
            for dst in range(3):
                tt(agg[:, :, dst], agg[:, :, dst], bc(S(HAS_), C), ALU.mult)
            d().then_inc(agg_done, 1)
            for g in GROUPS:
                k = ring["mm"]
                dve.wait_ge(mm_full, k + 1)
                s = slice(g[0], g[-1] + 1)
                v = mm[:, k % 2].rearrange("p (b c) -> p b c", c=2 * C)[:, 0:len(g)]
                tt(mpR[:, s], mpR[:, s], v[:, :, 0:C], ALU.add)
                tt(sR[:, s], v[:, :, C:2 * C], bc(S(RATIO_)[:, s], C), ALU.mult).then_inc(mm_evac, 1)
                ring["mm"] += 1
            d()
            tt(sR, sR, mpR, ALU.add)
            d().then_inc(out_done, 1)
            for pair in PAIRS:
                n = len(pair)
                mm_take(lambda bank: dve.tensor_copy(flat3(gates[:, pair[0]:pair[-1] + 1]), bank[:, 0:4 * C * n]))
            ask(d())
            gate = lambda k: gates[:, :, k * C:(k + 1) * C]
            tt(sR, gate(0), gate(3), ALU.mult)
            d()
            tt(sR, sR, gate(2), ALU.add)
            ask(d())
            tt(gate(0), x1R[:], sR, ALU.subtract)
            d()
            tt(gate(0), gate(0), gate(1), ALU.mult)
            d()
            tt(gate(0), gate(0), sR, ALU.add)
            d()
            tt(sR, gate(0), x1R[:], ALU.add)
            reset_loop()
            d()
            dve.tensor_copy(x1R[:], sR)
            d()
            layernorm(xN[:], x1R[:])
            d().then_inc(x2_done, 1)

            def sum_loop(L, buf, acc, w):
                for u in range(2):
                    dve.memset(buf[u], 0.0)
                dve.memset(acc, 0.0)
                begin_loop(L)
                pairs = dve.value_load(totI[0:1, 0:1], min_val=HI + 1, max_val=STEPS // 2 - 8)
                with dve.Fori(0, pairs) as i:
                    for u in range(2):
                        blk = step_head(L, i, u)
                        wait_rows(L, u)
                        tt(prod[:, :, 0:w], buf[u], bc(masks[u], w), ALU.mult).then_inc(L.rec_used, 1)
                        prepare_step(2 * i + u + 1, 1 - u)
                        d()
                        red_(red[:, 0:w], prod[:, :, 0:w].rearrange("p s c -> p c s"), X_AXIS, ALU.add)
                        d()
                        v_ = acc[:, bass.ds(blk, 1), :]
                        tt(v_, v_, red[:, 0:w].unsqueeze(1), ALU.add)
                        end_step(u)
                        d().then_inc(L.free, 1)
                dve.wait_ge(L.rec_landed[0], 16 * (pairs + 1))
                reset_loop()

            def conv_sums(c, src, parts, acc, w):
                dve.tensor_copy(parts[:, :, 0], src)
                d()
                tt(acc, src, parts[:, :, 0], ALU.subtract)
                d()
                dve.tensor_copy(parts[:, :, 1], acc)
                d()
                tt(acc, acc, parts[:, :, 1], ALU.subtract)
                d()
                dve.tensor_copy(parts[:, :, 2], acc)
                d().then_inc(parts_ready, 1)
                if c == 0:
                    d().then_inc(conv_evac, 5)
                with dve.Fori(0, 5) as i:
                    for k in range(5):
                        dve.wait_ge(conv_full, 5 * i + (k + 25 * c + 1))
                        red_(acc[:, bass.ds(5 * i + k, 1), :].rearrange("p a c -> p (a c)"),
                             conv_banks[k][:, 0:3 * w].rearrange("p (k c) -> p c k", k=3), X_AXIS,
                             ALU.add).then_inc(conv_evac, 1)
                d()

            big = dve.value_load(totI[0:1, 2:3], min_val=0, max_val=1)
            with dve.If(big < 1):
                conv_sums(0, xN[:], parts2, acc2, C)
            with dve.If(big > 0):
                sum_loop(LOOP2, G1, acc2, C)
            tt(sR, xN[:], acc2, ALU.add)
            d().then_inc(z_done, 1)
            ring["mm"] += 2 * len(GROUPS)
            dve.wait_ge(tp_evac, TP_H1)
            with dve.If(big < 1):
                conv_sums(1, h1R, parts3, acc3, 2 * C)
            with dve.If(big > 0):
                sum_loop(LOOP3, G3, acc3, 2 * C)
            tt(h1R, h1R, acc3, ALU.add)
            d().then_inc(z_done, 1)
            ring["mm"] += 2 * len(GROUPS)
            for g in GROUPS:
                n = len(g)
                mm_take(lambda bank: tt(sR[:, g[0]:g[-1] + 1], xN[:, g[0]:g[-1] + 1],
                                        bank[:, 0:C * n].rearrange("p (b c) -> p b c", c=C), ALU.add))
            d()
            tt(sR, sR, bm(rowsB[:, 3], NB), ALU.add)
            d()
            layernorm(x1R[:], sR)
            dve.memset(T1[C:C + 1], 1.0)
            d().then_inc(x3_done, 1)
            dve.wait_ge(cnt_in, 16 * NB)
            dve.tensor_copy(cntR[:, :, 1], accT[:])
            d()
            cnts = cntR.rearrange("p b a r -> p b (a r)")
            red_(S(CNTT_), cnts, X_AXIS, ALU.add)
            d()
            ts(S(CNTT_), S(CNTT_), 1.0, None, op0=ALU.max)
            d()
            dve.reciprocal(S(CNTT_), S(CNTT_)).then_inc(counts_ready, 1)
            for lo, hi, b in ((lo, hi, b) for lo, hi in PARTS for b in range(lo, hi)):
                dve.wait_ge(l3_full, b + 1)
                for j in range(2):
                    last = tt(prodL3[b % 2][:, 6 * C * j:6 * C * (j + 1)].rearrange("p (r c) -> p r c", c=C),
                              rel_banks[b % 2][j][:, 0:6 * C].rearrange("p (r c) -> p r c", c=C),
                              bc(cnts[:, b, 6 * j:6 * j + 6], C), ALU.mult)
                last.then_inc(l3_used, 1)
                d()
                dve.wait_ge(l3_usedA, b + 1)
                red_(sumL3[:, b], prodL3[b % 2].rearrange("p (r c) -> p c r", c=C), X_AXIS, ALU.add).then_inc(
                    prod_summed, 1)
                if b == hi - 1:
                    v_ = sumL3[:, lo:hi]
                    d()
                    tt(v_, v_, bc(S(CNTT_)[:, lo:hi], C), ALU.mult)
                    d()
                    tt(v_, v_, x1R[:, lo:hi], ALU.add)
                    d()
                    layernorm(sumL3, sumL3, lo, hi)
                    d().then_inc(final_done, 1)


INPUTS = ["x", "src", "dst", "edge_attr_4", "edge_type_9", "node_vec",
          *("L0_gnn_" + k for k in ("Wq", "bq", "Wk", "bk", "Wv", "bv", "Wo", "bo", "Wf", "bf", "gamma", "beta")),
          *("L1_gnn_" + k for k in ("W", "We", "be", "Wpre", "bpre", "Wpost", "bpost", "Wih", "bih", "Whh", "bhh")),
          *("L2_gnn_" + k for k in ("W1a", "b1a", "W1b", "b1b", "W2a", "b2a", "W2b", "b2b", "Wlin", "blin")),
          "L3_gnn_weights", "L3_gnn_biases"]


def kernel(**inputs):
    import numpy as np
    import concourse.bacc as bacc
    from concourse import mybir as mb
    from concourse.bass_utils import run_bass_kernel_spmd

    nc = bacc.Bacc("TRN2", target_bir_lowering=False, num_devices=1)
    arrays, args = {}, {}
    for name in INPUTS:
        v = np.ascontiguousarray(inputs[name])
        arrays["in_" + name] = v
        args[name] = nc.dram_tensor("in_" + name, v.shape, mb.dt.from_np(v.dtype), kind="ExternalInput").ap()
    out = nc.dram_tensor("out_0", (N, C), mb.dt.float32, kind="ExternalOutput").ap()
    build(nc, args, out)
    r = run_bass_kernel_spmd(nc, [arrays], core_ids=[0])
    return r.results[0]["out_0"]
```
